# Optimizing a Trainium2 kernel written in Bass

```python
import numpy as np
import jax
import jax.numpy as jnp

def _softmax(x, axis=-1):
    return jax.nn.softmax(x, axis=axis)

def _gelu(x):
    return jax.nn.gelu(x, approximate=True)

def _silu(x):
    return jax.nn.silu(x)

def _sigmoid(x):
    return jax.nn.sigmoid(x)

def _layernorm(x, axis=-1, eps=1e-05):
    m = jnp.mean(x, axis=axis, keepdims=True)
    v = jnp.var(x, axis=axis, keepdims=True)
    return (x - m) / jnp.sqrt(v + eps)

def _scatter_add(tgt, idx, src, axis=0):
    return tgt.at[idx].add(src)

def _segment_sum(src, seg, n):
    return jax.ops.segment_sum(src, seg, n)
kernel_name = 'mk_metaformer_d4_conv_nchw256_r4_406051'

def setup_inputs(seed: int=0):
    np.random.seed(seed)
    _w = jnp.asarray

    def _rec_inputs():
        import jax
        import jax.numpy as jnp
        _gk = jax.random.key(seed)
        x = 7.22e-05 + 1 * jax.random.normal(jax.random.fold_in(_gk, 1), (8, 64, 16, 16), jnp.float32)
        return x
    x = _rec_inputs()

    def _L0_conv_setup():
        import jax, jax.numpy as jnp
        import numpy as np
        from math import sqrt
        EPS_PN = 1e-08
        EPS_BN = 1e-05
        NUM_HEADS = 8
        HIDDEN_DIM = 64

        def pixelnorm(x, axis=1):
            return x * jax.lax.rsqrt(jnp.mean(x * x, axis=axis, keepdims=True) + EPS_PN)

        def conv1x1(x, W, b):
            return jnp.einsum('bchw,oc->bohw', x, W) + b[None, :, None, None]
        key = jax.random.key(seed)
        ks = jax.random.split(key, 13)
        B, Cin, H, W = (8, 64, 16, 16)
        Cout, Ch = (64, 64)
        return {'x': jax.random.normal(ks[0], (B, Cin, H, W), jnp.float32), 'Wq': jax.random.normal(ks[1], (Cout, Cin), jnp.float32) * 0.05, 'bq': jax.random.normal(ks[2], (Cout,), jnp.float32) * 0.05, 'Wk': jax.random.normal(ks[3], (Cout, Cin), jnp.float32) * 0.05, 'bk': jax.random.normal(ks[4], (Cout,), jnp.float32) * 0.05, 'Wv': jax.random.normal(ks[5], (Cout + Ch, Cin), jnp.float32) * 0.05, 'bv': jax.random.normal(ks[6], (Cout + Ch,), jnp.float32) * 0.05, 'Wf': jax.random.normal(ks[7], (Cout, Cout), jnp.float32) * 0.05, 'bf': jax.random.normal(ks[8], (Cout,), jnp.float32) * 0.05, 'bn_gamma': jax.random.uniform(ks[9], (Cout,), jnp.float32, 0.5, 1.5), 'bn_beta': jax.random.normal(ks[10], (Cout,), jnp.float32) * 0.05, 'bn_mean': jax.random.normal(ks[11], (Cout,), jnp.float32) * 0.05, 'bn_var': jax.random.uniform(ks[12], (Cout,), jnp.float32, 0.5, 1.5)}
    _L0_conv_all = _L0_conv_setup()
    _L0_conv_in = {k: v for k, v in _L0_conv_all.items() if k in ('Wq', 'bq', 'Wk', 'bk', 'Wv', 'bv', 'Wf', 'bf', 'bn_gamma', 'bn_beta', 'bn_mean', 'bn_var')}
    del _L0_conv_all

    def _L0_ffn_setup():
        import jax, jax.numpy as jnp
        import numpy as np
        NUM_EXPERTS = 8
        TOP_K = 2
        B, S, D = (8, 2048, 64)

        def _moe(tokens, router_w, w1, b1, w2, b2):
            N = tokens.shape[0]
            E = router_w.shape[0]
            logits = tokens.astype(jnp.float32) @ router_w.astype(jnp.float32).T
            probs = jax.nn.softmax(logits, axis=-1)
            rw, re = jax.lax.top_k(probs, TOP_K)
            if TOP_K > 1:
                rw = rw / jnp.maximum(rw.sum(-1, keepdims=True), 1e-12)
            rw = rw.astype(tokens.dtype)
            combine = jnp.zeros((N, E), tokens.dtype).at[jnp.arange(N)[:, None], re].set(rw)
            out = tokens
            for e in range(E):
                h = jax.nn.gelu(tokens @ w1[e] + b1[e], approximate=False)
                y = h @ w2[e] + b2[e]
                out = out + combine[:, e:e + 1] * y
            return out
        key = jax.random.key(seed)
        ks = jax.random.split(key, 4)
        scale = 1.0 / np.sqrt(D).astype(np.float32)
        return {'input_embeddings': jax.random.normal(ks[0], (B, S, D), jnp.float32), 'router_w': jax.random.normal(ks[1], (NUM_EXPERTS, D), jnp.float32) * scale, 'w1': jax.random.normal(ks[2], (NUM_EXPERTS, D, D), jnp.float32) * scale, 'b1': jnp.zeros((NUM_EXPERTS, D), jnp.float32), 'w2': jax.random.normal(ks[3], (NUM_EXPERTS, D, D), jnp.float32) * scale, 'b2': jnp.zeros((NUM_EXPERTS, D), jnp.float32)}
    _L0_ffn_all = _L0_ffn_setup()
    _L0_ffn_in = {k: v for k, v in _L0_ffn_all.items() if k in ('router_w', 'w1', 'b1', 'w2', 'b2')}
    del _L0_ffn_all

    def _L1_conv_setup():
        import jax, jax.numpy as jnp
        import numpy as np
        DIM = 64
        NUM_HEADS = 8
        HEAD_DIM = DIM // NUM_HEADS
        DILATIONS = (1, 2, 4, 8)
        ND = len(DILATIONS)
        K = 3
        KK = K * K
        SCALE = HEAD_DIM ** (-0.5)
        LN_EPS = 1e-05

        def _unfold(t, dil, k=K):
            B, d, H, W = t.shape
            p = dil * (k - 1) // 2
            tp = jnp.pad(t, ((0, 0), (0, 0), (p, p), (p, p)))
            patches = [tp[:, :, i * dil:i * dil + H, j * dil:j * dil + W] for i in range(k) for j in range(k)]
            return jnp.stack(patches, axis=2)
        key = jax.random.key(seed)
        ks = jax.random.split(key, 10)
        B, C, H, W = (8, DIM, 16, 16)
        s = lambda fan: fan ** (-0.5)
        return {'x': jax.random.normal(ks[0], (B, C, H, W), jnp.float32), 'qkv_w': jax.random.normal(ks[1], (3 * C, C), jnp.float32) * s(C), 'qkv_b': jnp.zeros((3 * C,), jnp.float32), 'fc_w': jax.random.normal(ks[2], (ND, ND), jnp.float32) * s(ND), 'fc_b': jnp.zeros((ND,), jnp.float32), 'ln_g': jnp.ones((C // ND,), jnp.float32), 'ln_b': jnp.zeros((C // ND,), jnp.float32), 'proj_w': jax.random.normal(ks[3], (C, C), jnp.float32) * s(C), 'proj_b': jnp.zeros((C,), jnp.float32)}
    _L1_conv_all = _L1_conv_setup()
    _L1_conv_in = {k: v for k, v in _L1_conv_all.items() if k in ('qkv_w', 'qkv_b', 'fc_w', 'fc_b', 'ln_g', 'ln_b', 'proj_w', 'proj_b')}
    del _L1_conv_all

    def _L1_ffn_setup():
        import jax, jax.numpy as jnp
        import numpy as np
        D_MODEL = 64
        N_EXPERTS = 16
        HIDDEN = 128
        SCALE = 0.02
        key = jax.random.key(seed)
        ks = jax.random.split(key, 5)
        x = jax.random.normal(ks[0], (4, 2048, D_MODEL), dtype=jnp.float32)
        gate_w = jax.random.normal(ks[1], (D_MODEL, N_EXPERTS), dtype=jnp.float32) * SCALE
        gate_b = jnp.zeros((N_EXPERTS,), dtype=jnp.float32)
        w1 = jax.random.normal(ks[2], (N_EXPERTS, D_MODEL, HIDDEN), dtype=jnp.float32) * SCALE
        w2 = jax.random.normal(ks[3], (N_EXPERTS, D_MODEL, HIDDEN), dtype=jnp.float32) * SCALE
        w3 = jax.random.normal(ks[4], (N_EXPERTS, HIDDEN, D_MODEL), dtype=jnp.float32) * SCALE
        return {'x': x, 'gate_w': gate_w, 'gate_b': gate_b, 'w1': w1, 'w2': w2, 'w3': w3}
    _L1_ffn_all = _L1_ffn_setup()
    _L1_ffn_in = {k: v for k, v in _L1_ffn_all.items() if k in ('gate_w', 'gate_b', 'w1', 'w2', 'w3')}
    del _L1_ffn_all

    def _L2_conv_setup():
        import jax, jax.numpy as jnp
        import numpy as np
        N_STREAMS = 4

        def sinkhorn_knopp(H_tilde, t_max=20):
            M = jnp.exp(H_tilde)
            for _ in range(t_max):
                M = M / jnp.sum(M, axis=-1, keepdims=True)
                M = M / jnp.sum(M, axis=-2, keepdims=True)
            return M
        key = jax.random.key(seed)
        ks = jax.random.split(key, 8)
        B, C, H, W = (32, 64, 56, 56)
        n = N_STREAMS
        nC = n * C
        n_out = 2 * n + n * n
        x = jax.random.normal(ks[0], (B, C, H, W), dtype=jnp.float32)
        phi_w = jax.random.normal(ks[1], (n_out, nC), dtype=jnp.float32) * (1.0 / np.sqrt(nC))
        phi_b = jax.random.normal(ks[2], (n_out,), dtype=jnp.float32) * 0.01
        rms_w = jnp.ones((nC,), dtype=jnp.float32)
        alpha_pre = jnp.full((1,), 0.01, dtype=jnp.float32)
        alpha_post = jnp.full((1,), 0.01, dtype=jnp.float32)
        alpha_res = jnp.full((1,), 0.01, dtype=jnp.float32)
        conv_w = jax.random.normal(ks[3], (C, C, 3, 3), dtype=jnp.float32) * (1.0 / np.sqrt(C * 9))
        conv_b = jax.random.normal(ks[4], (C,), dtype=jnp.float32) * 0.01
        return {'x': x, 'phi_w': phi_w, 'phi_b': phi_b, 'rms_w': rms_w, 'alpha_pre': alpha_pre, 'alpha_post': alpha_post, 'alpha_res': alpha_res, 'conv_w': conv_w, 'conv_b': conv_b}
    _L2_conv_all = _L2_conv_setup()
    _L2_conv_in = {k: v for k, v in _L2_conv_all.items() if k in ('phi_w', 'phi_b', 'rms_w', 'alpha_pre', 'alpha_post', 'alpha_res', 'conv_w', 'conv_b')}
    del _L2_conv_all

    def _L2_ffn_setup():
        import jax, jax.numpy as jnp
        import numpy as np
        NUM_EXPERTS = 8
        TOP_K = 2
        B, S, D = (8, 2048, 64)

        def _moe(tokens, router_w, w1, b1, w2, b2):
            N = tokens.shape[0]
            E = router_w.shape[0]
            logits = tokens.astype(jnp.float32) @ router_w.astype(jnp.float32).T
            probs = jax.nn.softmax(logits, axis=-1)
            rw, re = jax.lax.top_k(probs, TOP_K)
            if TOP_K > 1:
                rw = rw / jnp.maximum(rw.sum(-1, keepdims=True), 1e-12)
            rw = rw.astype(tokens.dtype)
            combine = jnp.zeros((N, E), tokens.dtype).at[jnp.arange(N)[:, None], re].set(rw)
            out = tokens
            for e in range(E):
                h = jax.nn.gelu(tokens @ w1[e] + b1[e], approximate=False)
                y = h @ w2[e] + b2[e]
                out = out + combine[:, e:e + 1] * y
            return out
        key = jax.random.key(seed)
        ks = jax.random.split(key, 4)
        scale = 1.0 / np.sqrt(D).astype(np.float32)
        return {'input_embeddings': jax.random.normal(ks[0], (B, S, D), jnp.float32), 'router_w': jax.random.normal(ks[1], (NUM_EXPERTS, D), jnp.float32) * scale, 'w1': jax.random.normal(ks[2], (NUM_EXPERTS, D, D), jnp.float32) * scale, 'b1': jnp.zeros((NUM_EXPERTS, D), jnp.float32), 'w2': jax.random.normal(ks[3], (NUM_EXPERTS, D, D), jnp.float32) * scale, 'b2': jnp.zeros((NUM_EXPERTS, D), jnp.float32)}
    _L2_ffn_all = _L2_ffn_setup()
    _L2_ffn_in = {k: v for k, v in _L2_ffn_all.items() if k in ('router_w', 'w1', 'b1', 'w2', 'b2')}
    del _L2_ffn_all

    def _L3_conv_setup():
        import jax, jax.numpy as jnp
        import numpy as np
        NUM_CODES = 256
        LATENT_DIM = 64
        key = jax.random.key(seed)
        k1, k2 = jax.random.split(key)
        z = jax.random.normal(k1, (32, LATENT_DIM, 16, 16), dtype=jnp.float32)
        codebook = jax.random.uniform(k2, (NUM_CODES, LATENT_DIM), dtype=jnp.float32, minval=-1.0 / NUM_CODES, maxval=1.0 / NUM_CODES)
        return {'z': z, 'codebook': codebook}
    _L3_conv_all = _L3_conv_setup()
    _L3_conv_in = {k: v for k, v in _L3_conv_all.items() if k in ('codebook',)}
    del _L3_conv_all

    def _L3_ffn_setup():
        import jax, jax.numpy as jnp
        import numpy as np
        B, T, D, H, E = (16, 1024, 64, 128, 8)
        key = jax.random.key(seed)
        ks = jax.random.split(key, 5)
        x = jax.random.normal(ks[0], (B, T, D), dtype=jnp.float32)
        gate_w = jax.random.normal(ks[1], (D, E), dtype=jnp.float32) * 0.02
        gate_b = jnp.zeros((E,), dtype=jnp.float32)
        W1 = jax.random.normal(ks[2], (E, D, H), dtype=jnp.float32) * 0.02
        b1 = jnp.zeros((E, H), dtype=jnp.float32)
        W2 = jax.random.normal(ks[3], (E, H, D), dtype=jnp.float32) * 0.02
        b2 = jnp.zeros((E, D), dtype=jnp.float32)
        return {'x': x, 'gate_w': gate_w, 'gate_b': gate_b, 'W1': W1, 'b1': b1, 'W2': W2, 'b2': b2}
    _L3_ffn_all = _L3_ffn_setup()
    _L3_ffn_in = {k: v for k, v in _L3_ffn_all.items() if k in ('gate_w', 'gate_b', 'W1', 'b1', 'W2', 'b2')}
    del _L3_ffn_all
    return {'x': x, 'L0_conv_Wq': _L0_conv_in['Wq'], 'L0_conv_bq': _L0_conv_in['bq'], 'L0_conv_Wk': _L0_conv_in['Wk'], 'L0_conv_bk': _L0_conv_in['bk'], 'L0_conv_Wv': _L0_conv_in['Wv'], 'L0_conv_bv': _L0_conv_in['bv'], 'L0_conv_Wf': _L0_conv_in['Wf'], 'L0_conv_bf': _L0_conv_in['bf'], 'L0_conv_bn_gamma': _L0_conv_in['bn_gamma'], 'L0_conv_bn_beta': _L0_conv_in['bn_beta'], 'L0_conv_bn_mean': _L0_conv_in['bn_mean'], 'L0_conv_bn_var': _L0_conv_in['bn_var'], 'L0_ffn_router_w': _L0_ffn_in['router_w'], 'L0_ffn_w1': _L0_ffn_in['w1'], 'L0_ffn_b1': _L0_ffn_in['b1'], 'L0_ffn_w2': _L0_ffn_in['w2'], 'L0_ffn_b2': _L0_ffn_in['b2'], 'L1_conv_qkv_w': _L1_conv_in['qkv_w'], 'L1_conv_qkv_b': _L1_conv_in['qkv_b'], 'L1_conv_fc_w': _L1_conv_in['fc_w'], 'L1_conv_fc_b': _L1_conv_in['fc_b'], 'L1_conv_ln_g': _L1_conv_in['ln_g'], 'L1_conv_ln_b': _L1_conv_in['ln_b'], 'L1_conv_proj_w': _L1_conv_in['proj_w'], 'L1_conv_proj_b': _L1_conv_in['proj_b'], 'L1_ffn_gate_w': _L1_ffn_in['gate_w'], 'L1_ffn_gate_b': _L1_ffn_in['gate_b'], 'L1_ffn_w1': _L1_ffn_in['w1'], 'L1_ffn_w2': _L1_ffn_in['w2'], 'L1_ffn_w3': _L1_ffn_in['w3'], 'L2_conv_phi_w': _L2_conv_in['phi_w'], 'L2_conv_phi_b': _L2_conv_in['phi_b'], 'L2_conv_rms_w': _L2_conv_in['rms_w'], 'L2_conv_alpha_pre': _L2_conv_in['alpha_pre'], 'L2_conv_alpha_post': _L2_conv_in['alpha_post'], 'L2_conv_alpha_res': _L2_conv_in['alpha_res'], 'L2_conv_conv_w': _L2_conv_in['conv_w'], 'L2_conv_conv_b': _L2_conv_in['conv_b'], 'L2_ffn_router_w': _L2_ffn_in['router_w'], 'L2_ffn_w1': _L2_ffn_in['w1'], 'L2_ffn_b1': _L2_ffn_in['b1'], 'L2_ffn_w2': _L2_ffn_in['w2'], 'L2_ffn_b2': _L2_ffn_in['b2'], 'L3_conv_codebook': _L3_conv_in['codebook'], 'L3_ffn_gate_w': _L3_ffn_in['gate_w'], 'L3_ffn_gate_b': _L3_ffn_in['gate_b'], 'L3_ffn_W1': _L3_ffn_in['W1'], 'L3_ffn_b1': _L3_ffn_in['b1'], 'L3_ffn_W2': _L3_ffn_in['W2'], 'L3_ffn_b2': _L3_ffn_in['b2']}

def reference(x, L0_conv_Wq, L0_conv_bq, L0_conv_Wk, L0_conv_bk, L0_conv_Wv, L0_conv_bv, L0_conv_Wf, L0_conv_bf, L0_conv_bn_gamma, L0_conv_bn_beta, L0_conv_bn_mean, L0_conv_bn_var, L0_ffn_router_w, L0_ffn_w1, L0_ffn_b1, L0_ffn_w2, L0_ffn_b2, L1_conv_qkv_w, L1_conv_qkv_b, L1_conv_fc_w, L1_conv_fc_b, L1_conv_ln_g, L1_conv_ln_b, L1_conv_proj_w, L1_conv_proj_b, L1_ffn_gate_w, L1_ffn_gate_b, L1_ffn_w1, L1_ffn_w2, L1_ffn_w3, L2_conv_phi_w, L2_conv_phi_b, L2_conv_rms_w, L2_conv_alpha_pre, L2_conv_alpha_post, L2_conv_alpha_res, L2_conv_conv_w, L2_conv_conv_b, L2_ffn_router_w, L2_ffn_w1, L2_ffn_b1, L2_ffn_w2, L2_ffn_b2, L3_conv_codebook, L3_ffn_gate_w, L3_ffn_gate_b, L3_ffn_W1, L3_ffn_b1, L3_ffn_W2, L3_ffn_b2):
    import jax
    import jax.numpy as jnp

    def _L0_conv_ref(x, Wq, bq, Wk, bk, Wv, bv, Wf, bf, bn_gamma, bn_beta, bn_mean, bn_var):
        import jax, jax.numpy as jnp
        import numpy as np
        from math import sqrt
        EPS_PN = 1e-08
        EPS_BN = 1e-05
        NUM_HEADS = 8
        HIDDEN_DIM = 64

        def pixelnorm(x, axis=1):
            return x * jax.lax.rsqrt(jnp.mean(x * x, axis=axis, keepdims=True) + EPS_PN)

        def conv1x1(x, W, b):
            return jnp.einsum('bchw,oc->bohw', x, W) + b[None, :, None, None]
        B, Cin, H, W = x.shape
        g = NUM_HEADS
        Cout = Wq.shape[0]
        hidden_per_head = HIDDEN_DIM // g
        q = pixelnorm(conv1x1(x, Wq, bq))
        k = pixelnorm(conv1x1(x, Wk, bk))
        v = conv1x1(x, Wv, bv)

        def to_heads(t):
            c = t.shape[1] // g
            return t.reshape(B, g, c, H, W).reshape(B * g, c, H, W)
        q, k, v = (to_heads(q), to_heads(k), to_heads(v))
        kv = jnp.einsum('bchw,bChw->bcC', k, v)
        qkv = jnp.einsum('bchw,bcC->bChw', q, pixelnorm(kv, axis=1))
        Cq = qkv.shape[1] - hidden_per_head
        qkv, gate_in = (qkv[:, :Cq], qkv[:, Cq:])
        T = sqrt(H * W)
        hidden_gate = jnp.mean(gate_in, axis=1, keepdims=True)
        gate = jax.nn.softmax((hidden_gate / T).reshape(B * g, -1), axis=-1)
        gate = gate.reshape(B * g, 1, H, W)
        qkgv = gate * qkv
        qkgv = qkgv.reshape(B, g, Cq, H, W).reshape(B, g * Cq, H, W)
        y = conv1x1(qkgv, Wf, bf)
        y = (y - bn_mean[None, :, None, None]) * jax.lax.rsqrt(bn_var + EPS_BN)[None, :, None, None]
        y = y * bn_gamma[None, :, None, None] + bn_beta[None, :, None, None]
        return jax.nn.relu(y)

    def _L0_ffn_ref(input_embeddings, router_w, w1, b1, w2, b2):
        import jax, jax.numpy as jnp
        import numpy as np
        NUM_EXPERTS = 8
        TOP_K = 2
        B, S, D = (8, 2048, 64)

        def _moe(tokens, router_w, w1, b1, w2, b2):
            N = tokens.shape[0]
            E = router_w.shape[0]
            logits = tokens.astype(jnp.float32) @ router_w.astype(jnp.float32).T
            probs = jax.nn.softmax(logits, axis=-1)
            rw, re = jax.lax.top_k(probs, TOP_K)
            if TOP_K > 1:
                rw = rw / jnp.maximum(rw.sum(-1, keepdims=True), 1e-12)
            rw = rw.astype(tokens.dtype)
            combine = jnp.zeros((N, E), tokens.dtype).at[jnp.arange(N)[:, None], re].set(rw)
            out = tokens
            for e in range(E):
                h = jax.nn.gelu(tokens @ w1[e] + b1[e], approximate=False)
                y = h @ w2[e] + b2[e]
                out = out + combine[:, e:e + 1] * y
            return out
        b, s, d = input_embeddings.shape
        tokens = input_embeddings.reshape(b * s, d)
        return _moe(tokens, router_w, w1, b1, w2, b2).reshape(b, s, d)

    def _L1_conv_ref(x, qkv_w, qkv_b, fc_w, fc_b, ln_g, ln_b, proj_w, proj_b):
        import jax, jax.numpy as jnp
        import numpy as np
        DIM = 64
        NUM_HEADS = 8
        HEAD_DIM = DIM // NUM_HEADS
        DILATIONS = (1, 2, 4, 8)
        ND = len(DILATIONS)
        K = 3
        KK = K * K
        SCALE = HEAD_DIM ** (-0.5)
        LN_EPS = 1e-05

        def _unfold(t, dil, k=K):
            B, d, H, W = t.shape
            p = dil * (k - 1) // 2
            tp = jnp.pad(t, ((0, 0), (0, 0), (p, p), (p, p)))
            patches = [tp[:, :, i * dil:i * dil + H, j * dil:j * dil + W] for i in range(k) for j in range(k)]
            return jnp.stack(patches, axis=2)
        B, C, H, W = x.shape
        d = C // ND
        h = d // HEAD_DIM
        L = H * W
        qkv = jnp.einsum('bchw,oc->bohw', x, qkv_w) + qkv_b[None, :, None, None]
        qkv = qkv.reshape(B, 3, ND, d, H, W)
        feats = []
        for i, dil in enumerate(DILATIONS):
            q = qkv[:, 0, i]
            kmap = qkv[:, 1, i]
            vmap = qkv[:, 2, i]
            qr = q.reshape(B, h, HEAD_DIM, L)
            ku = _unfold(kmap, dil).reshape(B, h, HEAD_DIM, KK, L)
            vu = _unfold(vmap, dil).reshape(B, h, HEAD_DIM, KK, L)
            attn = jnp.einsum('bhcl,bhcpl->bhlp', qr, ku) * SCALE
            attn = jax.nn.softmax(attn, axis=-1)
            out = jnp.einsum('bhlp,bhcpl->bhlc', attn, vu)
            feats.append(out.transpose(0, 2, 1, 3).reshape(B, H, W, d))
        stacked = jnp.stack(feats, axis=3)
        fused = jnp.einsum('bhwsc,ts->bhwtc', stacked, fc_w) + fc_b[None, None, None, :, None]
        fused = fused + stacked
        mu = fused.mean(axis=-1, keepdims=True)
        var = fused.var(axis=-1, keepdims=True)
        fused = (fused - mu) * jax.lax.rsqrt(var + LN_EPS) * ln_g + ln_b
        y2 = fused.reshape(B, H, W, C)
        y3 = y2 @ proj_w.T + proj_b
        return y3.transpose(0, 3, 1, 2)

    def _L1_ffn_ref(x, gate_w, gate_b, w1, w2, w3):
        import jax, jax.numpy as jnp
        import numpy as np
        D_MODEL = 64
        N_EXPERTS = 16
        HIDDEN = 128
        SCALE = 0.02
        n_experts = w1.shape[0]
        logits = jnp.einsum('bsd,de->bse', x, gate_w) + gate_b
        probs = jax.nn.softmax(logits, axis=-1)
        top_probs, top_idx = jax.lax.top_k(probs, 2)
        top_probs = top_probs / jnp.sum(top_probs, axis=-1, keepdims=True)
        dispatch = jnp.sum(jax.nn.one_hot(top_idx, n_experts, dtype=x.dtype) * top_probs[..., None], axis=-2)
        h1 = jnp.einsum('bsd,edh->bseh', x, w1)
        h2 = jnp.einsum('bsd,edh->bseh', x, w2)
        hidden = jax.nn.silu(h1) * h2
        expert_out = jnp.einsum('bseh,eho->bseo', hidden, w3)
        return jnp.einsum('bseo,bse->bso', expert_out, dispatch)

    def _L2_conv_ref(x, phi_w, phi_b, rms_w, alpha_pre, alpha_post, alpha_res, conv_w, conv_b):
        import jax, jax.numpy as jnp
        import numpy as np
        N_STREAMS = 4

        def sinkhorn_knopp(H_tilde, t_max=20):
            M = jnp.exp(H_tilde)
            for _ in range(t_max):
                M = M / jnp.sum(M, axis=-1, keepdims=True)
                M = M / jnp.sum(M, axis=-2, keepdims=True)
            return M
        n = N_STREAMS
        B, C, H, W = x.shape
        nC = n * C
        x_l = jnp.broadcast_to(x[:, None], (B, n, C, H, W))
        x_pooled = jnp.mean(x_l.reshape(B, nC, H, W), axis=(2, 3))
        x_norm = x_pooled * jax.lax.rsqrt(jnp.mean(x_pooled * x_pooled, axis=-1, keepdims=True) + 1e-20) * rms_w
        coeffs = x_norm @ phi_w.T + phi_b
        H_pre = jax.nn.sigmoid(alpha_pre * coeffs[:, :n])
        H_post = 2.0 * jax.nn.sigmoid(alpha_post * coeffs[:, n:2 * n])
        H_res = sinkhorn_knopp(alpha_res * coeffs[:, 2 * n:].reshape(B, n, n))
        h_in = jnp.einsum('bn,bnchw->bchw', H_pre, x_l)
        h_out = jax.lax.conv_general_dilated(h_in, conv_w, (1, 1), 'SAME', dimension_numbers=('NCHW', 'OIHW', 'NCHW'))
        h_out = h_out + conv_b[None, :, None, None]
        post_part = jnp.einsum('bn,bchw->bnchw', H_post, h_out)
        res_part = jnp.einsum('bnn,bnchw->bnchw', H_res, x_l)
        return jnp.mean(res_part + post_part, axis=1)

    def _L2_ffn_ref(input_embeddings, router_w, w1, b1, w2, b2):
        import jax, jax.numpy as jnp
        import numpy as np
        NUM_EXPERTS = 8
        TOP_K = 2
        B, S, D = (8, 2048, 64)

        def _moe(tokens, router_w, w1, b1, w2, b2):
            N = tokens.shape[0]
            E = router_w.shape[0]
            logits = tokens.astype(jnp.float32) @ router_w.astype(jnp.float32).T
            probs = jax.nn.softmax(logits, axis=-1)
            rw, re = jax.lax.top_k(probs, TOP_K)
            if TOP_K > 1:
                rw = rw / jnp.maximum(rw.sum(-1, keepdims=True), 1e-12)
            rw = rw.astype(tokens.dtype)
            combine = jnp.zeros((N, E), tokens.dtype).at[jnp.arange(N)[:, None], re].set(rw)
            out = tokens
            for e in range(E):
                h = jax.nn.gelu(tokens @ w1[e] + b1[e], approximate=False)
                y = h @ w2[e] + b2[e]
                out = out + combine[:, e:e + 1] * y
            return out
        b, s, d = input_embeddings.shape
        tokens = input_embeddings.reshape(b * s, d)
        return _moe(tokens, router_w, w1, b1, w2, b2).reshape(b, s, d)

    def _L3_conv_ref(z, codebook):
        import jax, jax.numpy as jnp
        import numpy as np
        NUM_CODES = 256
        LATENT_DIM = 64
        z_nhwc = jnp.transpose(z, (0, 2, 3, 1))
        B, H, W, C = z_nhwc.shape
        z_flat = z_nhwc.reshape(-1, C)
        d = jnp.sum(z_flat * z_flat, axis=1, keepdims=True) + jnp.sum(codebook * codebook, axis=1) - 2.0 * jnp.einsum('nc,kc->nk', z_flat, codebook)
        idx = jnp.argmin(d, axis=1)
        z_q = codebook[idx].reshape(B, H, W, C)
        z_q = z_nhwc + jax.lax.stop_gradient(z_q - z_nhwc)
        return jnp.transpose(z_q, (0, 3, 1, 2))

    def _L3_ffn_ref(x, gate_w, gate_b, W1, b1, W2, b2):
        import jax, jax.numpy as jnp
        import numpy as np
        B, T, D, H, E = (16, 1024, 64, 128, 8)
        Bb, Tt, Dd = x.shape
        Ee = gate_w.shape[1]
        xf = x.reshape(-1, Dd)
        N = xf.shape[0]
        logits = xf @ gate_w + gate_b
        probs = jax.nn.softmax(logits, axis=-1)
        top2_vals, top2_idx = jax.lax.top_k(probs, 2)
        cw = jnp.zeros((N, Ee), dtype=xf.dtype).at[jnp.arange(N)[:, None], top2_idx].add(top2_vals)

        def step(acc, params):
            w1, bb1, w2, bb2, we = params
            h = jax.nn.gelu(xf @ w1 + bb1, approximate=False)
            y = h @ w2 + bb2
            return (acc + we[:, None] * y, None)
        out, _ = jax.lax.scan(step, jnp.zeros_like(xf), (W1, b1, W2, b2, cw.T))
        return out.reshape(Bb, Tt, Dd)

    def _gn(v, G=32, eps=1e-05):
        B_, C_, H_, W_ = v.shape
        g = v.reshape(B_, G, C_ // G, H_, W_)
        m = jnp.mean(g, axis=(2, 3, 4), keepdims=True)
        s = jnp.var(g, axis=(2, 3, 4), keepdims=True)
        return ((g - m) / jnp.sqrt(s + eps)).reshape(v.shape)

    def _ln_c(v, eps=1e-06):
        m = jnp.mean(v, axis=1, keepdims=True)
        s = jnp.var(v, axis=1, keepdims=True)
        return (v - m) / jnp.sqrt(s + eps)

    def _ln_t(v, eps=1e-05):
        m = jnp.mean(v, axis=-1, keepdims=True)
        s = jnp.var(v, axis=-1, keepdims=True)
        return (v - m) / jnp.sqrt(s + eps)

    def _to_tokens(v):
        B_, C_, H_, W_ = v.shape
        return v.reshape(B_, C_, H_ * W_).transpose(0, 2, 1)

    def _from_tokens(t, like):
        B_, C_, H_, W_ = like.shape
        return t.transpose(0, 2, 1).reshape(B_, C_, H_, W_)
    x = x + _L0_conv_ref(_ln_c(x), L0_conv_Wq, L0_conv_bq, L0_conv_Wk, L0_conv_bk, L0_conv_Wv, L0_conv_bv, L0_conv_Wf, L0_conv_bf, L0_conv_bn_gamma, L0_conv_bn_beta, L0_conv_bn_mean, L0_conv_bn_var)
    t = _to_tokens(x)
    t = t + _L0_ffn_ref(_ln_t(t), L0_ffn_router_w, L0_ffn_w1, L0_ffn_b1, L0_ffn_w2, L0_ffn_b2)
    x = _from_tokens(t, x)
    x = x + _L1_conv_ref(_ln_c(x), L1_conv_qkv_w, L1_conv_qkv_b, L1_conv_fc_w, L1_conv_fc_b, L1_conv_ln_g, L1_conv_ln_b, L1_conv_proj_w, L1_conv_proj_b)
    t = _to_tokens(x)
    t = t + _L1_ffn_ref(_ln_t(t), L1_ffn_gate_w, L1_ffn_gate_b, L1_ffn_w1, L1_ffn_w2, L1_ffn_w3)
    x = _from_tokens(t, x)
    x = x + _L2_conv_ref(_ln_c(x), L2_conv_phi_w, L2_conv_phi_b, L2_conv_rms_w, L2_conv_alpha_pre, L2_conv_alpha_post, L2_conv_alpha_res, L2_conv_conv_w, L2_conv_conv_b)
    t = _to_tokens(x)
    t = t + _L2_ffn_ref(_ln_t(t), L2_ffn_router_w, L2_ffn_w1, L2_ffn_b1, L2_ffn_w2, L2_ffn_b2)
    x = _from_tokens(t, x)
    x = x + _L3_conv_ref(_ln_c(x), L3_conv_codebook)
    t = _to_tokens(x)
    t = t + _L3_ffn_ref(_ln_t(t), L3_ffn_gate_w, L3_ffn_gate_b, L3_ffn_W1, L3_ffn_b1, L3_ffn_W2, L3_ffn_b2)
    x = _from_tokens(t, x)
    return x

_drawn_inputs = setup_inputs


def setup_inputs(seed=0):
    import zlib

    import numpy as np

    out = dict(_drawn_inputs(seed))
    spreads = {'L0_ffn_b1': (0.0, 0.1),
     'L0_ffn_b2': (0.0, 0.1),
     'L1_conv_qkv_b': (0.0, 0.1),
     'L1_conv_fc_b': (0.0, 2.0),
     'L1_conv_ln_g': (1.0, 0.2),
     'L1_conv_ln_b': (0.0, 0.1),
     'L1_conv_proj_b': (0.0, 0.1),
     'L1_ffn_gate_b': (0.0, 0.8),
     'L2_conv_rms_w': (1.0, 0.6),
     'L2_ffn_b1': (0.0, 0.636),
     'L2_ffn_b2': (0.0, 0.455),
     'L3_ffn_gate_b': (0.0, 0.8),
     'L3_ffn_b1': (0.0, 0.8),
     'L3_ffn_b2': (0.0, 0.8)}
    factors = {'L0_conv_Wq': 4.22,
     'L0_conv_bq': 23.349,
     'L0_conv_Wk': 3.87,
     'L0_conv_bk': 8.0,
     'L0_conv_Wv': 3.784,
     'L0_conv_bv': 8.0,
     'L0_conv_Wf': 3.752,
     'L0_conv_bn_var': 4.7,
     'L1_ffn_gate_w': 8.0,
     'L1_ffn_w1': 8.0,
     'L1_ffn_w2': 8.0,
     'L1_ffn_w3': 8.0,
     'L2_conv_phi_w': 26.995,
     'L2_conv_phi_b': 64.0,
     'L2_conv_conv_b': 8.0,
     'L3_conv_codebook': 64.0,
     'L3_ffn_gate_w': 8.0,
     'L3_ffn_W1': 8.0,
     'L3_ffn_W2': 8.0}
    for name, (base, spread) in spreads.items():
        noise = np.random.default_rng([zlib.crc32(name.encode()), seed]).standard_normal(out[name].shape)
        drawn = base * np.exp(spread * noise) if base else spread * noise
        out[name] = jnp.asarray(drawn.astype(out[name].dtype))
    for name, factor in factors.items():
        out[name] = (out[name] * factor).astype(out[name].dtype)
    return out
```

```python
import concourse.bass as bass
from concourse import mybir
from contextlib import ExitStack

B, C, H, W = 8, 64, 16, 16
P = 128
NT = B * H * W // P
HALF = NT // 2
NPIX = H * W
DILS = (1, 2, 4, 8)
PADX = 8
CODES = 256
EPS_C, EPS_T = 1e-6, 1e-5

MOE = [dict(E=8, D2=64, act="gelu", skip=True, norm=True, swiglu=False),
       dict(E=16, D2=128, act="silu", skip=False, norm=True, swiglu=True),
       dict(E=8, D2=64, act="gelu", skip=True, norm=True, swiglu=False),
       dict(E=8, D2=128, act="gelu", skip=False, norm=False, swiglu=False)]

PACKS = {
    "c0": [("ident", P, P), ("xT", P, NT * C), ("wqkv", P, 256), ("bqkv", P, 256), ("headmask", P, 128),
           ("headmean", P, P)],
    "c1": [("xR", P, NT * C), ("wf", P, 64), ("bf", P, 64), ("bng", P, 64), ("bnb", P, 64),
           ("bnm", P, 64), ("bnv", P, 64)],
    "m0": [("rw0", P, 8), ("w1_0", P, 512), ("b1_0", P, 4), ("w2_0", P, 256), ("b2_0", 24, 64), ("rank8", P, 8),
           ("rank16", P, 16)],
    "l1": [("qkvw", P, 192), ("qkvb", P, 192), ("shift", P, 8 * P), ("fcrep", P, 4), ("fcb", P, 4), ("fcmask", P, 64),
           ("lng", P, 1), ("lnb", P, P), ("projw", P, 64), ("projb", P, 64)],
    "m1": [("rw1", P, 16), ("gb1", P, 16), ("w1_1", P, 2048), ("wu_1", P, 2048), ("w2_1", P, 1024)],
    "l2": [("samebatch", P, P), ("phi", 64, 96), ("rms", 64, 4), ("phib", P, 24), ("alpha", P, 24),
           ("convp", P, 192), ("convs", P, 192), ("convb", P, 64)],
    "m2": [("rw2", P, 8), ("w1_2", P, 512), ("b1_2", P, 4), ("w2_2", P, 256), ("b2_2", 24, 64)],
    "l3": [("cbT", P, CODES), ("halfones", P, P)],
    "m3": [("rw3", P, 8), ("gb3", P, 8), ("w1_3", P, 1024), ("b1_3", P, 8), ("w2_3", P, 512), ("b2_3", 24, 64)],
}
BF_PACK = [("identb", P, P), ("sel0", 24, 4 * P), ("sel1", 48, 16 * P), ("sel3", 24, 8 * P)]


def pack_columns(spec):
    at, where = 0, {}
    for name, rows, cols in spec:
        where[name] = (at, rows, cols)
        at += cols
    return where, at


def metaformer(nc: bass.Bass, dram, codebook, out):
    fp32, bf16, u32 = mybir.dt.float32, mybir.dt.bfloat16, mybir.dt.uint32
    ALU = mybir.AluOpType
    ACT = mybir.ActivationFunctionType
    AX = mybir.AxisListType.X

    ctx = ExitStack()
    with ctx:
        def sb(name, shape, dt=fp32):
            return ctx.enter_context(nc.sbuf_tensor(name, shape, dt))

        def sem(name):
            return ctx.enter_context(nc.semaphore(name))

        packs, K = {}, {}
        for pk, spec in PACKS.items():
            where, width = pack_columns(spec)
            packs[pk] = sb("pack_" + pk, [P, width])
            for name, (at, rows, cols) in where.items():
                K[name] = packs[pk][0:rows, at:at + cols]
        where, width = pack_columns(BF_PACK)
        packs["bf"] = sb("pack_bf", [P, width], bf16)
        for name, (at, rows, cols) in where.items():
            K[name] = packs["bf"][0:rows, at:at + cols]

        res = sb("res", [P, NT, C])
        base = sb("base", [P, NT, C])
        xnp = sb("xnp", [P, NT + 2, C])
        xn = xnp[:, 1:NT + 1, :]
        xnC = sb("xnC", [P, HALF, P])
        bst = sb("bst", [P, NT, 6])
        mv = sb("mv", [P, NT, 2])
        veps = sb("veps", [P, 64])
        rstd = sb("rstd", [P, 64])
        mhalf = sb("mhalf", [P, 512])

        kvx_mem = sb("kvx_mem", [P, 3 * (NT + 2 * PADX) * 2 * C])
        qkv = kvx_mem[:, 0:NT * 256].rearrange("p (t c) -> p t c", c=256)
        big = sb("big", [P, 2 * 2304])
        qC = sb("qC", [P, HALF, P])
        ms = sb("ms", [P, 32])
        kvm = sb("kvm", [P, 4, P])
        kvs = sb("kvs", [P, 4, P])
        kvr = sb("kvr", [P, 4, P])
        gsum = sb("gsum", [P, 4, 8])
        bdc = sb("bdc", [P, 4, 2, 64])
        bdg = sb("bdg", [P, 4, 2, 64])
        eg = big[:, 2048:3072].rearrange("p (j n) -> p j n", j=4)
        qkg = big[:, 3072:4096].rearrange("p (j n) -> p j n", j=4)
        bns = sb("bns", [P, 64])
        wfs = sb("wfs", [P, 64])
        bfs = sb("bfs", [P, 64])
        ones = sb("ones", [P, 64])
        small = sb("small", [P, 64])

        q1 = sb("q1", [P, NT, C])
        kvx = kvx_mem[:, :].rearrange("p (r x a c) -> p r x a c", r=3, a=2, c=C)
        lg = sb("lg", [P, NT, 4, 2, 9])
        le = lg
        lm = sb("lm", [P, P])
        ls = sb("ls", [P, P])
        stk = q1
        mix = sb("mix", [64 * 2, 64])
        projs = sb("projs", [P, 64])
        pbias = sb("pbias", [P, 64])
        fx = sb("fx", [P, NT, C])
        fq = qC[:, :, :].rearrange("p i (t c) -> p (i t) c", c=C)

        stack = kvx_mem[:, 0:3 * (NT + 1) * P].rearrange("p (r x b y) -> p r x b y", r=3, b=B, y=H)
        xsum = sb("xsum", [P, 64])
        pooled = sb("pooled", [P, 64])
        pooledT = sb("pooledT", [64, P])
        phig = sb("phig", [64, 24, 4])
        phis = sb("phis", [64, 24])
        co = sb("co", [P, 24])
        hx = sb("hx", [P, 24])
        rs4 = sb("rs4", [P, 4])
        sc = sb("sc", [P, 8])
        cbs = sb("cbs", [P, 64])

        cc, cb2 = kvx_mem[:, 0:CODES], kvx_mem[:, CODES:2 * CODES]
        zc = kvx_mem[:, 512:1024].rearrange("p (a c) -> p a c", a=2)
        nd = kvx_mem[:, 1024:1536].rearrange("p (a c) -> p a c", a=2)
        mx8 = sb("mx8", [P, NT, 8])
        ix8 = sb("ix8", [P, NT, 8], u32)
        zz = sb("zz", [P, NT])
        zq = kvx_mem[:, 2048:2048 + NT * C].rearrange("p (t c) -> p t c", c=C)

        rl = sb("rl", [P, NT, 16])
        rp = sb("rp", [P, NT, 16])
        rk = sb("rk", [P, NT, 16])
        o1 = sb("o1", [P, NT, 16])
        o2 = sb("o2", [P, NT, 16])
        rm = [sb(f"rm{i}", [P, NT]) for i in range(6)]
        c3 = sb("c3", [P, NT, 48], bf16)
        cT = sb("cT", [48, NT * P], bf16)
        b2s = sb("b2s", [24, 3, 64], bf16)
        b2f = sb("b2f", [24, 64])
        g = sb("g", [P, 3, 512])
        u = big[:, 0:1024].rearrange("p (a c) -> p a c", a=2)
        gc = sb("gc", [P, 3, 512])

        bank = [ctx.enter_context(nc.psum_tensor(f"bank{i}", [P, 512], fp32)) for i in range(8)]

        loaded = {pk: sem("loaded_" + pk) for pk in packs}
        S = {n: sem(n) for n in (
            "vec_step act_step pool_step stats_ready rstd_ready normed normed_T chan_ready "
            "setup_ready consts_set qkv_out qkv_in sq_ready ms_ready mrs_ready qk_normed q_T q_chan kv_out kv_sq "
            "kvn_out kvn_eps kvn_rs heads_ready gate_out gmax_ready gexp_ready gated wf_in wf_out "
            "logits_out sub_ready exp_ready comb_ready comb_T comb_chan b2_ready "
            "h_out act_out cb_out gc_ready second_out acc_in "
            "kv1_out kv1_in shift_out shift_in att_sub att_exp stk_ready stk_T stk_chan mix_set mix_out pb_out pbias_in "
            "cent_ready fsq_ready fvar_ready frs_ready fln_ready fln_T fln_chan proj_out "
            "pads_set stack_set stack_T stack_in xsum_ready pool_out phis_ready poolT_in co_out pvar_ready prs_ready cz_ready "
            "ce_ready conv_out cb_sq zz_ready zc_ready dot_out dot_in idx_ready gathered vqdone stored").split()}

        block = ctx.enter_context(nc.Block())

        chunks = 4
        CH = {0: 0, 1: 1, 2: 2, 3: 3, 5: 4, 6: 5, 7: 6}
        units = [m["E"] * m["D2"] // P for m in MOE]
        first_unit = [chunks * sum(units[:m]) for m in range(4)]

        def tiles(h, i, k):
            return slice(2 * i + h, 2 * (i + k) + h - 1, 2)

        @block.sync
        def _(sp):
            for pk in ("c0", "m0", "l1", "l2", "l3"):
                sp.dma_start(packs[pk][:, :], dram[pk]).then_inc(loaded[pk], 16)
            for c in range(chunks):
                sp.wait_ge(S["acc_in"], 3 * chunks + c + 1)
                t = tiles(c // 2, 4 * (c % 2), 4)
                sp.dma_start(out[:, t, :], res[:, t, :]).then_inc(S["stored"], 16)
            sp.wait_ge(S["stored"], 16 * chunks)

        @block.gpsimd
        def _(pool):
            nc.gpsimd.memset(mhalf[:, :], -0.5).then_inc(S["consts_set"], 1)
            nc.gpsimd.memset(ones[:, :], 1.0).then_inc(S["consts_set"], 1)
            nc.gpsimd.memset(bdc[:, :, :, :], 0.0).then_inc(S["consts_set"], 1)
            nc.gpsimd.memset(bdg[:, :, :, :], 0.0).then_inc(S["consts_set"], 1)
            nc.gpsimd.memset(xnp[:, :, :], 0.0).then_inc(S["consts_set"], 1)
            pool.wait_ge(S["consts_set"], 1)

            def rsqrt(dst, src, ready, value, done):
                pool.wait_ge(ready, value)
                nc.gpsimd.tensor_tensor(dst, src, mhalf[:, 0:src.shape[1]], ALU.pow).then_inc(done, 1)

            def ln_rstd(s):
                rsqrt(rstd[:, 0:NT], veps[:, 0:NT], S["stats_ready"], s + 1, S["rstd_ready"])

            rsqrt(bns[:, :], small[:, :], S["setup_ready"], 1, S["mrs_ready"])
            ln_rstd(0)
            rsqrt(ms[:, :], veps[:, 0:32], S["ms_ready"], 1, S["mrs_ready"])
            rsqrt(kvr[:, :, :].rearrange("p a b -> p (a b)"), kvs[:, :, :].rearrange("p a b -> p (a b)"),
                  S["kvn_eps"], 1, S["kvn_rs"])
            ln_rstd(1)
            pool.wait_ge(S["kv_out"], 1)
            pool.wait_ge(S["q_T"], 2)
            nc.gpsimd.memset(kvx_mem[:, :], 0.0).then_inc(S["pads_set"], 1)
            ln_rstd(2)
            rsqrt(rstd[:, :], veps[:, :], S["fvar_ready"], 1, S["frs_ready"])
            ln_rstd(3)
            pool.wait_ge(S["stk_ready"], 1)
            nc.gpsimd.memset(kvx_mem[:, 0:3 * (NT + 1) * P], 0.0).then_inc(S["stack_set"], 1)
            ln_rstd(4)
            rsqrt(sc[:, 1:2], sc[:, 0:1], S["pvar_ready"], 1, S["prs_ready"])
            for s in (5, 6):
                ln_rstd(s)
            for k in range(NT):
                x = 2 * (k % HALF) + k // HALF
                pool.wait_ge(S["idx_ready"], k + 1)
                nc.gpsimd.indirect_dma_start(
                    out=zq[:, x, :], out_offset=None, in_=codebook,
                    in_offset=bass.IndirectOffsetOnAxis(ap=ix8[:, x, 0:1], axis=0)).then_inc(S["gathered"], 16)
            ln_rstd(7)

        @block.scalar
        def _(act):
            for pk in ("c1", "bf", "m1", "m2", "m3"):
                act.dma_start(packs[pk][:, :], dram[pk]).then_inc(loaded[pk], 16)

            def ln_chan(s):
                for j in range(2):
                    act.wait_ge(S["normed_T"], 2 * CH[s] + j + 1)
                    nc.scalar.activation(xnC[:, 4 * j:4 * j + 4, :], bank[6 + j][:, :], ACT.Copy)\
                        .then_inc(S["chan_ready"], 1)

            def moe(m):
                cfg = MOE[m]
                E = cfg["E"]
                act.wait_ge(S["sub_ready"], m + 1)
                nc.scalar.activation(rp[:, :, 0:E], rl[:, :, 0:E], ACT.Exp).then_inc(S["exp_ready"], 1)
                for j in range(2):
                    act.wait_ge(S["comb_T"], 2 * m + j + 1)
                    nc.scalar.activation(cT[0:3 * E, 1024 * j:1024 * j + 1024],
                                         bank[4 + j][0:3 * E, :].bitcast(bf16), ACT.Copy)\
                        .then_inc(S["comb_chan"], 1)
                for c in range(chunks):
                    for un in range(units[m]):
                        n = first_unit[m] + c * units[m] + un
                        act.wait_ge(S["h_out"], n + 1)
                        if n >= 3:
                            act.wait_ge(S["gc_ready"], n - 2)
                        if cfg["swiglu"]:
                            nc.scalar.activation(g[:, n % 3, :], bank[n % 2][:, :], ACT.Silu)\
                                .then_inc(S["act_out"], 1)
                        else:
                            nc.scalar.activation(g[:, n % 3, :], bank[n % 2][:, :], ACT.Gelu,
                                                 bias=K[f"b1_{m}"][:, un:un + 1]).then_inc(S["act_out"], 1)

            ln_chan(0)
            act.wait_ge(S["qkv_in"], 8)
            nc.scalar.activation(big[:, 0:2048].rearrange("p (t c) -> p t c", c=P), qkv[:, :, 0:P], ACT.Square)\
                .then_inc(S["sq_ready"], 1)
            for j in range(2):
                act.wait_ge(S["q_T"], j + 1)
                nc.scalar.activation(qC[:, 4 * j:4 * j + 4, :], bank[6 + j][:, :], ACT.Copy)\
                    .then_inc(S["q_chan"], 1)
            act.wait_ge(S["gmax_ready"], 1)
            for j in range(4):
                nc.scalar.activation(eg[:, j, :], bank[2 + j // 2][:, 256 * (j % 2):256 * (j % 2) + 256], ACT.Exp,
                                     bias=small[:, 4 + j:5 + j], scale=1.0 / 128,
                                     accum_out=small[:, 8 + j:9 + j]).then_inc(S["gexp_ready"], 1)
            ln_chan(1)
            for pk in ("m0",):
                act.wait_ge(loaded[pk], 16)
            moe(0)
            ln_chan(2)
            act.wait_ge(S["pads_set"], 1)
            for n in range(8):
                i, r = n // 2, 2 * (n % 2)
                act.wait_ge(S["shift_out"], n + 1)
                for kv in range(2):
                    nc.scalar.activation(kvx[:, r, PADX:PADX + NT, kv, 16 * i:16 * i + 16],
                                         bank[n][:, :].rearrange("p (x a c) -> p x a c", a=2, c=16)[:, :, kv, :],
                                         ACT.Copy).then_inc(S["shift_in"], 1)
            act.wait_ge(S["att_sub"], 1)
            nc.scalar.activation(le[:, :, :, :, :], lg[:, :, :, :, :], ACT.Exp, scale=8 ** -0.5)\
                .then_inc(S["att_exp"], 1)
            for j in range(2):
                act.wait_ge(S["stk_T"], j + 1)
                nc.scalar.activation(xnC[:, 4 * j:4 * j + 4, :], bank[6 + j][:, :], ACT.Copy)\
                    .then_inc(S["stk_chan"], 1)
            act.wait_ge(S["cent_ready"], 1)
            nc.scalar.activation(fq[:, :, :], fx[:, :, :], ACT.Square).then_inc(S["fsq_ready"], 1)
            for j in range(2):
                act.wait_ge(S["fln_T"], j + 1)
                nc.scalar.activation(xnC[:, 4 * j:4 * j + 4, :], bank[6 + j][:, :], ACT.Copy)\
                    .then_inc(S["fln_chan"], 1)
            ln_chan(3)
            moe(1)
            act.wait_ge(S["stack_set"], 1)
            for n in range(5):
                act.wait_ge(S["stack_T"], n + 1)
                k = min(4, NT + 1 - 4 * n)
                src = bank[n][:, 0:P * k].rearrange("p (x b y) -> p (x b) y", b=B, y=H)
                for r in range(3):
                    y0, y1 = max(0, 1 - r), min(H, H + 1 - r)
                    nc.scalar.activation(
                        stack[:, r, 4 * n:4 * n + k, :, :].rearrange("p x b y -> p (x b) y")[:, :, y0:y1],
                        src[:, :, y0 + r - 1:y1 + r - 1], ACT.Copy).then_inc(S["stack_in"], 1)
            act.wait_ge(S["cz_ready"], 1)
            nc.scalar.activation(hx[:, 0:8], co[:, 0:8], ACT.Exp, scale=-1.0).then_inc(S["ce_ready"], 1)
            nc.scalar.activation(hx[:, 8:24], co[:, 8:24], ACT.Exp).then_inc(S["ce_ready"], 1)
            ln_chan(5)
            act.wait_ge(loaded["m2"], 16)
            moe(2)
            ln_chan(6)
            act.wait_ge(S["zz_ready"], 1)
            for k in range(NT):
                x = 2 * (k % HALF) + k // HALF
                if k >= 2:
                    act.wait_ge(S["dot_in"], k - 1)
                nc.scalar.activation(zc[:, k % 2, :], cc, ACT.Identity, bias=zz[:, x:x + 1])\
                    .then_inc(S["zc_ready"], 1)
            ln_chan(7)
            act.wait_ge(loaded["m3"], 16)
            moe(3)

        @block.vector
        def _(dve):
            V = nc.vector
            steps = [0]

            def seq(ins):
                steps[0] += 1
                ins.then_inc(S["vec_step"], 1)
                dve.wait_ge(S["vec_step"], steps[0])

            def bc(ap, n):
                return ap.unsqueeze(len(ap.shape)).broadcast_to(list(ap.shape) + [n])

            def row(ap, n):
                return ap.unsqueeze(1).broadcast_to([ap.shape[0], n] + list(ap.shape[1:]))

            def ln(s, src, eps):
                for x in range(NT):
                    last = V.bn_stats(bst[:, x, :], src[:, x, :])
                seq(last)
                for x in range(NT):
                    last = V.bn_aggr(mv[:, x, :], bst[:, x, :])
                seq(last)
                V.tensor_scalar_add(veps[:, 0:NT], mv[:, :, 1], eps).then_inc(S["stats_ready"], 1)
                dve.wait_ge(S["rstd_ready"], s + 1)
                if s == 0:
                    dve.wait_ge(S["consts_set"], 5)
                for i in range(HALF):
                    for x in (2 * i, 2 * i + 1):
                        last = V.tensor_scalar(xn[:, x, :], src[:, x, :], mv[:, x, 0:1], rstd[:, x:x + 1],
                                               ALU.subtract, ALU.mult)
                    last.then_inc(S["normed"], 1)

            def routing(m):
                cfg = MOE[m]
                E = cfg["E"]
                L, Pb, Kk, O1, O2 = (a[:, :, 0:E] for a in (rl, rp, rk, o1, o2))
                mxl, sm, m1, m2, r1, den = (a[:, :] for a in rm)
                rank = row(K["rank8" if E == 8 else "rank16"], NT)
                dve.wait_ge(S["logits_out"], 2 * m + 2)
                for h in range(2):
                    src = bank[4 + h][:, 0:HALF * E].rearrange("p (t e) -> p t e", e=E)
                    dst = rl[:, h:NT:2, 0:E]
                    if f"gb{m}" in K:
                        last = V.tensor_tensor(dst, src, row(K[f"gb{m}"], HALF), ALU.add)
                    else:
                        last = V.tensor_copy(dst, src)
                seq(last)
                seq(V.tensor_reduce(mxl, L, AX, ALU.max))
                V.tensor_tensor(L, L, bc(mxl, E), ALU.subtract).then_inc(S["sub_ready"], 1)
                if cfg["skip"]:
                    V.tensor_tensor(base[:, :, :], res[:, :, :], xn, ALU.add)
                dve.wait_ge(S["exp_ready"], m + 1)
                seq(V.tensor_reduce(sm, Pb, AX, ALU.add))
                seq(V.reciprocal(sm, sm))
                seq(V.tensor_tensor(Pb, Pb, bc(sm, E), ALU.mult))
                seq(V.tensor_reduce(m1, Pb, AX, ALU.max))
                seq(V.tensor_tensor(Kk, Pb, bc(m1, E), ALU.is_equal))
                seq(V.tensor_tensor(Kk, Kk, rank, ALU.mult))
                seq(V.tensor_reduce(r1, Kk, AX, ALU.max))
                seq(V.tensor_tensor(O1, Kk, bc(r1, E), ALU.is_equal))
                seq(V.scalar_tensor_tensor(L, O1, -2.0, Pb, ALU.mult, ALU.add))
                seq(V.tensor_reduce(m2, L, AX, ALU.max))
                seq(V.tensor_tensor(Kk, L, bc(m2, E), ALU.is_equal))
                seq(V.tensor_tensor(Kk, Kk, rank, ALU.mult))
                seq(V.tensor_reduce(r1, Kk, AX, ALU.max))
                seq(V.tensor_tensor(O2, Kk, bc(r1, E), ALU.is_equal))
                seq(V.tensor_tensor(O1, O1, O2, ALU.add))
                if cfg["norm"]:
                    seq(V.tensor_tensor(den, m1, m2, ALU.add))
                    if m != 1:
                        seq(V.tensor_scalar_max(den, den, 1e-12))
                    seq(V.reciprocal(den, den))
                    seq(V.tensor_tensor(Pb, Pb, bc(den, E), ALU.mult))
                seq(V.tensor_tensor(Pb, Pb, O1, ALU.mult))
                hi, mid, lo = (c3[:, :, E * k:E * k + E] for k in range(3))
                seq(V.tensor_copy(hi, Pb))
                seq(V.tensor_tensor(Pb, Pb, hi, ALU.subtract))
                seq(V.tensor_copy(mid, Pb))
                V.tensor_tensor(lo, Pb, mid, ALU.subtract).then_inc(S["comb_ready"], 1)
                if f"b2_{m}" in K:
                    seq(V.tensor_copy(b2s[:, 0, :], K[f"b2_{m}"]))
                    seq(V.tensor_tensor(b2f[:, :], K[f"b2_{m}"], b2s[:, 0, :], ALU.subtract))
                    seq(V.tensor_copy(b2s[:, 1, :], b2f[:, :]))
                    V.tensor_tensor(b2s[:, 2, :], b2f[:, :], b2s[:, 1, :], ALU.subtract).then_inc(S["b2_ready"], 1)

            def moe(m):
                cfg = MOE[m]
                routing(m)
                for c in range(chunks):
                    for un in range(units[m]):
                        n = first_unit[m] + c * units[m] + un
                        dve.wait_ge(S["act_out"], n + 1)
                        src = g[:, n % 3, :]
                        if cfg["swiglu"]:
                            seq(V.tensor_tensor(u[:, n % 2, :], src, bank[2 + n % 2][:, :], ALU.mult))
                            src = u[:, n % 2, :]
                        dve.wait_ge(S["cb_out"], n + 1)
                        if n >= 3:
                            dve.wait_ge(S["second_out"], n - 2)
                        V.tensor_tensor(gc[:, n % 3, :], src, bank[4 + n % 2][:, :], ALU.mult)\
                            .then_inc(S["gc_ready"], 1)
                    dve.wait_ge(S["second_out"], n + 1)
                    src = base if cfg["skip"] else res
                    t = tiles(c // 2, 4 * (c % 2), 4)
                    V.tensor_tensor(res[:, t, :], src[:, t, :],
                                    bank[6 + c % 2][:, 0:256].rearrange("p (t c) -> p t c", c=C), ALU.add)\
                        .then_inc(S["acc_in"], 1)
                dve.wait_ge(S["acc_in"], (m + 1) * chunks)

            dve.wait_ge(loaded["c1"], 16)
            V.tensor_scalar_add(small[:, :], K["bnv"], 1e-5).then_inc(S["setup_ready"], 1)
            dve.wait_ge(loaded["c0"], 16)
            ln(0, K["xT"].rearrange("p (t c) -> p t c", c=C), EPS_C)
            dve.wait_ge(S["mrs_ready"], 1)
            seq(V.tensor_tensor(bns[:, :], bns[:, :], K["bng"], ALU.mult))
            V.tensor_tensor(wfs[:, :], K["wf"], bns[:, :], ALU.mult)
            seq(V.tensor_tensor(bfs[:, :], K["bf"], K["bnm"], ALU.subtract))
            seq(V.tensor_tensor(bfs[:, :], bfs[:, :], bns[:, :], ALU.mult))
            V.tensor_tensor(bfs[:, :], bfs[:, :], K["bnb"], ALU.add).then_inc(S["wf_in"], 1)
            for n in range(8):
                h, i = n // 4, 2 * (n % 4)
                dve.wait_ge(S["qkv_out"], n + 1)
                V.tensor_tensor(qkv[:, tiles(h, i, 2), :], bank[n % 4][:, :].rearrange("p (t c) -> p t c", c=256),
                                row(K["bqkv"], 2), ALU.add).then_inc(S["qkv_in"], 1)
            dve.wait_ge(S["sq_ready"], 1)
            seq(V.tensor_reduce(veps[:, 0:32], big[:, 0:2048].rearrange("p (t c) -> p t c", c=64), AX, ALU.add))
            V.tensor_scalar(veps[:, 0:32], veps[:, 0:32], 1.0 / 64, 1e-8, ALU.mult, ALU.add)\
                .then_inc(S["ms_ready"], 1)
            dve.wait_ge(S["mrs_ready"], 2)
            qk = qkv[:, :, 0:P].rearrange("p t (a c) -> p t a c", a=2)
            rq = ms[:, :].rearrange("p (t a) -> p t a", a=2)
            for a, dst in ((0, q1[:, :, :]), (1, qk[:, :, 1, :])):
                V.tensor_tensor(dst, qk[:, :, a, :], bc(rq[:, :, a], 64), ALU.mult)\
                    .then_inc(S["qk_normed"], 1)
            dve.wait_ge(S["kv_out"], 1)
            seq(V.tensor_tensor(kvm[:, :, :], bank[4][:, :].rearrange("p (j c) -> p j c", c=P),
                                row(K["headmask"], 4), ALU.mult))
            V.tensor_tensor(kvs[:, :, :], kvm[:, :, :], kvm[:, :, :], ALU.mult).then_inc(S["kv_sq"], 1)
            dve.wait_ge(S["kvn_out"], 1)
            V.tensor_scalar_add(kvs[:, :, :], bank[5][:, :].rearrange("p (j c) -> p j c", c=P), 1e-8)\
                .then_inc(S["kvn_eps"], 1)
            dve.wait_ge(S["kvn_rs"], 1)
            seq(V.tensor_tensor(kvm[:, :, :], kvm[:, :, :], kvr[:, :, :], ALU.mult))
            kv4 = kvm[:, :, :].rearrange("p j (g c) -> p j g c", c=16)
            for j in range(4):
                last = V.tensor_reduce(gsum[:, j, :], kv4[:, j, :, 8:16], AX, ALU.add)
            seq(last)
            for h in range(2):
                q = slice(64 * h, 64 * h + 64)
                for j in range(4):
                    V.tensor_copy(bdc[q, j, h, :].rearrange("p (g c) -> p g c", c=8), kv4[q, j, :, 0:8])
                    last = V.tensor_copy(bdg[q, j, h, :].rearrange("p (g c) -> p g c", c=8), bc(gsum[q, j, :], 8))
            last.then_inc(S["heads_ready"], 1)
            dve.wait_ge(S["gate_out"], 1)
            for j in range(2):
                last = V.tensor_reduce(small[:, 2 * j:2 * j + 2],
                                       bank[2 + j][:, :].rearrange("p (a c) -> p a c", c=NPIX), AX, ALU.max)
            seq(last)
            V.tensor_scalar_mul(small[:, 4:8], small[:, 0:4], -1.0 / 128).then_inc(S["gmax_ready"], 1)
            dve.wait_ge(S["gexp_ready"], 4)
            seq(V.reciprocal(small[:, 12:16], small[:, 8:12]))
            for j in range(4):
                V.scalar_tensor_tensor(qkg[:, j, :], bank[j // 2][:, 256 * (j % 2):256 * (j % 2) + 256],
                                       small[:, 12 + j:13 + j], eg[:, j, :], ALU.mult, ALU.mult)\
                    .then_inc(S["gated"], 1)
            dve.wait_ge(S["wf_out"], 1)
            xR = K["xR"].rearrange("p (t c) -> p t c", c=C)
            for h in range(2):
                q = slice(64 * h, 64 * h + 64)
                for j in range(2):
                    last = V.scalar_tensor_tensor(res[q, 8 * j:8 * j + 8, :],
                                                  bank[2 * h + j][q, :].rearrange("p (t c) -> p t c", c=C), 0.0,
                                                  xR[q, 8 * j:8 * j + 8, :], ALU.max, ALU.add)
            seq(last)
            dve.wait_ge(loaded["m0"], 16)
            ln(1, res, EPS_T)
            moe(0)

            ln(2, res, EPS_C)
            dve.wait_ge(loaded["l1"], 16)
            dve.wait_ge(S["pads_set"], 1)
            seq(V.tensor_tensor(mix[:, :].rearrange("p (t c) -> p t c", c=16),
                                K["fcmask"].rearrange("p (t c) -> p t c", c=16), bc(K["fcrep"], 16), ALU.mult))
            for h in range(2):
                q = slice(64 * h, 64 * h + 64)
                V.tensor_tensor(mix[q, :], mix[q, :], K["ident"][q, 64 * h:64 * h + 64], ALU.add)
            V.tensor_scalar_mul(projs[:, :], K["projw"], K["lng"]).then_inc(S["mix_set"], 1)
            for n in range(8):
                h, i = n // 4, 2 * (n % 4)
                t = tiles(h, i, 2)
                dve.wait_ge(S["kv1_out"], n + 1)
                src = bank[n % 4][:, 0:384].rearrange("p (t c) -> p t c", c=192)
                V.tensor_tensor(q1[:, t, :], src[:, :, 0:64], row(K["qkvb"][:, 0:64], 2), ALU.add)
                V.tensor_tensor(kvx[:, 1, PADX + t.start:PADX + t.stop:2, :, :].rearrange("p t a c -> p t (a c)"),
                                src[:, :, 64:192], row(K["qkvb"][:, 64:192], 2), ALU.add)\
                    .then_inc(S["kv1_in"], 1)
            dve.wait_ge(S["kv1_in"], 8)
            dve.wait_ge(S["pb_out"], 1)
            V.tensor_tensor(pbias[:, :], bank[4][:, 0:64], K["projb"], ALU.add).then_inc(S["pbias_in"], 1)
            for r in (1, 0, 2):
                for i, d in enumerate(DILS):
                    if r != 1:
                        dve.wait_ge(S["shift_in"], 2 * (2 * i + r // 2) + 2)
                    pr = big[:, 2304 * (i % 2):2304 * (i % 2) + 768].rearrange("p (x s c) -> p x s c", s=3, c=16)
                    for s in range(3):
                        x0 = PADX + (s - 1) * d
                        last = V.tensor_tensor(pr[:, :, s, :], q1[:, :, 16 * i:16 * i + 16],
                                               kvx[:, r, x0:x0 + NT, 0, 16 * i:16 * i + 16], ALU.mult)
                    seq(last)
                    for hd in range(2):
                        V.tensor_reduce(lg[:, :, i, hd, 3 * r:3 * r + 3], pr[:, :, :, 8 * hd:8 * hd + 8], AX, ALU.add)
            seq(V.tensor_copy(ls[:, 0:1], K["projb"][:, 0:1]))
            lg3 = lg[:, :, :, :, :].rearrange("p x i h t -> p (x i h) t")
            le3 = le[:, :, :, :, :].rearrange("p x i h t -> p (x i h) t")
            seq(V.tensor_reduce(lm[:, :], lg3, AX, ALU.max))
            V.tensor_tensor(lg3, lg3, bc(lm[:, :], 9), ALU.subtract).then_inc(S["att_sub"], 1)
            dve.wait_ge(S["att_exp"], 1)
            seq(V.tensor_reduce(ls[:, :], le3, AX, ALU.add))
            seq(V.reciprocal(ls[:, :], ls[:, :]))
            for i, d in enumerate(DILS):
                pv = big[:, 2304 * (i % 2):2304 * (i % 2) + 2304].rearrange("p (x c t) -> p x c t", c=16, t=9)
                for t in range(9):
                    r, s = t // 3, t % 3
                    x0 = PADX + (s - 1) * d
                    last = V.tensor_tensor(
                        pv[:, :, :, t].rearrange("p x (h c) -> p x h c", h=2), bc(le[:, :, i, :, t], 8),
                        kvx[:, r, x0:x0 + NT, 1, 16 * i:16 * i + 16].rearrange("p x (h c) -> p x h c", h=2),
                        ALU.mult)
                seq(last)
                seq(V.tensor_reduce(stk[:, :, 16 * i:16 * i + 16], pv, AX, ALU.add))
            seq(V.tensor_tensor(stk[:, :, :].rearrange("p x (g c) -> p (x g) c", c=8),
                                stk[:, :, :].rearrange("p x (g c) -> p (x g) c", c=8), bc(ls[:, :], 8), ALU.mult))
            V.tensor_tensor(base[:, :, :], res[:, :, :], row(pbias[:, :], NT), ALU.add).then_inc(S["stk_ready"], 1)
            dve.wait_ge(S["mix_out"], 1)
            for h in range(2):
                src = bank[h][:, :].rearrange("p (x t c) -> p x t c", t=4, c=16)
                dst = fx[:, h:NT:2, :].rearrange("p x (t c) -> p x t c", c=16)
                for t in range(4):
                    last = V.tensor_scalar_add(dst[:, :, t, :], src[:, :, t, :], K["fcb"][:, t:t + 1])
            seq(last)
            f3 = fx[:, :, :].rearrange("p x (t c) -> p (x t) c", c=16)
            seq(V.tensor_reduce(small[:, :], f3, AX, ALU.add))
            seq(V.tensor_scalar_mul(small[:, :], small[:, :], 1.0 / 16))
            V.tensor_tensor(f3, f3, bc(small[:, :], 16), ALU.subtract).then_inc(S["cent_ready"], 1)
            dve.wait_ge(S["fsq_ready"], 1)
            seq(V.tensor_reduce(veps[:, :], fq[:, :, :].rearrange("p x (t c) -> p (x t) c", c=16), AX, ALU.add))
            V.tensor_scalar(veps[:, :], veps[:, :], 1.0 / 16, 1e-5, ALU.mult, ALU.add).then_inc(S["fvar_ready"], 1)
            dve.wait_ge(S["frs_ready"], 1)
            V.tensor_tensor(f3, f3, bc(rstd[:, :], 16), ALU.mult).then_inc(S["fln_ready"], 1)
            dve.wait_ge(S["proj_out"], 1)
            for h in range(2):
                last = V.tensor_tensor(res[:, h:NT:2, :], base[:, h:NT:2, :],
                                       bank[h][:, :].rearrange("p (x c) -> p x c", c=C), ALU.add)
            seq(last)
            ln(3, res, EPS_T)
            dve.wait_ge(loaded["m1"], 16)
            moe(1)

            ln(4, res, EPS_C)
            dve.wait_ge(S["normed"], 40)
            V.tensor_reduce(xsum[:, :], xn.rearrange("p x c -> p c x"), AX, ALU.add).then_inc(S["xsum_ready"], 1)
            dve.wait_ge(loaded["l2"], 16)
            seq(V.tensor_tensor(phig[:, :, :], K["phi"].rearrange("p (k n) -> p k n", n=4), row(K["rms"], 24), ALU.mult))
            V.tensor_reduce(phis[:, :], phig[:, :, :], AX, ALU.add).then_inc(S["phis_ready"], 1)
            dve.wait_ge(S["pool_out"], 1)
            V.tensor_scalar_mul(pooledT[:, :], bank[5][0:64, 0:P], 1.0 / NPIX).then_inc(S["poolT_in"], 1)
            seq(V.tensor_scalar_mul(pooled[:, :], bank[5][:, P:P + 64], 1.0 / NPIX))
            seq(V.tensor_tensor(cbs[:, :], pooled[:, :], pooled[:, :], ALU.mult))
            seq(V.tensor_reduce(sc[:, 0:1], cbs[:, :], AX, ALU.add))
            V.tensor_scalar(sc[:, 0:1], sc[:, 0:1], 1.0 / 64, 1e-20, ALU.mult, ALU.add).then_inc(S["pvar_ready"], 1)
            dve.wait_ge(S["prs_ready"], 1)
            dve.wait_ge(S["co_out"], 1)
            seq(V.scalar_tensor_tensor(co[:, :], bank[6][:, 0:24], sc[:, 1:2], K["phib"], ALU.mult, ALU.add))
            V.tensor_tensor(co[:, :], co[:, :], K["alpha"], ALU.mult).then_inc(S["cz_ready"], 1)
            dve.wait_ge(S["ce_ready"], 2)
            seq(V.tensor_scalar_add(hx[:, 0:8], hx[:, 0:8], 1.0))
            seq(V.reciprocal(hx[:, 0:8], hx[:, 0:8]))
            V.tensor_reduce(sc[:, 2:4], hx[:, 0:8].rearrange("p (a n) -> p a n", n=4), AX, ALU.add)
            M = hx[:, 8:24].rearrange("p (a b) -> p a b", b=4)
            MT = hx[:, 8:24].rearrange("p (a b) -> p b a", b=4)
            for _ in range(20):
                for v in (M, MT):
                    seq(V.tensor_reduce(rs4[:, :], v, AX, ALU.add))
                    seq(V.reciprocal(rs4[:, :], rs4[:, :]))
                    seq(V.tensor_tensor(v, v, bc(rs4[:, :], 4), ALU.mult))
            seq(V.tensor_reduce(sc[:, 4:5], hx[:, 8:24:5], AX, ALU.add))
            V.tensor_scalar_mul(sc[:, 4:5], sc[:, 4:5], 0.25)
            seq(V.tensor_scalar_mul(sc[:, 3:4], sc[:, 3:4], 0.5))
            V.tensor_tensor(sc[:, 5:6], sc[:, 2:3], sc[:, 3:4], ALU.mult)
            seq(V.tensor_scalar_mul(cbs[:, :], K["convb"], sc[:, 3:4]))
            seq(V.scalar_tensor_tensor(base[:, :, :], xn, sc[:, 4:5], res[:, :, :], ALU.mult, ALU.add))
            seq(V.tensor_tensor(base[:, :, :], base[:, :, :], row(cbs[:, :], NT), ALU.add))
            for h in range(2):
                dve.wait_ge(S["conv_out"], h + 1)
                last = V.scalar_tensor_tensor(res[:, 8 * h:8 * h + 8, :],
                                              bank[h][:, :].rearrange("p (x c) -> p x c", c=C), sc[:, 5:6],
                                              base[:, 8 * h:8 * h + 8, :], ALU.mult, ALU.add)
            seq(last)
            ln(5, res, EPS_T)
            moe(2)

            ln(6, res, EPS_C)
            dve.wait_ge(S["normed"], 56)
            dve.wait_ge(loaded["l3"], 16)
            V.tensor_tensor(cb2, K["cbT"], K["cbT"], ALU.mult).then_inc(S["cb_sq"], 1)
            seq(V.tensor_tensor(fq[:, :, :], xn, xn, ALU.mult))
            V.tensor_reduce(zz[:, :], fq[:, :, :], AX, ALU.add)
            dve.wait_ge(S["dot_out"], 1)
            V.tensor_copy(cc, bank[5][:, 0:CODES]).then_inc(S["zz_ready"], 1)
            for n in range(NT // 2):
                h, i = n // 4, 2 * (n % 4)
                dve.wait_ge(S["dot_out"], n + 2)
                for e in range(2):
                    k = 2 * n + e
                    x = 2 * (i + e) + h
                    dve.wait_ge(S["zc_ready"], k + 1)
                    V.scalar_tensor_tensor(nd[:, e, :], bank[n % 4][:, 256 * e:256 * e + 256], 2.0,
                                           zc[:, e, :], ALU.mult, ALU.subtract).then_inc(S["dot_in"], 1)
                    dve.wait_ge(S["dot_in"], k + 1)
                    seq(V.max(mx8[:, x, :], nd[:, e, :]))
                    V.max_index(ix8[:, x, :], mx8[:, x, :], nd[:, e, :]).then_inc(S["idx_ready"], 1)
            dve.wait_ge(S["gathered"], 16 * NT)
            seq(V.tensor_tensor(zq[:, :, :], zq[:, :, :], xn, ALU.subtract))
            seq(V.tensor_tensor(zq[:, :, :], zq[:, :, :], xn, ALU.add))
            seq(V.tensor_tensor(res[:, :, :], res[:, :, :], zq[:, :, :], ALU.add))
            ln(7, res, EPS_T)
            moe(3)

        @block.tensor
        def _(pe):
            T = nc.tensor
            ident = K["ident"]

            def ln_T(s, src=None):
                for i in range(HALF):
                    pe.wait_ge(S["normed"], HALF * s + i + 1)
                    mm = T.transpose(bank[6 + i // 4][:, P * (i % 4):P * (i % 4) + P], xn[:, 2 * i:2 * i + 2, :], ident)
                    if i % 4 == 3:
                        mm.then_inc(S["normed_T"], 1)

            def all_T(src, ready, value, done):
                pe.wait_ge(ready, value)
                for i in range(HALF):
                    mm = T.transpose(bank[6 + i // 4][:, P * (i % 4):P * (i % 4) + P], src[:, 2 * i:2 * i + 2, :], ident)
                    if i % 4 == 3:
                        mm.then_inc(done, 1)

            def chan(h, i):
                return xnC[64 * h:64 * h + 64, i, :]

            def moe(m):
                cfg = MOE[m]
                E, U = cfg["E"], units[m]
                w1 = K[f"w1_{m}"]
                w2 = K[f"w2_{m}"]
                sel = K["sel1" if m == 1 else "sel3" if m == 3 else "sel0"]
                N = chunks * U
                n0 = first_unit[m]

                def first(k):
                    n, c, un = n0 + k, k // U, k % U
                    h, q = c // 2, c % 2
                    if n >= 2:
                        pe.wait_ge(S["act_out"], n - 1)
                    if cfg["swiglu"] and k >= 2:
                        pe.wait_ge(S["gc_ready"], n - 1)
                    rows = slice(64 * h, 64 * h + 64)
                    x = xnC[rows, 4 * q:4 * q + 4, :]
                    mm = T.matmul(bank[n % 2][:, :], w1[rows, P * un:P * un + P], x, start=True, stop=True)
                    if cfg["swiglu"]:
                        mm = T.matmul(bank[2 + n % 2][:, :], K["wu_1"][rows, P * un:P * un + P], x,
                                      start=True, stop=True)
                    mm.then_inc(S["h_out"], 1)

                def spread(k):
                    n, c, un = n0 + k, k // U, k % U
                    if k >= 2:
                        pe.wait_ge(S["gc_ready"], n - 1)
                    T.matmul(bank[4 + n % 2][:, :], sel[:, P * un:P * un + P], cT[0:3 * E, 512 * c:512 * c + 512],
                             start=True, stop=True).then_inc(S["cb_out"], 1)

                def bias(c):
                    if m * chunks + c >= 2:
                        pe.wait_ge(S["acc_in"], m * chunks + c - 1)
                    if cfg["swiglu"]:
                        return
                    for t in range(4):
                        for j in range(3):
                            T.matmul(bank[6 + c % 2][:, 64 * t:64 * t + 64],
                                     cT[0:3 * E, 512 * c + P * t:512 * c + P * t + P], b2s[:, j, :],
                                     start=(t == 0 and j == 0), stop=False, skip_group_check=True)

                def second(k):
                    n, c, un = n0 + k, k // U, k % U
                    if un == 0:
                        bias(c)
                    pe.wait_ge(S["gc_ready"], n + 1)
                    for t in range(4):
                        mm = T.matmul(bank[6 + c % 2][:, 64 * t:64 * t + 64], gc[:, n % 3, P * t:P * t + P],
                                      w2[:, 64 * un:64 * un + 64],
                                      start=(cfg["swiglu"] and un == 0 and t == 0), stop=(un == U - 1),
                                      skip_group_check=True)
                    mm.then_inc(S["second_out"], 1)

                s = 2 * m + 1
                pe.wait_ge(S["chan_ready"], 2 * CH[s] + 2)
                for h in range(2):
                    for i in range(HALF):
                        mm = T.matmul(bank[4 + h][:, E * i:E * i + E], chan(h, i),
                                      K[f"rw{m}"][64 * h:64 * h + 64, :], start=True, stop=True)
                    mm.then_inc(S["logits_out"], 1)
                first(0)
                first(1)
                pe.wait_ge(S["comb_ready"], m + 1)
                for j in range(2):
                    for i in range(HALF):
                        mm = T.transpose(bank[4 + j][0:3 * E, :].bitcast(bf16)[:, P * i:P * i + P],
                                         c3[:, 2 * i + j, 0:3 * E], K["identb"])
                    mm.then_inc(S["comb_T"], 1)
                pe.wait_ge(S["comb_chan"], 2 * m + 2)
                if not cfg["swiglu"]:
                    pe.wait_ge(S["b2_ready"], [1, 0, 2, 3][m])
                spread(0)
                spread(1)
                for k in range(N):
                    if k + 2 < N:
                        if not cfg["swiglu"]:
                            first(k + 2)
                    second(k)
                    if k + 2 < N:
                        if cfg["swiglu"]:
                            first(k + 2)
                        spread(k + 2)

            pe.wait_ge(loaded["c0"], 16)
            ln_T(0)
            pe.wait_ge(S["chan_ready"], 2)
            for n in range(8):
                h, i = n // 4, 2 * (n % 4)
                if n >= 4:
                    pe.wait_ge(S["qkv_in"], n - 3)
                for e in range(2):
                    mm = T.matmul(bank[n % 4][:, 256 * e:256 * e + 256], chan(h, i + e),
                                  K["wqkv"][64 * h:64 * h + 64, :], start=True, stop=True)
                mm.then_inc(S["qkv_out"], 1)
            pe.wait_ge(S["qk_normed"], 1)
            for i in range(HALF):
                mm = T.transpose(bank[6 + i // 4][:, P * (i % 4):P * (i % 4) + P],
                                 q1[:, 2 * i:2 * i + 2, :], ident)
                if i % 4 == 3:
                    mm.then_inc(S["q_T"], 1)
            pe.wait_ge(S["qk_normed"], 2)
            for h in range(2):
                for j in range(4):
                    for e in range(2):
                        tt = 2 * (2 * j + e) + h
                        mm = T.matmul(bank[4][64 * h:64 * h + 64, P * j:P * j + P], qkv[:, tt, 64:128],
                                      qkv[:, tt, 128:256], start=(j == 0 and e == 0), stop=(j == 3 and e == 1),
                                      skip_group_check=True)
            mm.then_inc(S["kv_out"], 1)
            pe.wait_ge(S["kv_sq"], 1)
            T.matmul(bank[5][:, :], K["headmean"], kvs[:, :, :], start=True, stop=True).then_inc(S["kvn_out"], 1)
            pe.wait_ge(S["heads_ready"], 1)
            pe.wait_ge(S["q_chan"], 2)
            for bd, b0 in ((bdg, 2), (bdc, 0)):
                for j in range(4):
                    mm = T.matmul(bank[b0 + j // 2][:, 256 * (j % 2):256 * (j % 2) + 256], bd[:, j, :, :],
                                  qC[:, 2 * j:2 * j + 2, :], start=True, stop=True)
            mm.then_inc(S["gate_out"], 1)
            pe.wait_ge(S["gated"], 4)
            pe.wait_ge(S["wf_in"], 1)
            for h in range(2):
                q = slice(64 * h, 64 * h + 64)
                for j in range(2):
                    T.matmul(bank[2 * h + j][q, :], ones[64 * h:64 * h + 1, :],
                             bfs[64 * h:64 * h + 1, :].unsqueeze(1).broadcast_to([1, 8, 64]),
                             start=True, stop=False, skip_group_check=True)
                    for x in range(8):
                        mm = T.matmul(bank[2 * h + j][q, 64 * x:64 * x + 64],
                                      qkg[q, :, :].rearrange("p j (y x) -> p (j y) x", x=W)[:, :, 8 * j + x],
                                      wfs[q, :], start=False, stop=True, skip_group_check=True)
            mm.then_inc(S["wf_out"], 1)
            ln_T(1)
            pe.wait_ge(loaded["m0"], 16)
            pe.wait_ge(loaded["bf"], 16)
            moe(0)

            ln_T(2)
            pe.wait_ge(loaded["l1"], 16)
            pe.wait_ge(S["mix_set"], 1)
            T.matmul(bank[4][:, 0:64], K["lnb"][0:64, :], K["projw"][0:64, :], start=True, stop=True)\
                .then_inc(S["pb_out"], 1)
            pe.wait_ge(S["chan_ready"], 6)
            for n in range(8):
                h, i = n // 4, 2 * (n % 4)
                if n >= 4:
                    pe.wait_ge(S["kv1_in"], n - 3)
                for e in range(2):
                    mm = T.matmul(bank[n % 4][:, 192 * e:192 * e + 192], chan(h, i + e),
                                  K["qkvw"][64 * h:64 * h + 64, :], start=True, stop=True)
                mm.then_inc(S["kv1_out"], 1)
            pe.wait_ge(S["kv1_in"], 8)
            pe.wait_ge(S["pbias_in"], 1)
            for n in range(8):
                i = n // 2
                mm = T.matmul(bank[n][:, :], K["shift"][:, P * n:P * n + P],
                              kvx[:, 1, PADX:PADX + NT, :, 16 * i:16 * i + 16], start=True, stop=True)
                mm.then_inc(S["shift_out"], 1)
            all_T(stk, S["stk_ready"], 1, S["stk_T"])
            pe.wait_ge(S["stk_chan"], 2)
            for h in range(2):
                for i in range(HALF):
                    mm = T.matmul(bank[h][:, 64 * i:64 * i + 64], chan(h, i), mix[64 * h:64 * h + 64, :],
                                  start=True, stop=True)
            mm.then_inc(S["mix_out"], 1)
            all_T(fx, S["fln_ready"], 1, S["fln_T"])
            pe.wait_ge(S["fln_chan"], 2)
            for h in range(2):
                for i in range(HALF):
                    mm = T.matmul(bank[h][:, 64 * i:64 * i + 64], chan(h, i), projs[64 * h:64 * h + 64, :],
                                  start=True, stop=True)
            mm.then_inc(S["proj_out"], 1)
            ln_T(3)
            pe.wait_ge(loaded["m1"], 16)
            moe(1)

            pe.wait_ge(S["normed"], 40)
            for j in range(NT + 1):
                mm = T.transpose(bank[j // 4][:, P * (j % 4):P * (j % 4) + P], xnp[:, j:j + 2, :], ident)
                if j % 4 == 3 or j == NT:
                    mm.then_inc(S["stack_T"], 1)
            pe.wait_ge(loaded["l2"], 16)
            pe.wait_ge(S["xsum_ready"], 1)
            T.matmul(bank[5][0:64, 0:P], xsum[:, :], K["samebatch"], start=True, stop=True)
            T.matmul(bank[5][:, P:P + 64], K["samebatch"], xsum[:, :], start=True, stop=True)\
                .then_inc(S["pool_out"], 1)
            pe.wait_ge(S["poolT_in"], 1)
            pe.wait_ge(S["phis_ready"], 1)
            T.matmul(bank[6][:, 0:24], pooledT[:, :], phis[:, :], start=True, stop=True).then_inc(S["co_out"], 1)
            pe.wait_ge(S["stack_in"], 15)
            def column(r, x):
                return stack[:, r, x, :, :].rearrange("p b y -> p (b y)")

            for h in range(2):
                for x in range(8 * h, 8 * h + 8):
                    o = bank[h][:, 64 * (x % 8):64 * (x % 8) + 64]
                    for dy in range(3):
                        T.matmul(o, column(dy, x), K["convp"][:, 64 * dy:64 * dy + 64],
                                 start=(x % 8 == 0 and dy == 0), stop=False, skip_group_check=True)
                for x in range(8 * h, 8 * h + 8):
                    o = bank[h][:, 64 * (x % 8):64 * (x % 8) + 64]
                    for dy in range(3):
                        mm = T.matmul(o, column(dy, x + 1)[64:128, :], K["convs"][64:128, 64 * dy:64 * dy + 64],
                                      start=False, stop=(dy == 2), skip_group_check=True)
                mm.then_inc(S["conv_out"], 1)
            ln_T(5)
            pe.wait_ge(loaded["m2"], 16)
            moe(2)

            ln_T(6)
            pe.wait_ge(loaded["l3"], 16)
            pe.wait_ge(S["cb_sq"], 1)
            T.matmul(bank[5][:, 0:CODES], K["halfones"], cb2, start=True, stop=True).then_inc(S["dot_out"], 1)
            pe.wait_ge(S["chan_ready"], 12)
            for n in range(8):
                h, i = n // 4, 2 * (n % 4)
                if n >= 4:
                    pe.wait_ge(S["dot_in"], 2 * (n - 3))
                for e in range(2):
                    mm = T.matmul(bank[n % 4][:, 256 * e:256 * e + 256], chan(h, i + e),
                                  K["cbT"][64 * h:64 * h + 64, :], start=True, stop=True)
                mm.then_inc(S["dot_out"], 1)
            ln_T(7)
            pe.wait_ge(loaded["m3"], 16)
            moe(3)


def kernel(**inputs):
    import numpy as np
    import ml_dtypes
    import concourse.bacc as bacc
    from concourse.bass_utils import run_bass_kernel_spmd

    v = {k: np.asarray(a) for k, a in inputs.items()}
    two = lambda a: np.concatenate([a, a], axis=0)
    every = lambda a: np.broadcast_to(a, (P,) + a.shape)
    x = v["x"]
    parts = {"ident": np.eye(P, dtype=np.float32)}
    parts["xT"] = x.reshape(2, 4, C, 2, P).transpose(4, 1, 3, 0, 2).reshape(P, NT * C)
    parts["xR"] = x.transpose(0, 2, 3, 1).reshape(P, NT * C)
    parts["wqkv"] = two(np.concatenate([v["L0_conv_Wq"].T, v["L0_conv_Wk"].T, v["L0_conv_Wv"].T], axis=1))
    parts["bqkv"] = every(np.concatenate([v["L0_conv_bq"], v["L0_conv_bk"], v["L0_conv_bv"]]))
    head = np.arange(64) // 8
    parts["headmask"] = two((head[:, None] == np.arange(128)[None, :] // 16).astype(np.float32))
    parts["headmean"] = (np.arange(P)[:, None] // 8 == np.arange(P)[None, :] // 8).astype(np.float32) / np.float32(8)
    parts["wf"] = two(v["L0_conv_Wf"].T)
    for name, src in (("bf", "bf"), ("bng", "bn_gamma"), ("bnb", "bn_beta"), ("bnm", "bn_mean"), ("bnv", "bn_var")):
        parts[name] = every(v["L0_conv_" + src])
    parts["rank8"] = every(np.arange(8, 0, -1, dtype=np.float32))
    parts["rank16"] = every(np.arange(16, 0, -1, dtype=np.float32))
    for m, s in ((0, "L0_ffn_"), (2, "L2_ffn_")):
        parts[f"rw{m}"] = two(v[s + "router_w"].T)
        parts[f"w1_{m}"] = two(v[s + "w1"].transpose(1, 0, 2).reshape(64, 512))
        parts[f"b1_{m}"] = v[s + "b1"].reshape(4, P).T
        parts[f"w2_{m}"] = v[s + "w2"].reshape(4, P, 64).transpose(1, 0, 2).reshape(P, 256)
        parts[f"b2_{m}"] = np.concatenate([v[s + "b2"]] * 3, axis=0)
    parts["rw1"], parts["gb1"] = two(v["L1_ffn_gate_w"]), every(v["L1_ffn_gate_b"])
    parts["w1_1"] = two(v["L1_ffn_w1"].transpose(1, 0, 2).reshape(64, 2048))
    parts["wu_1"] = two(v["L1_ffn_w2"].transpose(1, 0, 2).reshape(64, 2048))
    parts["w2_1"] = v["L1_ffn_w3"].transpose(1, 0, 2).reshape(P, 1024)
    parts["rw3"], parts["gb3"] = two(v["L3_ffn_gate_w"]), every(v["L3_ffn_gate_b"])
    parts["w1_3"] = two(v["L3_ffn_W1"].transpose(1, 0, 2).reshape(64, 1024))
    parts["b1_3"] = v["L3_ffn_b1"].T
    parts["w2_3"] = v["L3_ffn_W2"].transpose(1, 0, 2).reshape(P, 512)
    parts["b2_3"] = np.concatenate([v["L3_ffn_b2"]] * 3, axis=0)
    parts["qkvw"], parts["qkvb"] = two(v["L1_conv_qkv_w"].T), every(v["L1_conv_qkv_b"])
    b, y = np.arange(P) // H, np.arange(P) % H
    shift = [(b[:, None] == b[None, :]) & (y[:, None] == y[None, :] + r * d) for d in DILS for r in (-1, 1)]
    parts["shift"] = np.stack(shift, axis=1).astype(np.float32).reshape(P, 8 * P)
    parts["fcrep"] = two(np.repeat(v["L1_conv_fc_w"].T, 16, axis=0))
    parts["fcb"] = every(v["L1_conv_fc_b"])
    ch = np.arange(64) % 16
    parts["fcmask"] = two((ch[:, None] == ch[None, :]).astype(np.float32))
    parts["lng"] = np.tile(v["L1_conv_ln_g"], 8)[:, None]
    parts["lnb"] = np.broadcast_to(np.tile(v["L1_conv_ln_b"], 8)[:, None], (P, P))
    parts["projw"], parts["projb"] = two(v["L1_conv_proj_w"].T), every(v["L1_conv_proj_b"])
    parts["samebatch"] = (b[:, None] == b[None, :]).astype(np.float32)
    parts["phi"] = v["L2_conv_phi_w"].reshape(24, 4, 64).transpose(2, 0, 1).reshape(64, 96)
    parts["rms"] = v["L2_conv_rms_w"].reshape(4, 64).T
    parts["phib"] = every(v["L2_conv_phi_b"])
    parts["alpha"] = every(np.concatenate([np.repeat(v["L2_conv_alpha_" + n], k)
                                           for n, k in (("pre", 4), ("post", 4), ("res", 16))]))
    taps = v["L2_conv_conv_w"].transpose(3, 1, 2, 0)
    parts["convp"] = taps[0:2].reshape(P, 192)
    parts["convs"] = two(taps[2].reshape(64, 192))
    parts["convb"] = every(v["L2_conv_conv_b"])
    parts["cbT"] = two(v["L3_conv_codebook"].T)
    parts["halfones"] = np.concatenate([np.ones((64, P), np.float32), np.zeros((64, P), np.float32)])
    parts["identb"] = np.eye(P)
    for name, E, per in (("sel0", 8, 2), ("sel1", 16, 1), ("sel3", 8, 1)):
        expert = np.arange(E // per * P) // (P // per)
        parts[name] = np.tile(np.arange(E), 3)[:, None] == expert[None, :]

    def pack(spec, dtype):
        where, width = pack_columns(spec)
        a = np.zeros((P, width), dtype)
        for name, (at, rows, cols) in where.items():
            a[0:rows, at:at + cols] = parts[name].astype(dtype) if dtype != np.float32 else parts[name]
        return a

    nc = bacc.Bacc("TRN2", target_bir_lowering=False, num_devices=1)
    arrays, dram = {}, {}
    for pk, spec in PACKS.items():
        arrays["in_" + pk] = pack(spec, np.float32)
    arrays["in_bf"] = pack(BF_PACK, ml_dtypes.bfloat16)
    arrays["in_codebook"] = np.ascontiguousarray(v["L3_conv_codebook"])
    for name, a in arrays.items():
        dram[name[3:]] = nc.dram_tensor(name, a.shape, mybir.dt.from_np(a.dtype), kind="ExternalInput").ap()
    codebook = dram.pop("codebook")
    out = nc.dram_tensor("out_tokens", (P, NT, C), mybir.dt.float32, kind="ExternalOutput").ap()
    metaformer(nc, dram, codebook, out)
    r = run_bass_kernel_spmd(nc, [arrays], core_ids=[0])
    tokens = r.results[0]["out_tokens"]
    return tokens.reshape(B, H, W, C).transpose(0, 3, 1, 2)
```

```python
import concourse.bass as bass
from concourse import mybir
from contextlib import ExitStack

B, C, H, W = 8, 64, 16, 16
P = 128
NT = B * H * W // P
HALF = NT // 2
NPIX = H * W
DILS = (1, 2, 4, 8)
PADX = 8
CODES = 256
EPS_C, EPS_T = 1e-6, 1e-5

MOE = [dict(E=8, D2=64, act="gelu", skip=True, norm=True, swiglu=False),
       dict(E=16, D2=128, act="silu", skip=False, norm=True, swiglu=True),
       dict(E=8, D2=64, act="gelu", skip=True, norm=True, swiglu=False),
       dict(E=8, D2=128, act="gelu", skip=False, norm=False, swiglu=False)]

PACKS = {
    "c0": [("wqkv", P, 256), ("xT", P, NT * C), ("bqkv", P, 256), ("ident", P, P), ("headmask", P, 128),
           ("headmean", P, P), ("blockmask", P, 16)],
    "c1": [("xR", P, NT * C), ("wf", P, 64), ("bf", P, 64), ("bng", P, 64), ("bnb", P, 64),
           ("bnm", P, 64), ("bnv", P, 64)],
    "r": [("rw0", P, 8), ("rw1", P, 16), ("rw2", P, 8), ("rw3", P, 8), ("gb1", P, 16), ("gb3", P, 8),
          ("b1_0", P, 4), ("b1_2", P, 4), ("b1_3", P, 8), ("b2_0", 16, 64), ("b2_2", 16, 64), ("b2_3", 16, 64),
          ("rank8", P, 8), ("rank16", P, 16)],
    "l1": [("qkvw", P, 192), ("qkvb", P, 192), ("shift", P, 8 * P), ("fcrep", P, 4), ("fcb", P, 64), ("fcmask", P, 64),
           ("lng", P, 1), ("lnb", P, P), ("projw", P, 64), ("projb", P, 64)],
    "l2": [("samebatch", P, P), ("phi", 64, 96), ("rms", 64, 4), ("phib", P, 24), ("alpha", P, 24),
           ("convw", P, 576), ("convb", P, 64), ("cbT", P, CODES), ("halfones", P, P)],
    "m0": [("w1_0", P, 512), ("w2_0", P, 256)],
    "m1": [("w1_1", P, 2048), ("wu_1", P, 2048), ("w2_1", P, 1024)],
    "m2": [("w1_2", P, 512), ("w2_2", P, 256)],
    "m3": [("w1_3", P, 1024), ("w2_3", P, 512)],
}
STAGED = ("m0", "m1", "m2", "m3")
WSCALE = 64.0
CSCALE = 16.0
SPLIT = [("c0", "wqkv"), ("r", "rw0"), ("m0", "w1_0"), ("m0", "w2_0"), ("l1", "qkvw"), ("r", "rw1"), ("m1", "w1_1"),
         ("m1", "wu_1"), ("m1", "w2_1"), ("l2", "convw"), ("r", "rw2"), ("m2", "w1_2"), ("m2", "w2_2"), ("l2", "cbT"),
         ("r", "rw3"), ("m3", "w1_3"), ("m3", "w2_3")]
HALF_PACK = [("identh", P, P), ("rowshift", P, 3 * P), ("sel0", 16, 4 * P), ("sel1", 32, 16 * P), ("sel3", 16, 8 * P)]


def pack_columns(spec):
    at, where = 0, {}
    for name, rows, cols in spec:
        where[name] = (at, rows, cols)
        at += cols
    return where, at


def metaformer(nc: bass.Bass, dram, codebook, out):
    fp32, fp16, i32, u32 = mybir.dt.float32, mybir.dt.float16, mybir.dt.int32, mybir.dt.uint32
    ALU = mybir.AluOpType
    ACT = mybir.ActivationFunctionType
    AX = mybir.AxisListType.X

    ctx = ExitStack()
    with ctx:
        def sb(name, shape, dt=fp32):
            return ctx.enter_context(nc.sbuf_tensor(name, shape, dt))

        def sem(name):
            return ctx.enter_context(nc.semaphore(name))

        packs, K = {}, {}
        kvx_mem = sb("kvx_mem", [P, 3 * (NT + 2 * PADX) * 2 * C])
        staged_at = NT * 256
        for pk, spec in PACKS.items():
            where, width = pack_columns(spec)
            if pk in STAGED:
                packs[pk] = kvx_mem[:, staged_at:staged_at + width]
                staged_at += width
            else:
                packs[pk] = sb("pack_" + pk, [P, width])[:, :]
            for name, (at, rows, cols) in where.items():
                K[name] = packs[pk][0:rows, at:at + cols]
        where, width = pack_columns(HALF_PACK)
        packs["half"] = sb("pack_half", [P, width], fp16)[:, :]
        for name, (at, rows, cols) in where.items():
            K[name] = packs["half"][0:rows, at:at + cols]
        WH, WL = {}, {}
        for _, name in SPLIT + [("", "mix"), ("", "projs")]:
            cols = K[name].shape[1] if name in K else 64
            WH[name] = sb(name + "_high", [P, cols], fp16)[:, :]
            WL[name] = sb(name + "_low", [P, cols], fp16)[:, :]

        res = sb("res", [P, NT, C])
        base = sb("base", [P, NT, C])
        xn = sb("xn", [P, NT, C])
        xt = sb("xt", [P, NT, 2, C], fp16)
        xs = sb("xs", [P, NT * P], fp16)
        bst = sb("bst", [P, NT, 6])
        mv = sb("mv", [P, NT, 2])
        veps = sb("veps", [P, 64])
        rstd = sb("rstd", [P, 64])
        seed = sb("seed", [P, 64], i32)

        qkv = kvx_mem[:, 0:NT * 256].rearrange("p (t c) -> p t c", c=256)
        big = sb("big", [P, 2 * 2304])
        qC = sb("qC", [P, HALF, P])
        ms = sb("ms", [P, 32])
        kvm = sb("kvm", [P, 4, P])
        kvc = sb("kvc", [P, 4, 16])
        kvs = sb("kvs", [P, 64])
        gsum = sb("gsum", [P, 4])
        lg_mem = sb("lg_mem", [P, NT * 72])
        bdc = lg_mem[:, 0:512].rearrange("p (j b c) -> p j b c", j=4, b=16)
        bdg = lg_mem[:, 512:1024].rearrange("p (j b c) -> p j b c", j=4, b=16)
        eg = big[:, 2048:3072].rearrange("p (j n) -> p j n", j=4)
        qkg = big[:, 3072:4096].rearrange("p (j n) -> p j n", j=4)
        bns = sb("bns", [P, 64])
        wfs = sb("wfs", [P, 64])
        bfs = sb("bfs", [P, 64])
        ones = sb("ones", [P, 64])
        small = sb("small", [P, 64])

        q1 = sb("q1", [P, NT, C])
        kvx = kvx_mem[:, :].rearrange("p (r x a c) -> p r x a c", r=3, a=2, c=C)
        lg = lg_mem[:, :].rearrange("p (x i h t) -> p x i h t", i=4, h=2, t=9)
        le = lg
        lm = sb("lm", [P, P])
        ls = sb("ls", [P, P])
        stk = q1
        mix = sb("mix", [64 * 2, 64])
        projs = sb("projs", [P, 64])
        pbias = sb("pbias", [P, 64])
        fx = sb("fx", [P, NT, C])
        fq = qC[:, :, :].rearrange("p i (t c) -> p (i t) c", c=C)

        stack = kvx_mem[:, 0:3 * NT * P // 2].bitcast(fp16).rearrange("p (r x t) -> p r x t", r=3, t=P)
        zrow = sb("zrow", [1, 512], fp16)
        xsum = sb("xsum", [P, 64])
        pooled = sb("pooled", [P, 64])
        pooledT = sb("pooledT", [64, P])
        phig = sb("phig", [64, 24, 4])
        phis = sb("phis", [64, 24])
        co = sb("co", [P, 24])
        hx = sb("hx", [P, 24])
        rs4 = sb("rs4", [P, 4])
        sc = sb("sc", [P, 8])
        cbs = sb("cbs", [P, 64])

        cc, cb2 = kvx_mem[:, 0:CODES], kvx_mem[:, CODES:2 * CODES]
        zc = kvx_mem[:, 512:1024].rearrange("p (a c) -> p a c", a=2)
        nd = kvx_mem[:, 1024:1536].rearrange("p (a c) -> p a c", a=2)
        mx8 = sb("mx8", [P, NT, 8])
        ix8 = sb("ix8", [P, NT, 8], u32)
        zz = sb("zz", [P, NT])
        zq = kvx_mem[:, 2048:2048 + NT * C].rearrange("p (t c) -> p t c", c=C)

        rl = sb("rl", [P, NT, 16])
        rp = sb("rp", [P, NT, 16])
        rk = sb("rk", [P, NT, 16])
        o1 = sb("o1", [P, NT, 16])
        o2 = sb("o2", [P, NT, 16])
        rm = [sb(f"rm{i}", [P, NT]) for i in range(6)]
        c2 = sb("c2", [P, NT, 32], fp16)
        cT = sb("cT", [32, NT * P], fp16)
        b2s = sb("b2s", [16, 2, 64], fp16)
        b2f = sb("b2f", [16, 64])
        DEPTH, LAG = 4, 3
        g = sb("g", [P, DEPTH, 512])
        u = big[:, 0:DEPTH * 512].rearrange("p (a c) -> p a c", a=DEPTH)
        gw = big[:, DEPTH * 512:2 * DEPTH * 512].rearrange("p (a c) -> p a c", a=DEPTH)
        gh, gl = (a[:, :, :].rearrange("p t c -> p (t c)").bitcast(fp16).rearrange("p (a c) -> p a c", a=DEPTH)
                  for a in (q1, fx))

        bank = [ctx.enter_context(nc.psum_tensor(f"bank{i}", [P, 512], fp32)) for i in range(8)]

        loaded = {pk: sem("loaded_" + pk) for pk in packs}
        S = {n: sem(n) for n in (
            "vec_step src_ready high_ready low_ready halves_T chan_act chan_vec wsplit_high wsplit "
            "consts_set qkv_out qkv_in sq_ready qk_normed q_T q_chan kv_out kv_sq "
            "kvn_out heads_ready gate_out gmax_ready gexp_ready gated wf_in wf_out "
            "logits_out sub_ready exp_ready comb_ready comb_T comb_act comb_vec b2_ready "
            "h_out act_out branch_in cb_out weighted unit_high unit_low_vec unit_low_pool second_out acc_in "
            "kv1_out kv1_in shift_out shift_in att_sub att_exp stk_ready mix_set mix_out pb_out pbias_in "
            "cent_ready fsq_ready proj_out "
            "pads_set stack_T stack_act stack_vec xsum_ready pool_out phis_ready poolT_in co_out cz_ready "
            "ce_ready conv_out cb_sq zz_ready zc_ready dot_out dot_in idx_ready gathered vqdone stored").split()}

        block = ctx.enter_context(nc.Block())

        chunks = 4
        SPL = ["ln0", "ln1", "ln2", "stk", "fln", "ln3", "ln4", "ln5", "ln6", "ln7"]
        TRN = [x for x in SPL if x != "ln4"]
        units = [m["E"] * m["D2"] // P for m in MOE]
        first_unit = [chunks * sum(units[:m]) for m in range(4)]

        def tiles(h, i, k):
            return slice(2 * i + h, 2 * (i + k) + h - 1, 2)

        def low_on_pool(m, k):
            return MOE[m]["swiglu"] or k % 2 == 1

        def lows(m, k, pool):
            before = sum(low_on_pool(a, b) == pool for a in range(m) for b in range(chunks * units[a]))
            return before + sum(low_on_pool(m, b) == pool for b in range(k + 1))

        @block.sync
        def _(sp):
            for pk in ("c0", "r", "m1", "l2", "m3"):
                sp.dma_start(packs[pk], dram[pk]).then_inc(loaded[pk], 16)
            for c in range(chunks):
                sp.wait_ge(S["acc_in"], 3 * chunks + c + 1)
                t = slice(4 * c, 4 * c + 4)
                sp.dma_start(out[:, t, :], res[:, t, :]).then_inc(S["stored"], 16)
            sp.wait_ge(S["stored"], 16 * chunks)

        @block.gpsimd
        def _(pool):
            nc.gpsimd.memset(ones[:, :], 1.0).then_inc(S["consts_set"], 1)
            nc.gpsimd.memset(zrow[:, :], 0.0).then_inc(S["consts_set"], 1)
            for n, (pk, name) in enumerate(SPLIT):
                pool.wait_ge(loaded[pk], 16)
                nc.gpsimd.tensor_scalar(K[name], K[name], WSCALE, 1.0, ALU.mult, ALU.mult)\
                    .then_inc(S["wsplit_high"], 1)
                pool.wait_ge(S["wsplit_high"], 2 * n + 1)
                nc.gpsimd.tensor_copy(WH[name], K[name]).then_inc(S["wsplit_high"], 1)
                pool.wait_ge(S["wsplit_high"], 2 * n + 2)
                nc.gpsimd.tensor_tensor(WL[name], K[name], WH[name], ALU.subtract).then_inc(S["wsplit"], 1)
            pool.wait_ge(S["wsplit"], len(SPLIT))
            pool.wait_ge(S["kv_out"], 1)
            pool.wait_ge(S["halves_T"], 4)
            nc.gpsimd.memset(kvx_mem[:, :], 0.0).then_inc(S["pads_set"], 1)

            def unit_lows(m):
                for k in range(chunks * units[m]):
                    if low_on_pool(m, k):
                        n = first_unit[m] + k
                        pool.wait_ge(S["unit_high"], n + 1)
                        nc.gpsimd.tensor_tensor(gl[:, n % DEPTH, :], gw[:, n % DEPTH, :], gh[:, n % DEPTH, :],
                                                ALU.subtract).then_inc(S["unit_low_pool"], 1)

            for m in range(3):
                unit_lows(m)
            for x in range(NT):
                pool.wait_ge(S["idx_ready"], x + 1)
                nc.gpsimd.indirect_dma_start(
                    out=zq[:, x, :], out_offset=None, in_=codebook,
                    in_offset=bass.IndirectOffsetOnAxis(ap=ix8[:, x, 0:1], axis=0)).then_inc(S["gathered"], 16)
            unit_lows(3)

        @block.scalar
        def _(act):
            for pk in ("c1", "half", "m0", "l1", "m2"):
                act.dma_start(packs[pk], dram[pk]).then_inc(loaded[pk], 16)

            def split(name):
                src = {"stk": stk, "fln": fx}.get(name, xn)
                for j in range(2):
                    act.wait_ge(S["src_ready"], 2 * SPL.index(name) + j + 1)
                    nc.scalar.activation(xt[:, 8 * j:8 * j + 8, 0, :], src[:, 8 * j:8 * j + 8, :], ACT.Copy)\
                        .then_inc(S["high_ready"], 1)
                if name in TRN:
                    act.wait_ge(S["halves_T"], 2 * TRN.index(name) + 1)
                    nc.scalar.activation(xs[:, 0:1024], bank[6][:, :].bitcast(fp16), ACT.Copy)\
                        .then_inc(S["chan_act"], 1)

            def moe(m):
                cfg = MOE[m]
                E = cfg["E"]
                act.wait_ge(S["sub_ready"], m + 1)
                nc.scalar.activation(rp[:, :, 0:E], rl[:, :, 0:E], ACT.Exp).then_inc(S["exp_ready"], 1)
                act.wait_ge(S["comb_T"], 2 * m + 1)
                nc.scalar.activation(cT[0:2 * E, 0:1024], bank[4][0:2 * E, :].bitcast(fp16), ACT.Copy)\
                    .then_inc(S["comb_act"], 1)
                N = chunks * units[m]
                for k in range(N + 1):
                    n = first_unit[m] + k
                    if k < N:
                        act.wait_ge(S["h_out"], n + 1)
                        if n >= DEPTH:
                            act.wait_ge(S["second_out"], n - DEPTH + 1)
                        if cfg["swiglu"]:
                            nc.scalar.activation(g[:, n % DEPTH, :], bank[k % 2][:, :], ACT.Silu, scale=1 / WSCALE)\
                                .then_inc(S["act_out"], 1)
                        else:
                            nc.scalar.activation(g[:, n % DEPTH, :], bank[k % 4][:, :], ACT.Gelu,
                                                 bias=K[f"b1_{m}"][:, k % units[m]:k % units[m] + 1],
                                                 scale=1 / WSCALE).then_inc(S["act_out"], 1)
                    if k >= 1:
                        act.wait_ge(S["weighted"], n)
                        nc.scalar.activation(gh[:, (n - 1) % DEPTH, :], gw[:, (n - 1) % DEPTH, :], ACT.Copy)\
                            .then_inc(S["unit_high"], 1)

            split("ln0")
            act.wait_ge(S["qkv_in"], 8)
            nc.scalar.activation(big[:, 0:2048].rearrange("p (t c) -> p t c", c=P), qkv[:, :, 0:P], ACT.Square)\
                .then_inc(S["sq_ready"], 1)
            for j in range(2):
                act.wait_ge(S["q_T"], j + 1)
                nc.scalar.activation(qC[:, 4 * j:4 * j + 4, :], bank[6 + j][:, :], ACT.Copy)\
                    .then_inc(S["q_chan"], 1)
            act.wait_ge(S["gmax_ready"], 1)
            for j in range(4):
                nc.scalar.activation(eg[:, j, :], bank[2 + j // 2][:, 256 * (j % 2):256 * (j % 2) + 256], ACT.Exp,
                                     bias=small[:, 4 + j:5 + j], scale=1.0 / 128,
                                     accum_out=small[:, 8 + j:9 + j]).then_inc(S["gexp_ready"], 1)
            split("ln1")
            act.wait_ge(loaded["r"], 16)
            moe(0)
            split("ln2")
            act.wait_ge(S["pads_set"], 1)
            for n in range(8):
                i, r = n // 2, 2 * (n % 2)
                act.wait_ge(S["shift_out"], n + 1)
                for kv in range(2):
                    nc.scalar.activation(kvx[:, r, PADX:PADX + NT, kv, 16 * i:16 * i + 16],
                                         bank[n][:, :].rearrange("p (x a c) -> p x a c", a=2, c=16)[:, :, kv, :],
                                         ACT.Copy).then_inc(S["shift_in"], 1)
            act.wait_ge(S["att_sub"], 1)
            nc.scalar.activation(le[:, :, :, :, :], lg[:, :, :, :, :], ACT.Exp, scale=8 ** -0.5)\
                .then_inc(S["att_exp"], 1)
            split("stk")
            act.wait_ge(S["cent_ready"], 1)
            nc.scalar.activation(fq[:, :, :], fx[:, :, :], ACT.Square).then_inc(S["fsq_ready"], 1)
            split("fln")
            split("ln3")
            moe(1)
            split("ln4")
            for x in range(0, NT, 2):
                act.wait_ge(S["stack_T"], x + 1)
                nc.scalar.activation(stack[:, :, x, :], bank[2 + x % 4][:, 0:3 * P].rearrange("p (r t) -> p r t", r=3),
                                     ACT.Copy).then_inc(S["stack_act"], 1)
            act.wait_ge(S["cz_ready"], 1)
            nc.scalar.activation(hx[:, 0:8], co[:, 0:8], ACT.Exp, scale=-1.0).then_inc(S["ce_ready"], 1)
            nc.scalar.activation(hx[:, 8:24], co[:, 8:24], ACT.Exp).then_inc(S["ce_ready"], 1)
            split("ln5")
            moe(2)
            split("ln6")
            act.wait_ge(S["zz_ready"], 1)
            for x in range(NT):
                if x >= 2:
                    act.wait_ge(S["dot_in"], x - 1)
                nc.scalar.activation(zc[:, x % 2, :], cc, ACT.Identity, bias=zz[:, x:x + 1])\
                    .then_inc(S["zc_ready"], 1)
            split("ln7")
            moe(3)

        @block.vector
        def _(dve):
            V = nc.vector
            steps = [0]

            def seq(ins):
                steps[0] += 1
                ins.then_inc(S["vec_step"], 1)
                dve.wait_ge(S["vec_step"], steps[0])

            def bc(ap, n):
                return ap.unsqueeze(len(ap.shape)).broadcast_to(list(ap.shape) + [n])

            def row(ap, n):
                return ap.unsqueeze(1).broadcast_to([ap.shape[0], n] + list(ap.shape[1:]))

            def rsqrt(dst, src, n):
                bits = seed[:, 0:n]
                seq(V.tensor_scalar(bits, src.bitcast(i32), 1, None, ALU.arith_shift_right))
                seq(V.tensor_scalar(dst.bitcast(i32), bits, -1.0, float(0x5F3759DF), ALU.mult, ALU.add))
                tmp = bits.bitcast(fp32)
                for _ in range(3):
                    seq(V.scalar_tensor_tensor(tmp, dst, -0.5, dst, ALU.mult, ALU.mult))
                    seq(V.tensor_tensor(tmp, tmp, src, ALU.mult))
                    seq(V.scalar_tensor_tensor(dst, tmp, 1.5, dst, ALU.add, ALU.mult))

            def split(name):
                src = {"stk": stk, "fln": fx}.get(name, xn)
                for j in range(2):
                    t = slice(8 * j, 8 * j + 8)
                    dve.wait_ge(S["high_ready"], 2 * SPL.index(name) + j + 1)
                    V.tensor_tensor(xt[:, t, 1, :], src[:, t, :], xt[:, t, 0, :], ALU.subtract)\
                        .then_inc(S["low_ready"], 1)
                if name in TRN:
                    dve.wait_ge(S["halves_T"], 2 * TRN.index(name) + 2)
                    V.tensor_copy(xs[:, 1024:2048], bank[7][:, :].bitcast(fp16)).then_inc(S["chan_vec"], 1)

            def ln(s, src, eps):
                for x in range(NT):
                    last = V.bn_stats(bst[:, x, :], src[:, x, :])
                seq(last)
                for x in range(NT):
                    last = V.bn_aggr(mv[:, x, :], bst[:, x, :])
                seq(last)
                seq(V.tensor_scalar_add(veps[:, 0:NT], mv[:, :, 1], eps))
                rsqrt(rstd[:, 0:NT], veps[:, 0:NT], NT)
                seq(V.tensor_tensor(xn[:, :, :], src[:, :, :], bc(mv[:, :, 0], C), ALU.subtract))
                for j in range(2):
                    t = slice(8 * j, 8 * j + 8)
                    V.tensor_tensor(xn[:, t, :], xn[:, t, :], bc(rstd[:, t], C), ALU.mult).then_inc(S["src_ready"], 1)
                dve.wait_ge(S["src_ready"], 2 * SPL.index(f"ln{s}") + 2)
                split(f"ln{s}")

            def routing(m):
                cfg = MOE[m]
                E = cfg["E"]
                L, Pb, Kk, O1, O2 = (a[:, :, 0:E] for a in (rl, rp, rk, o1, o2))
                mxl, sm, m1, m2, r1, den = (a[:, :] for a in rm)
                rank = row(K["rank8" if E == 8 else "rank16"], NT)
                dve.wait_ge(S["logits_out"], m + 1)
                src = bank[5][:, 0:NT * E].rearrange("p (t e) -> p t e", e=E)
                if f"gb{m}" in K:
                    seq(V.scalar_tensor_tensor(L, src, 1 / WSCALE, row(K[f"gb{m}"], NT), ALU.mult, ALU.add))
                else:
                    seq(V.tensor_scalar_mul(L, src, 1 / WSCALE))
                seq(V.tensor_reduce(mxl, L, AX, ALU.max))
                V.tensor_tensor(L, L, bc(mxl, E), ALU.subtract).then_inc(S["sub_ready"], 1)
                if cfg["skip"]:
                    V.tensor_tensor(base[:, :, :], res[:, :, :], xn[:, :, :], ALU.add)
                dve.wait_ge(S["exp_ready"], m + 1)
                seq(V.tensor_reduce(sm, Pb, AX, ALU.add))
                seq(V.reciprocal(sm, sm))
                seq(V.tensor_tensor(Pb, Pb, bc(sm, E), ALU.mult))
                seq(V.tensor_reduce(m1, Pb, AX, ALU.max))
                seq(V.tensor_tensor(Kk, Pb, bc(m1, E), ALU.is_equal))
                seq(V.tensor_tensor(Kk, Kk, rank, ALU.mult))
                seq(V.tensor_reduce(r1, Kk, AX, ALU.max))
                seq(V.tensor_tensor(O1, Kk, bc(r1, E), ALU.is_equal))
                seq(V.scalar_tensor_tensor(L, O1, -2.0, Pb, ALU.mult, ALU.add))
                seq(V.tensor_reduce(m2, L, AX, ALU.max))
                seq(V.tensor_tensor(Kk, L, bc(m2, E), ALU.is_equal))
                seq(V.tensor_tensor(Kk, Kk, rank, ALU.mult))
                seq(V.tensor_reduce(r1, Kk, AX, ALU.max))
                seq(V.tensor_tensor(O2, Kk, bc(r1, E), ALU.is_equal))
                seq(V.tensor_tensor(O1, O1, O2, ALU.add))
                if cfg["norm"]:
                    seq(V.tensor_tensor(den, m1, m2, ALU.add))
                    if m != 1:
                        seq(V.tensor_scalar_max(den, den, 1e-12))
                    seq(V.reciprocal(den, den))
                    seq(V.tensor_tensor(Pb, Pb, bc(den, E), ALU.mult))
                seq(V.tensor_tensor(Pb, Pb, O1, ALU.mult))
                hi, lo = c2[:, :, 0:E], c2[:, :, E:2 * E]
                seq(V.tensor_scalar_mul(hi, Pb, CSCALE))
                V.scalar_tensor_tensor(lo, Pb, CSCALE, hi, ALU.mult, ALU.subtract).then_inc(S["comb_ready"], 1)
                if f"b2_{m}" in K:
                    seq(V.tensor_scalar_mul(b2s[:, 0, :], K[f"b2_{m}"], WSCALE))
                    V.scalar_tensor_tensor(b2s[:, 1, :], K[f"b2_{m}"], WSCALE, b2s[:, 0, :], ALU.mult, ALU.subtract)\
                        .then_inc(S["b2_ready"], 1)
                dve.wait_ge(S["comb_T"], 2 * m + 2)
                V.tensor_copy(cT[0:2 * E, 1024:2048], bank[5][0:2 * E, :].bitcast(fp16)).then_inc(S["comb_vec"], 1)

            def moe(m):
                cfg = MOE[m]
                routing(m)
                U = units[m]
                N = chunks * U
                for k in range(N + LAG + 1):
                    n = first_unit[m] + k
                    if k < N:
                        dve.wait_ge(S["act_out"], n + 1)
                        src = g[:, n % DEPTH, :]
                        if cfg["swiglu"]:
                            V.tensor_tensor(u[:, n % DEPTH, :], src, bank[2 + k % 2][:, :], ALU.mult)\
                                .then_inc(S["branch_in"], 1)
                            dve.wait_ge(S["branch_in"], k + 1)
                            src = u[:, n % DEPTH, :]
                        dve.wait_ge(S["cb_out"], n + 1)
                        V.tensor_tensor(gw[:, n % DEPTH, :], src, bank[4 + k % 2][:, :], ALU.mult)\
                            .then_inc(S["weighted"], 1)
                    if 1 <= k <= N and not low_on_pool(m, k - 1):
                        dve.wait_ge(S["unit_high"], n)
                        V.tensor_tensor(gl[:, (n - 1) % DEPTH, :], gw[:, (n - 1) % DEPTH, :],
                                        gh[:, (n - 1) % DEPTH, :], ALU.subtract).then_inc(S["unit_low_vec"], 1)
                    if k > LAG and (k - LAG) % U == 0:
                        c = (k - LAG) // U - 1
                        dve.wait_ge(S["second_out"], first_unit[m] + U * (c + 1))
                        src = base if cfg["skip"] else res
                        t = slice(4 * c, 4 * c + 4)
                        acc = bank[6 + c % 2][:, :].rearrange("p (t a c) -> p t a c", a=2, c=C)
                        seq(V.scalar_tensor_tensor(res[:, t, :], acc[:, :, 0, :], 1 / (WSCALE * CSCALE), src[:, t, :],
                                                   ALU.mult, ALU.add))
                        V.scalar_tensor_tensor(res[:, t, :], acc[:, :, 1, :], 1 / (WSCALE * CSCALE), res[:, t, :],
                                               ALU.mult, ALU.add).then_inc(S["acc_in"], 1)
                dve.wait_ge(S["acc_in"], (m + 1) * chunks)

            dve.wait_ge(loaded["c0"], 16)
            ln(0, K["xT"].rearrange("p (t c) -> p t c", c=C), EPS_C)
            dve.wait_ge(loaded["c1"], 16)
            seq(V.tensor_scalar_add(small[:, :], K["bnv"], 1e-5))
            rsqrt(bns[:, :], small[:, :], 64)
            seq(V.tensor_tensor(bns[:, :], bns[:, :], K["bng"], ALU.mult))
            V.tensor_tensor(wfs[:, :], K["wf"], bns[:, :], ALU.mult)
            seq(V.tensor_tensor(bfs[:, :], K["bf"], K["bnm"], ALU.subtract))
            seq(V.tensor_tensor(bfs[:, :], bfs[:, :], bns[:, :], ALU.mult))
            V.tensor_tensor(bfs[:, :], bfs[:, :], K["bnb"], ALU.add).then_inc(S["wf_in"], 1)
            for n in range(8):
                dve.wait_ge(S["qkv_out"], n + 1)
                V.scalar_tensor_tensor(qkv[:, 2 * n:2 * n + 2, :],
                                       bank[n % 4][:, :].rearrange("p (t c) -> p t c", c=256), 1 / WSCALE,
                                       row(K["bqkv"], 2), ALU.mult, ALU.add).then_inc(S["qkv_in"], 1)
            dve.wait_ge(S["sq_ready"], 1)
            seq(V.tensor_reduce(veps[:, 0:32], big[:, 0:2048].rearrange("p (t c) -> p t c", c=64), AX, ALU.add))
            seq(V.tensor_scalar(veps[:, 0:32], veps[:, 0:32], 1.0 / 64, 1e-8, ALU.mult, ALU.add))
            rsqrt(ms[:, :], veps[:, 0:32], 32)
            qk = qkv[:, :, 0:P].rearrange("p t (a c) -> p t a c", a=2)
            rq = ms[:, :].rearrange("p (t a) -> p t a", a=2)
            for a, dst in ((0, q1[:, :, :]), (1, qk[:, :, 1, :])):
                V.tensor_tensor(dst, qk[:, :, a, :], bc(rq[:, :, a], 64), ALU.mult)\
                    .then_inc(S["qk_normed"], 1)
            dve.wait_ge(S["kv_out"], 1)
            seq(V.tensor_tensor(kvm[:, :, :], bank[4][:, :].rearrange("p (j c) -> p j c", c=P),
                                row(K["headmask"], 4), ALU.mult))
            seq(V.tensor_reduce(kvc[:, :, :], kvm[:, :, :].rearrange("p j (g c) -> p j c g", c=16), AX, ALU.add))
            flat = kvc[:, :, :].rearrange("p j c -> p (j c)")
            V.tensor_tensor(kvs[:, :], flat, flat, ALU.mult).then_inc(S["kv_sq"], 1)
            dve.wait_ge(S["kvn_out"], 1)
            seq(V.tensor_scalar_add(veps[:, :], bank[5][:, 0:64], 1e-8))
            rsqrt(kvs[:, :], veps[:, :], 64)
            seq(V.tensor_tensor(flat, flat, kvs[:, :], ALU.mult))
            seq(V.tensor_reduce(gsum[:, :], kvc[:, :, 8:16], AX, ALU.add))
            blocks = row(bc(K["blockmask"], 8), 4)
            V.tensor_tensor(bdg[:, :, :, :], bc(bc(gsum[:, :], 16), 8), blocks, ALU.mult)
            V.tensor_tensor(bdc[:, :, :, :], kvc[:, :, 0:8].unsqueeze(2).broadcast_to([P, 4, 16, 8]), blocks,
                            ALU.mult).then_inc(S["heads_ready"], 1)
            dve.wait_ge(S["gate_out"], 1)
            for j in range(2):
                last = V.tensor_reduce(small[:, 2 * j:2 * j + 2],
                                       bank[2 + j][:, :].rearrange("p (a c) -> p a c", c=NPIX), AX, ALU.max)
            seq(last)
            V.tensor_scalar_mul(small[:, 4:8], small[:, 0:4], -1.0 / 128).then_inc(S["gmax_ready"], 1)
            dve.wait_ge(S["gexp_ready"], 4)
            seq(V.reciprocal(small[:, 12:16], small[:, 8:12]))
            for j in range(4):
                V.scalar_tensor_tensor(qkg[:, j, :], bank[j // 2][:, 256 * (j % 2):256 * (j % 2) + 256],
                                       small[:, 12 + j:13 + j], eg[:, j, :], ALU.mult, ALU.mult)\
                    .then_inc(S["gated"], 1)
            dve.wait_ge(S["wf_out"], 1)
            xR = K["xR"].rearrange("p (t c) -> p t c", c=C)
            for h in range(2):
                q = slice(64 * h, 64 * h + 64)
                for j in range(2):
                    last = V.scalar_tensor_tensor(res[q, 8 * j:8 * j + 8, :],
                                                  bank[2 * h + j][q, :].rearrange("p (t c) -> p t c", c=C), 0.0,
                                                  xR[q, 8 * j:8 * j + 8, :], ALU.max, ALU.add)
            seq(last)
            dve.wait_ge(loaded["r"], 16)
            ln(1, res, EPS_T)
            moe(0)

            ln(2, res, EPS_C)
            dve.wait_ge(loaded["l1"], 16)
            dve.wait_ge(S["pads_set"], 1)
            seq(V.tensor_tensor(mix[:, :].rearrange("p (t c) -> p t c", c=16),
                                K["fcmask"].rearrange("p (t c) -> p t c", c=16), bc(K["fcrep"], 16), ALU.mult))
            for h in range(2):
                q = slice(64 * h, 64 * h + 64)
                V.tensor_tensor(mix[q, :], mix[q, :], K["ident"][q, 64 * h:64 * h + 64], ALU.add)
            seq(V.tensor_scalar_mul(projs[:, :], K["projw"], K["lng"]))
            for name, a in (("mix", mix[:, :]), ("projs", projs[:, :])):
                seq(V.tensor_scalar_mul(WH[name], a, WSCALE))
                V.scalar_tensor_tensor(WL[name], a, WSCALE, WH[name], ALU.mult, ALU.subtract)\
                    .then_inc(S["mix_set"], 1)
            for n in range(8):
                t = slice(2 * n, 2 * n + 2)
                dve.wait_ge(S["kv1_out"], n + 1)
                src = bank[n % 4][:, 0:384].rearrange("p (t c) -> p t c", c=192)
                V.scalar_tensor_tensor(q1[:, t, :], src[:, :, 0:64], 1 / WSCALE, row(K["qkvb"][:, 0:64], 2),
                                       ALU.mult, ALU.add)
                V.scalar_tensor_tensor(kvx[:, 1, PADX + 2 * n:PADX + 2 * n + 2, :, :].rearrange("p t a c -> p t (a c)"),
                                       src[:, :, 64:192], 1 / WSCALE, row(K["qkvb"][:, 64:192], 2), ALU.mult, ALU.add)\
                    .then_inc(S["kv1_in"], 1)
            dve.wait_ge(S["kv1_in"], 8)
            dve.wait_ge(S["pb_out"], 1)
            V.tensor_tensor(pbias[:, :], bank[4][:, 0:64], K["projb"], ALU.add).then_inc(S["pbias_in"], 1)
            for r in (1, 0, 2):
                for i, d in enumerate(DILS):
                    if r != 1:
                        dve.wait_ge(S["shift_in"], 2 * (2 * i + r // 2) + 2)
                    pr = big[:, 2304 * (i % 2):2304 * (i % 2) + 768].rearrange("p (x s c) -> p x s c", s=3, c=16)
                    for s in range(3):
                        x0 = PADX + (s - 1) * d
                        last = V.tensor_tensor(pr[:, :, s, :], q1[:, :, 16 * i:16 * i + 16],
                                               kvx[:, r, x0:x0 + NT, 0, 16 * i:16 * i + 16], ALU.mult)
                    seq(last)
                    for hd in range(2):
                        V.tensor_reduce(lg[:, :, i, hd, 3 * r:3 * r + 3], pr[:, :, :, 8 * hd:8 * hd + 8], AX, ALU.add)
            seq(V.tensor_copy(ls[:, 0:1], K["projb"][:, 0:1]))
            lg3 = lg[:, :, :, :, :].rearrange("p x i h t -> p (x i h) t")
            le3 = le[:, :, :, :, :].rearrange("p x i h t -> p (x i h) t")
            seq(V.tensor_reduce(lm[:, :], lg3, AX, ALU.max))
            V.tensor_tensor(lg3, lg3, bc(lm[:, :], 9), ALU.subtract).then_inc(S["att_sub"], 1)
            dve.wait_ge(S["att_exp"], 1)
            seq(V.tensor_reduce(ls[:, :], le3, AX, ALU.add))
            seq(V.reciprocal(ls[:, :], ls[:, :]))
            for i, d in enumerate(DILS):
                pv = big[:, 2304 * (i % 2):2304 * (i % 2) + 2304].rearrange("p (x c t) -> p x c t", c=16, t=9)
                for t in range(9):
                    r, s = t // 3, t % 3
                    x0 = PADX + (s - 1) * d
                    last = V.tensor_tensor(
                        pv[:, :, :, t].rearrange("p x (h c) -> p x h c", h=2), bc(le[:, :, i, :, t], 8),
                        kvx[:, r, x0:x0 + NT, 1, 16 * i:16 * i + 16].rearrange("p x (h c) -> p x h c", h=2),
                        ALU.mult)
                seq(last)
                seq(V.tensor_reduce(stk[:, :, 16 * i:16 * i + 16], pv, AX, ALU.add))
            s3 = stk[:, :, :].rearrange("p x (g c) -> p (x g) c", c=8)
            for j in range(2):
                q = slice(64 * j, 64 * j + 64)
                V.tensor_tensor(s3[:, q, :], s3[:, q, :], bc(ls[:, q], 8), ALU.mult).then_inc(S["src_ready"], 1)
            dve.wait_ge(S["src_ready"], 2 * SPL.index("stk") + 2)
            split("stk")
            V.tensor_tensor(base[:, :, :], res[:, :, :], row(pbias[:, :], NT), ALU.add).then_inc(S["stk_ready"], 1)
            dve.wait_ge(S["mix_out"], 1)
            for h in range(2):
                last = V.scalar_tensor_tensor(fx[:, 8 * h:8 * h + 8, :],
                                              bank[h][:, :].rearrange("p (x c) -> p x c", c=C), 1 / WSCALE,
                                              row(K["fcb"], 8), ALU.mult, ALU.add)
            seq(last)
            f3 = fx[:, :, :].rearrange("p x (t c) -> p (x t) c", c=16)
            seq(V.tensor_reduce(small[:, :], f3, AX, ALU.add))
            seq(V.tensor_scalar_mul(small[:, :], small[:, :], 1.0 / 16))
            V.tensor_tensor(f3, f3, bc(small[:, :], 16), ALU.subtract).then_inc(S["cent_ready"], 1)
            dve.wait_ge(S["fsq_ready"], 1)
            seq(V.tensor_reduce(veps[:, :], fq[:, :, :].rearrange("p x (t c) -> p (x t) c", c=16), AX, ALU.add))
            seq(V.tensor_scalar(veps[:, :], veps[:, :], 1.0 / 16, 1e-5, ALU.mult, ALU.add))
            rsqrt(rstd[:, :], veps[:, :], 64)
            for j in range(2):
                V.tensor_tensor(f3[:, 32 * j:32 * j + 32, :], f3[:, 32 * j:32 * j + 32, :],
                                bc(rstd[:, 32 * j:32 * j + 32], 16), ALU.mult).then_inc(S["src_ready"], 1)
            dve.wait_ge(S["src_ready"], 2 * SPL.index("fln") + 2)
            split("fln")
            dve.wait_ge(S["proj_out"], 1)
            for h in range(2):
                t = slice(8 * h, 8 * h + 8)
                last = V.scalar_tensor_tensor(res[:, t, :], bank[h][:, :].rearrange("p (x c) -> p x c", c=C),
                                              1 / WSCALE, base[:, t, :], ALU.mult, ALU.add)
            seq(last)
            ln(3, res, EPS_T)
            moe(1)

            ln(4, res, EPS_C)
            V.tensor_reduce(xsum[:, :], xn[:, :, :].rearrange("p x c -> p c x"), AX, ALU.add).then_inc(S["xsum_ready"], 1)
            dve.wait_ge(loaded["l2"], 16)
            seq(V.tensor_tensor(phig[:, :, :], K["phi"].rearrange("p (k n) -> p k n", n=4), row(K["rms"], 24), ALU.mult))
            V.tensor_reduce(phis[:, :], phig[:, :, :], AX, ALU.add).then_inc(S["phis_ready"], 1)
            dve.wait_ge(S["pool_out"], 1)
            V.tensor_scalar_mul(pooledT[:, :], bank[6][0:64, 0:P], 1.0 / NPIX).then_inc(S["poolT_in"], 1)
            seq(V.tensor_scalar_mul(pooled[:, :], bank[6][:, P:P + 64], 1.0 / NPIX))
            seq(V.tensor_tensor(cbs[:, :], pooled[:, :], pooled[:, :], ALU.mult))
            seq(V.tensor_reduce(sc[:, 0:1], cbs[:, :], AX, ALU.add))
            seq(V.tensor_scalar(sc[:, 0:1], sc[:, 0:1], 1.0 / 64, 1e-20, ALU.mult, ALU.add))
            rsqrt(sc[:, 1:2], sc[:, 0:1], 1)
            for x in range(1, NT, 2):
                dve.wait_ge(S["stack_T"], x + 1)
                V.tensor_copy(stack[:, :, x, :], bank[2 + x % 4][:, 0:3 * P].rearrange("p (r t) -> p r t", r=3))\
                    .then_inc(S["stack_vec"], 1)
            dve.wait_ge(S["co_out"], 1)
            seq(V.scalar_tensor_tensor(co[:, :], bank[7][:, 0:24], sc[:, 1:2], K["phib"], ALU.mult, ALU.add))
            V.tensor_tensor(co[:, :], co[:, :], K["alpha"], ALU.mult).then_inc(S["cz_ready"], 1)
            dve.wait_ge(S["ce_ready"], 2)
            seq(V.tensor_scalar_add(hx[:, 0:8], hx[:, 0:8], 1.0))
            seq(V.reciprocal(hx[:, 0:8], hx[:, 0:8]))
            V.tensor_reduce(sc[:, 2:4], hx[:, 0:8].rearrange("p (a n) -> p a n", n=4), AX, ALU.add)
            M = hx[:, 8:24].rearrange("p (a b) -> p a b", b=4)
            MT = hx[:, 8:24].rearrange("p (a b) -> p b a", b=4)
            for _ in range(20):
                for v in (M, MT):
                    seq(V.tensor_reduce(rs4[:, :], v, AX, ALU.add))
                    seq(V.reciprocal(rs4[:, :], rs4[:, :]))
                    seq(V.tensor_tensor(v, v, bc(rs4[:, :], 4), ALU.mult))
            seq(V.tensor_reduce(sc[:, 4:5], hx[:, 8:24:5], AX, ALU.add))
            V.tensor_scalar_mul(sc[:, 4:5], sc[:, 4:5], 0.25)
            seq(V.tensor_scalar_mul(sc[:, 3:4], sc[:, 3:4], 0.5))
            V.scalar_tensor_tensor(sc[:, 5:6], sc[:, 2:3], 1 / WSCALE, sc[:, 3:4], ALU.mult, ALU.mult)
            seq(V.tensor_scalar_mul(cbs[:, :], K["convb"], sc[:, 3:4]))
            seq(V.scalar_tensor_tensor(base[:, :, :], xn[:, :, :], sc[:, 4:5], res[:, :, :], ALU.mult, ALU.add))
            seq(V.tensor_tensor(base[:, :, :], base[:, :, :], row(cbs[:, :], NT), ALU.add))
            for h in range(2):
                dve.wait_ge(S["conv_out"], h + 1)
                last = V.scalar_tensor_tensor(res[:, 8 * h:8 * h + 8, :],
                                              bank[h][:, :].rearrange("p (x c) -> p x c", c=C), sc[:, 5:6],
                                              base[:, 8 * h:8 * h + 8, :], ALU.mult, ALU.add)
            seq(last)
            ln(5, res, EPS_T)
            moe(2)

            ln(6, res, EPS_C)
            dve.wait_ge(S["wsplit"], len(SPLIT))
            V.tensor_tensor(cb2, K["cbT"], K["cbT"], ALU.mult).then_inc(S["cb_sq"], 1)
            seq(V.tensor_tensor(fq[:, :, :], xn[:, :, :], xn[:, :, :], ALU.mult))
            V.tensor_reduce(zz[:, :], fq[:, :, :], AX, ALU.add)
            dve.wait_ge(S["dot_out"], 1)
            V.tensor_scalar_mul(cc, bank[5][:, 0:CODES], WSCALE ** -2).then_inc(S["zz_ready"], 1)
            for x in range(NT):
                n, e = x // 2, x % 2
                if e == 0:
                    dve.wait_ge(S["dot_out"], n + 2)
                dve.wait_ge(S["zc_ready"], x + 1)
                V.scalar_tensor_tensor(nd[:, e, :], bank[n % 4][:, 256 * e:256 * e + 256], 2.0 / WSCALE,
                                       zc[:, e, :], ALU.mult, ALU.subtract).then_inc(S["dot_in"], 1)
                dve.wait_ge(S["dot_in"], x + 1)
                seq(V.max(mx8[:, x, :], nd[:, e, :]))
                V.max_index(ix8[:, x, :], mx8[:, x, :], nd[:, e, :]).then_inc(S["idx_ready"], 1)
            dve.wait_ge(S["gathered"], 16 * NT)
            seq(V.tensor_tensor(zq[:, :, :], zq[:, :, :], xn[:, :, :], ALU.subtract))
            seq(V.tensor_tensor(zq[:, :, :], zq[:, :, :], xn[:, :, :], ALU.add))
            seq(V.tensor_tensor(res[:, :, :], res[:, :, :], zq[:, :, :], ALU.add))
            dve.wait_ge(S["vec_step"], steps[0])
            ln(7, res, EPS_T)
            moe(3)

        @block.tensor
        def _(pe):
            T = nc.tensor
            ident = K["ident"]

            def transposed(name):
                for j in range(2):
                    pe.wait_ge(S["low_ready"], 2 * SPL.index(name) + j + 1)
                    for x in range(8):
                        mm = T.transpose(bank[6 + j][:, :].bitcast(fp16)[:, P * x:P * x + P],
                                         xt[:, 8 * j + x, :, :].rearrange("p a c -> p (a c)"), K["identh"])
                    mm.then_inc(S["halves_T"], 1)

            def chan_ready(name):
                pe.wait_ge(S["chan_act"], TRN.index(name) + 1)
                pe.wait_ge(S["chan_vec"], TRN.index(name) + 1)

            def project(dst, x, name):
                T.matmul(dst, xs[:, P * x:P * x + P], WH[name], start=True, stop=False)
                return T.matmul(dst, xs[:, P * x:P * x + P], WL[name], start=False, stop=True)

            def split_weights(name):
                pe.wait_ge(S["wsplit"], [b for _, b in SPLIT].index(name) + 1)

            def moe(m):
                cfg = MOE[m]
                E, U = cfg["E"], units[m]
                sel = K["sel1" if m == 1 else "sel3" if m == 3 else "sel0"]
                N = chunks * U
                n0 = first_unit[m]

                def first(k):
                    n, c, un = n0 + k, k // U, k % U
                    hb = 2 if cfg["swiglu"] else 4
                    if k >= hb:
                        pe.wait_ge(S["act_out"], n - hb + 1)
                    if cfg["swiglu"] and k >= 2:
                        pe.wait_ge(S["branch_in"], k - 1)
                    x = xs[:, 512 * c:512 * c + 512]
                    names = [(f"w1_{m}", bank[k % hb])] + ([("wu_1", bank[2 + k % 2])] if cfg["swiglu"] else [])
                    for name, dst in names:
                        T.matmul(dst[:, :], WH[name][:, P * un:P * un + P], x, start=True, stop=False)
                        mm = T.matmul(dst[:, :], WL[name][:, P * un:P * un + P], x, start=False, stop=True)
                    mm.then_inc(S["h_out"], 1)

                def spread(k):
                    n, c, un = n0 + k, k // U, k % U
                    if k >= 2:
                        pe.wait_ge(S["weighted"], n - 1)
                    T.matmul(bank[4 + k % 2][:, :], sel[:, P * un:P * un + P], cT[0:2 * E, 512 * c:512 * c + 512],
                             start=True, stop=True).then_inc(S["cb_out"], 1)

                def second(k):
                    n, c, un = n0 + k, k // U, k % U
                    out_bank = bank[6 + c % 2]
                    if un == 0:
                        if m * chunks + c >= 2:
                            pe.wait_ge(S["acc_in"], m * chunks + c - 1)
                        if not cfg["swiglu"]:
                            for t in range(4):
                                T.matmul(out_bank[:, P * t:P * t + P], cT[0:2 * E, 512 * c + P * t:512 * c + P * t + P],
                                         b2s[:, :, :].rearrange("p a c -> p (a c)"), start=(t == 0), stop=False,
                                         skip_group_check=True)
                    pe.wait_ge(S["unit_high"], n + 1)
                    for part, a in ((gh, 0), (gl, 1)):
                        if a == 1:
                            on_pool = low_on_pool(m, k)
                            pe.wait_ge(S["unit_low_pool" if on_pool else "unit_low_vec"], lows(m, k, on_pool))
                        for t in range(4):
                            for b, w in ((0, WH), (1, WL)):
                                mm = T.matmul(out_bank[:, P * t + 64 * b:P * t + 64 * b + 64],
                                              part[:, n % DEPTH, P * t:P * t + P],
                                              w[f"w2_{m}"][:, 64 * un:64 * un + 64],
                                              start=(cfg["swiglu"] and un == 0 and t == 0 and a == 0 and b == 0),
                                              stop=(un == U - 1 and a == 1), skip_group_check=True)
                    mm.then_inc(S["second_out"], 1)

                chan_ready(f"ln{2 * m + 1}")
                split_weights(f"w2_{m}")
                for x in range(NT):
                    mm = project(bank[5][:, E * x:E * x + E], x, f"rw{m}")
                mm.then_inc(S["logits_out"], 1)
                first(0)
                first(1)
                pe.wait_ge(S["comb_ready"], m + 1)
                for j in range(2):
                    for x in range(8):
                        mm = T.transpose(bank[4 + j][0:2 * E, :].bitcast(fp16)[:, P * x:P * x + P],
                                         c2[:, 8 * j + x, 0:2 * E], K["identh"])
                    mm.then_inc(S["comb_T"], 1)
                pe.wait_ge(S["comb_act"], m + 1)
                pe.wait_ge(S["comb_vec"], m + 1)
                if not cfg["swiglu"]:
                    pe.wait_ge(S["b2_ready"], [1, 0, 2, 3][m])
                for k in range(N + LAG):
                    if 2 <= k < N:
                        first(k)
                    if k < N:
                        spread(k)
                    if k >= LAG:
                        second(k - LAG)

            pe.wait_ge(loaded["half"], 16)
            transposed("ln0")
            chan_ready("ln0")
            split_weights("wqkv")
            for n in range(8):
                if n >= 4:
                    pe.wait_ge(S["qkv_in"], n - 3)
                for e in range(2):
                    mm = project(bank[n % 4][:, 256 * e:256 * e + 256], 2 * n + e, "wqkv")
                mm.then_inc(S["qkv_out"], 1)
            pe.wait_ge(S["qk_normed"], 1)
            for i in range(HALF):
                mm = T.transpose(bank[6 + i // 4][:, P * (i % 4):P * (i % 4) + P],
                                 q1[:, 2 * i:2 * i + 2, :], ident)
                if i % 4 == 3:
                    mm.then_inc(S["q_T"], 1)
            pe.wait_ge(S["qk_normed"], 2)
            for h in range(2):
                for j in range(4):
                    for e in range(2):
                        tt = 2 * (2 * j + e) + h
                        mm = T.matmul(bank[4][64 * h:64 * h + 64, P * j:P * j + P], qkv[:, tt, 64:128],
                                      qkv[:, tt, 128:256], start=(j == 0 and e == 0), stop=(j == 3 and e == 1),
                                      skip_group_check=True)
            mm.then_inc(S["kv_out"], 1)
            pe.wait_ge(S["kv_sq"], 1)
            T.matmul(bank[5][:, 0:64], K["headmean"], kvs[:, :], start=True, stop=True).then_inc(S["kvn_out"], 1)
            pe.wait_ge(S["heads_ready"], 1)
            pe.wait_ge(S["q_chan"], 2)
            for bd, b0 in ((bdg, 2), (bdc, 0)):
                for j in range(4):
                    mm = T.matmul(bank[b0 + j // 2][:, 256 * (j % 2):256 * (j % 2) + 256], bd[:, j, :, :].rearrange("p a c -> p (a c)"),
                                  qC[:, 2 * j:2 * j + 2, :], start=True, stop=True)
            mm.then_inc(S["gate_out"], 1)
            pe.wait_ge(S["gated"], 4)
            pe.wait_ge(S["wf_in"], 1)
            pe.wait_ge(S["consts_set"], 1)
            for h in range(2):
                q = slice(64 * h, 64 * h + 64)
                for j in range(2):
                    T.matmul(bank[2 * h + j][q, :], ones[64 * h:64 * h + 1, :],
                             bfs[64 * h:64 * h + 1, :].unsqueeze(1).broadcast_to([1, 8, 64]),
                             start=True, stop=False, skip_group_check=True)
                    for x in range(8):
                        mm = T.matmul(bank[2 * h + j][q, 64 * x:64 * x + 64],
                                      qkg[q, :, :].rearrange("p j (y x) -> p (j y) x", x=W)[:, :, 8 * j + x],
                                      wfs[q, :], start=False, stop=True, skip_group_check=True)
            mm.then_inc(S["wf_out"], 1)
            transposed("ln1")
            moe(0)

            transposed("ln2")
            pe.wait_ge(S["mix_set"], 2)
            T.matmul(bank[4][:, 0:64], K["lnb"][0:64, :], K["projw"][0:64, :], start=True, stop=True)\
                .then_inc(S["pb_out"], 1)
            chan_ready("ln2")
            split_weights("qkvw")
            for n in range(8):
                if n >= 4:
                    pe.wait_ge(S["kv1_in"], n - 3)
                for e in range(2):
                    mm = project(bank[n % 4][:, 192 * e:192 * e + 192], 2 * n + e, "qkvw")
                mm.then_inc(S["kv1_out"], 1)
            pe.wait_ge(S["kv1_in"], 8)
            pe.wait_ge(S["pbias_in"], 1)
            for n in range(8):
                i = n // 2
                mm = T.matmul(bank[n][:, :], K["shift"][:, P * n:P * n + P],
                              kvx[:, 1, PADX:PADX + NT, :, 16 * i:16 * i + 16], start=True, stop=True)
                mm.then_inc(S["shift_out"], 1)
            for name, weight, done in (("stk", "mix", "mix_out"), ("fln", "projs", "proj_out")):
                transposed(name)
                chan_ready(name)
                for x in range(NT):
                    mm = project(bank[x // 8][:, 64 * (x % 8):64 * (x % 8) + 64], x, weight)
                mm.then_inc(S[done], 1)
            transposed("ln3")
            moe(1)

            pe.wait_ge(S["low_ready"], 2 * SPL.index("ln4") + 2)
            for x in range(NT):
                if x >= 4:
                    pe.wait_ge(S["stack_act" if x % 2 == 0 else "stack_vec"], (x - 4) // 2 + 1)
                T.matmul(bank[2 + x % 4][:, 0:3 * P], xt[:, x, :, :].rearrange("p a c -> p (a c)"), K["rowshift"],
                         start=True, stop=True).then_inc(S["stack_T"], 1)
                if x == 3:
                    pe.wait_ge(S["xsum_ready"], 1)
                    T.matmul(bank[6][0:64, 0:P], xsum[:, :], K["samebatch"], start=True, stop=True)
                    T.matmul(bank[6][:, P:P + 64], K["samebatch"], xsum[:, :], start=True, stop=True)\
                        .then_inc(S["pool_out"], 1)
            pe.wait_ge(S["poolT_in"], 1)
            pe.wait_ge(S["phis_ready"], 1)
            T.matmul(bank[7][:, 0:24], pooledT[:, :], phis[:, :], start=True, stop=True).then_inc(S["co_out"], 1)
            split_weights("convw")
            for h in range(2):
                T.matmul(bank[h][:, :], zrow[:, 0:P], zrow[:, :], start=True, stop=False, skip_group_check=True)
            for x in range(NT):
                pe.wait_ge(S["stack_act" if x % 2 == 0 else "stack_vec"], x // 2 + 1)
                for x0, x1 in ((max(x - 1, 0), min(x + 2, 8)), (max(x - 1, 8), min(x + 2, NT))):
                    if x0 >= x1:
                        continue
                    dst = bank[x0 // 8][:, 64 * (x0 % 8):64 * (x0 % 8) + 64 * (x1 - x0)]
                    for r in range(3):
                        for w in (WH, WL):
                            taps = w["convw"][:, 192 * r + 64 * (x0 - x + 1):192 * r + 64 * (x1 - x + 1)]
                            mm = T.matmul(dst, stack[:, r, x, :], taps, start=False, stop=(x == NT - 1),
                                          skip_group_check=True)
                if x in (8, NT - 1):
                    mm.then_inc(S["conv_out"], 1)
            transposed("ln5")
            moe(2)

            transposed("ln6")
            pe.wait_ge(S["cb_sq"], 1)
            T.matmul(bank[5][:, 0:CODES], K["halfones"], cb2, start=True, stop=True).then_inc(S["dot_out"], 1)
            chan_ready("ln6")
            split_weights("cbT")
            for n in range(8):
                if n >= 4:
                    pe.wait_ge(S["dot_in"], 2 * (n - 3))
                for e in range(2):
                    mm = project(bank[n % 4][:, 256 * e:256 * e + 256], 2 * n + e, "cbT")
                mm.then_inc(S["dot_out"], 1)
            transposed("ln7")
            moe(3)


def kernel(**inputs):
    import numpy as np
    import concourse.bacc as bacc
    from concourse.bass_utils import run_bass_kernel_spmd

    v = {k: np.asarray(a) for k, a in inputs.items()}
    two = lambda a: np.concatenate([a, a], axis=0)
    every = lambda a: np.broadcast_to(a, (P,) + a.shape)
    x = v["x"]
    parts = {"ident": np.eye(P, dtype=np.float32)}
    parts["xT"] = x.reshape(2, 4, C, 2, P).transpose(4, 1, 3, 0, 2).reshape(P, NT * C)
    parts["xR"] = x.transpose(0, 2, 3, 1).reshape(P, NT * C)
    parts["wqkv"] = two(np.concatenate([v["L0_conv_Wq"].T, v["L0_conv_Wk"].T, v["L0_conv_Wv"].T], axis=1))
    parts["bqkv"] = every(np.concatenate([v["L0_conv_bq"], v["L0_conv_bk"], v["L0_conv_bv"]]))
    head = np.arange(64) // 8
    parts["headmask"] = two((head[:, None] == np.arange(128)[None, :] // 16).astype(np.float32))
    parts["headmean"] = (np.arange(P)[:, None] // 8 == np.arange(P)[None, :] // 8).astype(np.float32) / np.float32(8)
    parts["wf"] = two(v["L0_conv_Wf"].T)
    for name, src in (("bf", "bf"), ("bng", "bn_gamma"), ("bnb", "bn_beta"), ("bnm", "bn_mean"), ("bnv", "bn_var")):
        parts[name] = every(v["L0_conv_" + src])
    parts["rank8"] = every(np.arange(8, 0, -1, dtype=np.float32))
    parts["rank16"] = every(np.arange(16, 0, -1, dtype=np.float32))
    for m, s in ((0, "L0_ffn_"), (2, "L2_ffn_")):
        parts[f"rw{m}"] = two(v[s + "router_w"].T)
        parts[f"w1_{m}"] = two(v[s + "w1"].transpose(1, 0, 2).reshape(64, 512))
        parts[f"b1_{m}"] = v[s + "b1"].reshape(4, P).T
        parts[f"w2_{m}"] = v[s + "w2"].reshape(4, P, 64).transpose(1, 0, 2).reshape(P, 256)
        parts[f"b2_{m}"] = two(v[s + "b2"])
    parts["rw1"], parts["gb1"] = two(v["L1_ffn_gate_w"]), every(v["L1_ffn_gate_b"])
    parts["w1_1"] = two(v["L1_ffn_w1"].transpose(1, 0, 2).reshape(64, 2048))
    parts["wu_1"] = two(v["L1_ffn_w2"].transpose(1, 0, 2).reshape(64, 2048))
    parts["w2_1"] = v["L1_ffn_w3"].transpose(1, 0, 2).reshape(P, 1024)
    parts["rw3"], parts["gb3"] = two(v["L3_ffn_gate_w"]), every(v["L3_ffn_gate_b"])
    parts["w1_3"] = two(v["L3_ffn_W1"].transpose(1, 0, 2).reshape(64, 1024))
    parts["b1_3"] = v["L3_ffn_b1"].T
    parts["w2_3"] = v["L3_ffn_W2"].transpose(1, 0, 2).reshape(P, 512)
    parts["b2_3"] = two(v["L3_ffn_b2"])
    parts["qkvw"], parts["qkvb"] = two(v["L1_conv_qkv_w"].T), every(v["L1_conv_qkv_b"])
    b, y = np.arange(P) // H, np.arange(P) % H
    shift = [(b[:, None] == b[None, :]) & (y[:, None] == y[None, :] + r * d) for d in DILS for r in (-1, 1)]
    parts["shift"] = np.stack(shift, axis=1).astype(np.float32).reshape(P, 8 * P)
    parts["fcrep"] = two(np.repeat(v["L1_conv_fc_w"].T, 16, axis=0))
    parts["fcb"] = every(np.repeat(v["L1_conv_fc_b"], 16))
    ch = np.arange(64) % 16
    parts["fcmask"] = two((ch[:, None] == ch[None, :]).astype(np.float32))
    parts["lng"] = np.tile(v["L1_conv_ln_g"], 8)[:, None]
    parts["lnb"] = np.broadcast_to(np.tile(v["L1_conv_ln_b"], 8)[:, None], (P, P))
    parts["projw"], parts["projb"] = two(v["L1_conv_proj_w"].T), every(v["L1_conv_proj_b"])
    parts["samebatch"] = (b[:, None] == b[None, :]).astype(np.float32)
    parts["phi"] = v["L2_conv_phi_w"].reshape(24, 4, 64).transpose(2, 0, 1).reshape(64, 96)
    parts["rms"] = v["L2_conv_rms_w"].reshape(4, 64).T
    parts["phib"] = every(v["L2_conv_phi_b"])
    parts["alpha"] = every(np.concatenate([np.repeat(v["L2_conv_alpha_" + n], k)
                                           for n, k in (("pre", 4), ("post", 4), ("res", 16))]))
    parts["convw"] = two(v["L2_conv_conv_w"].transpose(1, 2, 3, 0)[:, :, ::-1, :].reshape(64, 576))
    parts["convb"] = every(v["L2_conv_conv_b"])
    parts["cbT"] = two(v["L3_conv_codebook"].T)
    parts["halfones"] = np.concatenate([np.ones((64, P), np.float32), np.zeros((64, P), np.float32)])
    parts["blockmask"] = (np.arange(P)[:, None] // 8 == np.arange(16)[None, :]).astype(np.float32)
    parts["identh"] = np.eye(P)
    parts["rowshift"] = np.concatenate([(b[:, None] == b[None, :]) & (y[:, None] == y[None, :] + r)
                                        for r in (-1, 0, 1)], axis=1)
    for name, E, per, size in (("sel0", 8, 2, 1.0), ("sel1", 16, 1, 1 / WSCALE), ("sel3", 8, 1, 1.0)):
        expert = np.arange(E // per * P) // (P // per)
        parts[name] = (np.tile(np.arange(E), 2)[:, None] == expert[None, :]) * size

    def pack(spec, dtype):
        where, width = pack_columns(spec)
        a = np.zeros((P, width), dtype)
        for name, (at, rows, cols) in where.items():
            a[0:rows, at:at + cols] = parts[name].astype(dtype) if dtype != np.float32 else parts[name]
        return a

    nc = bacc.Bacc("TRN2", target_bir_lowering=False, num_devices=1)
    arrays, dram = {}, {}
    for pk, spec in PACKS.items():
        arrays["in_" + pk] = pack(spec, np.float32)
    arrays["in_half"] = pack(HALF_PACK, np.float16)
    arrays["in_codebook"] = np.ascontiguousarray(v["L3_conv_codebook"])
    for name, a in arrays.items():
        dram[name[3:]] = nc.dram_tensor(name, a.shape, mybir.dt.from_np(a.dtype), kind="ExternalInput").ap()
    codebook = dram.pop("codebook")
    out = nc.dram_tensor("out_tokens", (P, NT, C), mybir.dt.float32, kind="ExternalOutput").ap()
    metaformer(nc, dram, codebook, out)
    r = run_bass_kernel_spmd(nc, [arrays], core_ids=[0])
    tokens = r.results[0]["out_tokens"]
    return tokens.reshape(B, H, W, C).transpose(0, 3, 1, 2)
```

```python
import concourse.bass as bass
from concourse import mybir
from contextlib import ExitStack

B, C, H, W = 8, 64, 16, 16
P = 128
NT = B * H * W // P
HALF = NT // 2
NPIX = H * W
DILS = (1, 2, 4, 8)
PADX = 8
CODES = 256
EPS_C, EPS_T = 1e-6, 1e-5

MOE = [dict(E=8, D2=64, act="gelu", skip=True, norm=True, swiglu=False),
       dict(E=16, D2=128, act="silu", skip=False, norm=True, swiglu=True),
       dict(E=8, D2=64, act="gelu", skip=True, norm=True, swiglu=False),
       dict(E=8, D2=128, act="gelu", skip=False, norm=False, swiglu=False)]

PACKS = {
    "x": [("xT", P, NT * C)],
    "c0": [("wqkv", P, 256), ("bqkv", P, 256), ("ident", P, P), ("headmask", P, 128),
           ("headmean", P, P), ("blockmask", P, 16), ("wf", P, 64), ("bf", P, 64), ("bng", P, 64), ("bnb", P, 64),
           ("bnm", P, 64), ("bnv", P, 64)],
    "c1": [("xR", P, NT * C)],
    "r": [("rw0", P, 8), ("rw1", P, 16), ("rw2", P, 8), ("rw3", P, 8), ("gb1", P, 16), ("gb3", P, 8),
          ("b1_0", P, 4), ("b1_2", P, 4), ("b1_3", P, 8), ("b2_0", 16, 64), ("b2_2", 16, 64), ("b2_3", 16, 64),
          ("rank8", P, 8), ("rank16", P, 16)],
    "l1": [("qkvw", P, 192), ("qkvb", P, 192), ("shift", P, 8 * P), ("fcrep", P, 4), ("fcb", P, 64), ("fcmask", P, 64),
           ("lng", P, 1), ("lnb", P, P), ("projw", P, 64), ("projb", P, 64)],
    "l2": [("samebatch", P, P), ("phi", 64, 96), ("rms", 64, 4), ("phib", P, 24), ("alpha", P, 24),
           ("convw", P, 576), ("convb", P, 64), ("cbT", P, CODES), ("first64", P, 1)],
    "m0": [("w1_0", P, 512), ("w2_0", P, 256)],
    "m1": [("w1_1", P, 2048), ("wu_1", P, 2048), ("w2_1", P, 1024)],
    "m2": [("w1_2", P, 512), ("w2_2", P, 256)],
    "m3": [("w1_3", P, 1024), ("w2_3", P, 512)],
}
STAGED = ("m0", "m1", "m2", "m3")
WSCALE = 64.0
CSCALE = 16.0
SPREAD = [0, 2, 3]
SPLIT = [("c0", "wqkv"), ("r", "rw0"), ("m0", "w1_0"), ("m0", "w2_0"), ("l1", "qkvw"), ("r", "rw1"), ("m1", "w1_1"),
         ("m1", "wu_1"), ("m1", "w2_1"), ("l2", "convw"), ("r", "rw2"), ("m2", "w1_2"), ("m2", "w2_2"), ("l2", "cbT"),
         ("r", "rw3"), ("m3", "w1_3"), ("m3", "w2_3")]
WIDE = ["w1_1", "wu_1", "w2_1", "convw", "w1_3"]
HALF_PACK = [("identh", P, P), ("rowshift", P, 3 * P), ("sel0", 16, 4 * P), ("sel3", 16, 8 * P)]


def pack_columns(spec):
    at, where = 0, {}
    for name, rows, cols in spec:
        where[name] = (at, rows, cols)
        at += cols
    return where, at


def metaformer(nc: bass.Bass, dram, codebook, out):
    fp32, fp16, i32, u32 = mybir.dt.float32, mybir.dt.float16, mybir.dt.int32, mybir.dt.uint32
    ALU = mybir.AluOpType
    ACT = mybir.ActivationFunctionType
    AX = mybir.AxisListType.X

    ctx = ExitStack()
    with ctx:
        def sb(name, shape, dt=fp32):
            return ctx.enter_context(nc.sbuf_tensor(name, shape, dt))

        def sem(name):
            return ctx.enter_context(nc.semaphore(name))

        packs, K = {}, {}
        kvx_mem = sb("kvx_mem", [P, 3 * (NT + 2 * PADX) * 2 * C])
        staged_at = NT * 256
        for pk, spec in PACKS.items():
            where, width = pack_columns(spec)
            if pk in STAGED:
                packs[pk] = kvx_mem[:, staged_at:staged_at + width]
                staged_at += width
            else:
                packs[pk] = sb("pack_" + pk, [P, width])[:, :]
            for name, (at, rows, cols) in where.items():
                K[name] = packs[pk][0:rows, at:at + cols]
        where, width = pack_columns(HALF_PACK)
        packs["half"] = sb("pack_half", [P, width], fp16)[:, :]
        for name, (at, rows, cols) in where.items():
            K[name] = packs["half"][0:rows, at:at + cols]
        WH, WL = {}, {}
        for _, name in SPLIT + [("", "mix"), ("", "projs")]:
            cols = K[name].shape[1] if name in K else 64
            WH[name] = sb(name + "_high", [P, cols], fp16)[:, :]
            WL[name] = sb(name + "_low", [P, cols], fp16)[:, :]

        res = sb("res", [P, NT, C])
        base = sb("base", [P, NT, C])
        xn = sb("xn", [P, NT, C])
        xt = sb("xt", [P, NT, 2, C], fp16)
        xs = sb("xs", [P, NT * P], fp16)
        bst = sb("bst", [P, NT, 6])
        mean = sb("mean", [P, NT])
        gap = sb("gap", [P, NT])
        veps = sb("veps", [P, 64])
        rstd = sb("rstd", [P, 64])
        seed = sb("seed", [P, 64], i32)
        step_part = sb("step_part", [P, 64])

        qkv = kvx_mem[:, 0:NT * 256].rearrange("p (t c) -> p t c", c=256)
        big = sb("big", [P, 2 * 2304])
        qC = sb("qC", [P, HALF, P])
        ms = sb("ms", [P, 32])
        kvm = sb("kvm", [P, 4, P])
        kvc = sb("kvc", [P, 4, 16])
        kvs = sb("kvs", [P, 64])
        gsum = sb("gsum", [P, 4])
        lg_mem = sb("lg_mem", [P, NT * 72])
        bdc = lg_mem[:, 0:512].rearrange("p (j b c) -> p j b c", j=4, b=16)
        bdg = lg_mem[:, 512:1024].rearrange("p (j b c) -> p j b c", j=4, b=16)
        eg = big[:, 2048:3072].rearrange("p (j n) -> p j n", j=4)
        qkg = big[:, 3072:4096].rearrange("p (j n) -> p j n", j=4)
        bns = sb("bns", [P, 64])
        wfs = sb("wfs", [P, 64])
        bfs = sb("bfs", [P, 64])
        ones = sb("ones", [P, 64])
        small = sb("small", [P, 64])

        q1 = sb("q1", [P, NT, C])
        kvx = kvx_mem[:, :].rearrange("p (r x a c) -> p r x a c", r=3, a=2, c=C)
        lg = lg_mem[:, :].rearrange("p (x i h t) -> p x i h t", i=4, h=2, t=9)
        le = lg
        pool_prod = sb("pool_prod", [P, 2304])
        lm = sb("lm", [P, P])
        ls = sb("ls", [P, P])
        stk = q1
        mix = sb("mix", [64 * 2, 64])
        projs = sb("projs", [P, 64])
        pbias = sb("pbias", [P, 64])
        fx = sb("fx", [P, NT, C])
        fq = qC[:, :, :].rearrange("p i (t c) -> p (i t) c", c=C)

        stack = kvx_mem[:, 0:3 * NT * P // 2].bitcast(fp16).rearrange("p (r x t) -> p r x t", r=3, t=P)
        probe = sb("probe", [1, 2])
        zrow = sb("zrow", [1, 512], fp16)
        xsum = sb("xsum", [P, 64])
        pooled = sb("pooled", [P, 64])
        pooledT = sb("pooledT", [64, P])
        phig = sb("phig", [64, 24, 4])
        phis = sb("phis", [64, 24])
        co = sb("co", [P, 24])
        hx = sb("hx", [P, 24])
        rs4 = sb("rs4", [P, 4])
        sc = sb("sc", [P, 8])
        cbs = sb("cbs", [P, 64])

        cb2 = big[:, 1024:1024 + CODES]
        code_norm = sb("code_norm", [1, 2, CODES], fp16)
        minus = sb("minus", [1, P], fp16)
        nd = kvx_mem[:, 0:NT * CODES].rearrange("p (a c) -> p a c", a=NT)
        mx8 = sb("mx8", [P, NT, 8])
        ix8 = sb("ix8", [P, NT, 8], u32)
        zz = sb("zz", [P, NT])
        zq = kvx_mem[:, NT * CODES:NT * (CODES + C)].rearrange("p (t c) -> p t c", c=C)

        rl = sb("rl", [P, NT, 16])
        rp = sb("rp", [P, NT, 16])
        rk = sb("rk", [P, NT, 16])
        o1 = sb("o1", [P, NT, 16])
        o2 = sb("o2", [P, NT, 16])
        rm = [sb(f"rm{i}", [P, NT]) for i in range(6)]
        c2 = sb("c2", [P, NT, 32], fp16)
        cT = sb("cT", [32, NT * P], fp16)
        b2s = sb("b2s", [16, 2, 64], fp16)
        DEPTH = 8
        HIGH_LAG, LOW_LAG, LAG = 2, 3, 5
        ring = DEPTH * 512
        g = kvx_mem[:, 0:ring].rearrange("p (a c) -> p a c", a=DEPTH)
        gw = kvx_mem[:, ring:2 * ring].rearrange("p (a c) -> p a c", a=DEPTH)
        gh = kvx_mem[:, 2 * ring:5 * ring // 2].bitcast(fp16).rearrange("p (a c) -> p a c", a=DEPTH)
        gl = kvx_mem[:, 5 * ring // 2:3 * ring].bitcast(fp16).rearrange("p (a c) -> p a c", a=DEPTH)
        weighed = big[:, 0:512].rearrange("p (a t c) -> p a t c", a=2, t=4)

        bank = [ctx.enter_context(nc.psum_tensor(f"bank{i}", [P, 512], fp32)) for i in range(8)]

        loaded = {pk: sem("loaded_" + pk) for pk in packs}
        S = {n: sem(n) for n in (
            "vec_step src_ready high_ready low_ready halves_T chan_act chan_vec wide_scaled wide_high wsplit_high wsplit "
            "consts_set qkv_out qkv_in sq_ready qk_normed q_T q_chan kv_out kv_sq "
            "norm_begun kvn_out heads_ready gate_out gmax_ready gexp_ready gated wf_in wf_out "
            "logits_out sub_ready exp_ready comb_ready comb_T comb_act comb_vec b2_ready "
            "h_out act_out cb_out weighted out_in out_added base_ready unit_high unit_low_vec unit_low_pool second_out acc_in "
            "qk_pool qk_pool_used values_summed pv_pool kv1_out kv1_in shift_out shift_in att_sub att_exp mix_set mix_out pb_out pbias_in "
            "cent_ready fsq_ready proj_out "
            "pads_set stack_T stack_act xsum_ready pool_out phis_ready poolT_in co_out cz_ready "
            "ce_ready post_ready bias_added conv_out conv_scaled conv_added cb_sq norm_out norm_set z_squared zz_ready dot_out nd_ready max_ready idx_ready gathered0 gathered1 gathered2 gathered3 stored").split()}

        block = ctx.enter_context(nc.Block())

        chunks = 4
        SPL = ["ln0", "ln1", "ln2", "stk", "fln", "ln3", "ln4", "ln5", "ln6", "ln7"]
        TRN = [x for x in SPL if x != "ln4"]
        units = [m["E"] * m["D2"] // P for m in MOE]
        first_unit = [chunks * sum(units[:m]) for m in range(4)]

        def spreads(m):
            return chunks * sum(units[a] for a in SPREAD if a < m)

        def low_on_pool(m, k):
            return MOE[m]["swiglu"] or k % 2 == 1

        def lows(m, k, pool):
            before = sum(low_on_pool(a, b) == pool for a in range(m) for b in range(chunks * units[a]))
            return before + sum(low_on_pool(m, b) == pool for b in range(k + 1))

        AFTER_MOE = ("ln2", "ln4", "ln6")

        TAP_ROWS = (1, 0, 2)
        BY_VECTOR = ((0, 0), (1, 0), (1, 1), (2, 0), (2, 1))
        BY_POOL = [(a, i) for a in range(3) for i in range(4) if (a, i) not in BY_VECTOR]

        def logit_products(engine, buffer, r, i):
            for s in range(3):
                x0 = PADX + (s - 1) * DILS[i]
                last = engine.tensor_tensor(buffer.rearrange("p (x s c) -> p x s c", s=3, c=16)[:, :, s, :],
                                            q1[:, :, 16 * i:16 * i + 16],
                                            kvx[:, r, x0:x0 + NT, 0, 16 * i:16 * i + 16], ALU.mult)
            return last

        def value_products(engine, buffer, i):
            pv = buffer.rearrange("p (x c t) -> p x c t", c=16, t=9)
            for t in range(9):
                r, s = t // 3, t % 3
                x0 = PADX + (s - 1) * DILS[i]
                last = engine.tensor_tensor(
                    pv[:, :, :, t].rearrange("p x (h c) -> p x h c", h=2),
                    le[:, :, i, :, t].unsqueeze(3).broadcast_to([P, NT, 2, 8]),
                    kvx[:, r, x0:x0 + NT, 1, 16 * i:16 * i + 16].rearrange("p x (h c) -> p x h c", h=2), ALU.mult)
            return last

        value_buffers = (big[:, 0:2304], big[:, 2304:4608], pool_prod[:, :], big[:, 0:2304])

        @block.sync
        def _(sp):
            for pk in ("x", "r", "m1", "l2", "m3"):
                sp.dma_start(packs[pk], dram[pk]).then_inc(loaded[pk], 16)
            for c in range(chunks):
                sp.wait_ge(S["acc_in"], SPREAD.index(3) * chunks + c + 1)
                t = slice(4 * c, 4 * c + 4)
                sp.dma_start(out[:, t, :], res[:, t, :]).then_inc(S["stored"], 16)
            sp.wait_ge(S["stored"], 16 * chunks)

        @block.gpsimd
        def _(pool):
            nc.gpsimd.memset(ones[:, :], 1.0).then_inc(S["consts_set"], 1)
            nc.gpsimd.memset(zrow[:, :], 0.0).then_inc(S["consts_set"], 1)
            nc.gpsimd.memset(probe[:, :], 0.0).then_inc(S["consts_set"], 1)
            nc.gpsimd.memset(minus[:, :], -WSCALE / 2).then_inc(S["consts_set"], 1)
            narrow = [name for _, name in SPLIT if name not in WIDE]
            for pk, name in SPLIT:
                if name == "qkvw":
                    for wide_pk, wide in SPLIT:
                        if wide in WIDE:
                            pool.wait_ge(loaded[wide_pk], 16)
                            nc.gpsimd.tensor_scalar(K[wide], K[wide], WSCALE, 1.0, ALU.mult, ALU.mult)\
                                .then_inc(S["wide_scaled"], 1)
                if name in WIDE:
                    pool.wait_ge(S["wide_high"], WIDE.index(name) + 1)
                else:
                    n = narrow.index(name)
                    pool.wait_ge(loaded[pk], 16)
                    nc.gpsimd.tensor_scalar(K[name], K[name], WSCALE, 1.0, ALU.mult, ALU.mult)\
                        .then_inc(S["wsplit_high"], 1)
                    pool.wait_ge(S["wsplit_high"], 2 * n + 1)
                    nc.gpsimd.tensor_copy(WH[name], K[name]).then_inc(S["wsplit_high"], 1)
                    pool.wait_ge(S["wsplit_high"], 2 * n + 2)
                nc.gpsimd.tensor_tensor(WL[name], K[name], WH[name], ALU.subtract).then_inc(S["wsplit"], 1)
            def with_skip(m):
                pool.wait_ge(S["src_ready"], chunks * (SPL.index(f"ln{2 * m + 1}") + 1))
                nc.gpsimd.tensor_tensor(base[:, :, :], res[:, :, :], xn[:, :, :], ALU.add).then_inc(S["base_ready"], 1)

            def unit_lows(m):
                for k in range(chunks * units[m]):
                    if low_on_pool(m, k):
                        n = first_unit[m] + k
                        pool.wait_ge(S["unit_high"], n + 1)
                        nc.gpsimd.tensor_tensor(gl[:, n % DEPTH, :], gw[:, n % DEPTH, :], gh[:, n % DEPTH, :],
                                                ALU.subtract).then_inc(S["unit_low_pool"], 1)

            with_skip(0)
            unit_lows(0)
            pool.wait_ge(S["second_out"], chunks * units[0])
            for x in (0, PADX + NT):
                nc.gpsimd.memset(kvx[:, :, x:x + PADX, :, :].rearrange("p r x a c -> p r (x a c)"), 0.0)\
                    .then_inc(S["pads_set"], 1)
            pool.wait_ge(S["kv1_in"], 8)
            pool.wait_ge(S["pads_set"], 2)
            for n, (a, i) in enumerate(BY_POOL):
                r = TAP_ROWS[a]
                if r != 1:
                    pool.wait_ge(S["shift_in"], 2 * (2 * i + r // 2) + 2)
                if n >= 3:
                    pool.wait_ge(S["qk_pool_used"], n - 2)
                logit_products(nc.gpsimd, pool_prod[:, 768 * (n % 3):768 * (n % 3) + 768], r, i)\
                    .then_inc(S["qk_pool"], 1)
            pool.wait_ge(S["att_exp"], 1)
            for i in (2, 3):
                if i == 3:
                    pool.wait_ge(S["values_summed"], 1)
                value_products(nc.gpsimd, value_buffers[i], i).then_inc(S["pv_pool"], 1)
            unit_lows(1)
            nc.gpsimd.tensor_tensor(cb2, K["cbT"], K["cbT"], ALU.mult).then_inc(S["cb_sq"], 1)
            pool.wait_ge(S["post_ready"], 1)
            nc.gpsimd.tensor_tensor(base[:, :, :], res[:, :, :],
                                    cbs[:, :].unsqueeze(1).broadcast_to([P, NT, C]), ALU.add)\
                .then_inc(S["bias_added"], 1)
            pool.wait_ge(S["bias_added"], 1)
            pool.wait_ge(S["conv_scaled"], 2)
            nc.gpsimd.tensor_tensor(base[:, :, :], base[:, :, :], fx[:, :, :], ALU.add).then_inc(S["conv_added"], 1)
            with_skip(2)
            unit_lows(2)
            for x in range(NT):
                pool.wait_ge(S["idx_ready"], x + 1)
                nc.gpsimd.indirect_dma_start(
                    out=zq[:, x, :], out_offset=None, in_=codebook,
                    in_offset=bass.IndirectOffsetOnAxis(ap=ix8[:, x, 0:1], axis=0))\
                    .then_inc(S[f"gathered{x // 4}"], 16)
            unit_lows(3)

        @block.scalar
        def _(act):
            for pk in ("c0", "half", "c1", "m0", "l1", "m2"):
                act.dma_start(packs[pk], dram[pk]).then_inc(loaded[pk], 16)

            def high(name, c, src=xn):
                act.wait_ge(S["src_ready"], chunks * SPL.index(name) + c + 1)
                nc.scalar.activation(xt[:, 4 * c:4 * c + 4, 0, :], src[:, 4 * c:4 * c + 4, :], ACT.Copy)\
                    .then_inc(S["high_ready"], 1)

            def split(name, between=None):
                src = {"stk": stk, "fln": fx}.get(name, xn)
                for c in range(2 if name in AFTER_MOE else 0, chunks):
                    high(name, c, src)
                if between:
                    between()
                if name in TRN:
                    act.wait_ge(S["halves_T"], 2 * TRN.index(name) + 1)
                    nc.scalar.activation(xs[:, 0:1024], bank[6][:, :].bitcast(fp16), ACT.Copy)\
                        .then_inc(S["chan_act"], 1)

            def load_table(function):
                act.wait_ge(S["consts_set"], 3)
                nc.scalar.activation(probe[:, 1:2], probe[:, 0:1], function)

            def moe(m):
                cfg = MOE[m]
                E = cfg["E"]
                for h in range(2):
                    act.wait_ge(S["sub_ready"], 2 * m + h + 1)
                    t = slice(HALF * h, HALF * h + HALF)
                    nc.scalar.activation(rp[:, t, 0:E], rl[:, t, 0:E], ACT.Exp).then_inc(S["exp_ready"], 1)
                load_table(ACT.Silu if cfg["swiglu"] else ACT.Gelu)
                if m in SPREAD:
                    act.wait_ge(S["comb_T"], 2 * SPREAD.index(m) + 1)
                    nc.scalar.activation(cT[0:2 * E, 0:1024], bank[4][0:2 * E, :].bitcast(fp16), ACT.Copy)\
                        .then_inc(S["comb_act"], 1)
                N = chunks * units[m]
                for k in range(N + LAG + 1):
                    n = first_unit[m] + k
                    if k == N + 3 and m < 3:
                        high(f"ln{2 * m + 2}", 0)
                        high(f"ln{2 * m + 2}", 1)
                    if k < N:
                        act.wait_ge(S["h_out"], n + 1)
                        if n >= DEPTH:
                            act.wait_ge(S["second_out"], n - DEPTH + 1)
                        if cfg["swiglu"]:
                            nc.scalar.activation(g[:, n % DEPTH, :], bank[k % 2][:, :], ACT.Silu, scale=1 / WSCALE)\
                                .then_inc(S["act_out"], 1)
                        else:
                            nc.scalar.activation(g[:, n % DEPTH, :], bank[k % 4][:, :], ACT.Gelu,
                                                 bias=K[f"b1_{m}"][:, k % units[m]:k % units[m] + 1],
                                                 scale=1 / WSCALE).then_inc(S["act_out"], 1)
                    if HIGH_LAG <= k < N + HIGH_LAG:
                        n -= HIGH_LAG
                        act.wait_ge(S["weighted"], n + 1)
                        nc.scalar.activation(gh[:, n % DEPTH, :], gw[:, n % DEPTH, :], ACT.Copy)\
                            .then_inc(S["unit_high"], 1)

            def wide_high(n):
                act.wait_ge(S["wide_scaled"], n + 1)
                nc.scalar.activation(WH[WIDE[n]], K[WIDE[n]], ACT.Copy).then_inc(S["wide_high"], 1)

            split("ln0")
            act.wait_ge(S["qkv_in"], 8)
            nc.scalar.activation(big[:, 0:2048].rearrange("p (t c) -> p t c", c=P), qkv[:, :, 0:P], ACT.Square)\
                .then_inc(S["sq_ready"], 1)
            wide_high(0)
            wide_high(1)
            for j in range(2):
                act.wait_ge(S["q_T"], j + 1)
                nc.scalar.activation(qC[:, 4 * j:4 * j + 4, :], bank[6 + j][:, :], ACT.Copy)\
                    .then_inc(S["q_chan"], 1)
            wide_high(2)
            wide_high(3)
            wide_high(4)
            act.wait_ge(S["gmax_ready"], 1)
            for j in range(4):
                nc.scalar.activation(eg[:, j, :], bank[2 + j // 2][:, 256 * (j % 2):256 * (j % 2) + 256], ACT.Exp,
                                     bias=small[:, 4 + j:5 + j], scale=1.0 / 128,
                                     accum_out=small[:, 8 + j:9 + j]).then_inc(S["gexp_ready"], 1)
            split("ln1")
            act.wait_ge(loaded["r"], 16)
            act.wait_ge(S["wsplit"], len(SPLIT))
            moe(0)
            load_table(ACT.Exp)
            split("ln2")
            for n in range(8):
                i, r = n // 2, 2 * (n % 2)
                act.wait_ge(S["shift_out"], n + 1)
                for kv in range(2):
                    nc.scalar.activation(kvx[:, r, PADX:PADX + NT, kv, 16 * i:16 * i + 16],
                                         bank[n][:, :].rearrange("p (x a c) -> p x a c", a=2, c=16)[:, :, kv, :],
                                         ACT.Copy).then_inc(S["shift_in"], 1)
            act.wait_ge(S["att_sub"], 1)
            nc.scalar.activation(le[:, :, :, :, :], lg[:, :, :, :, :], ACT.Exp, scale=8 ** -0.5)\
                .then_inc(S["att_exp"], 1)
            split("stk")
            for h in range(2):
                act.wait_ge(S["cent_ready"], h + 1)
                nc.scalar.activation(fq[:, 8 * h:8 * h + 8, :], fx[:, 8 * h:8 * h + 8, :], ACT.Square)\
                    .then_inc(S["fsq_ready"], 1)
            split("fln")
            split("ln3")
            moe(1)
            load_table(ACT.Exp)
            split("ln4")
            for x in range(NT):
                if x == 8:
                    act.wait_ge(S["cz_ready"], 1)
                    nc.scalar.activation(hx[:, 8:24], co[:, 8:24], ACT.Exp).then_inc(S["ce_ready"], 1)
                    nc.scalar.activation(hx[:, 0:8], co[:, 0:8], ACT.Exp, scale=-1.0).then_inc(S["ce_ready"], 1)
                act.wait_ge(S["stack_T"], x + 1)
                nc.scalar.activation(stack[:, :, x, :], bank[2 + x % 4][:, 0:3 * P].rearrange("p (r t) -> p r t", r=3),
                                     ACT.Copy).then_inc(S["stack_act"], 1)
            act.wait_ge(S["post_ready"], 1)
            for h in range(2):
                act.wait_ge(S["conv_out"], h + 1)
                nc.scalar.activation(fx[:, 8 * h:8 * h + 8, :], bank[h][:, :].rearrange("p (x c) -> p x c", c=C),
                                     ACT.Copy, scale=sc[:, 5:6]).then_inc(S["conv_scaled"], 1)
            split("ln5")
            moe(2)
            def squares(h):
                nc.scalar.activation(fq[:, 8 * h:8 * h + 8, :], xn[:, 8 * h:8 * h + 8, :], ACT.Square)\
                    .then_inc(S["z_squared"], 1)

            squares(0)
            load_table(ACT.Exp)
            split("ln6", between=lambda: squares(1))
            for x in range(NT):
                act.wait_ge(S["zz_ready"], x // 8 + 1)
                act.wait_ge(S["dot_out"], x // 2 + 1)
                nc.scalar.activation(nd[:, x, :], bank[x // 2 % 4][:, 256 * (x % 2):256 * (x % 2) + 256],
                                     ACT.Identity, scale=2.0 / WSCALE, bias=zz[:, x:x + 1])\
                    .then_inc(S["nd_ready"], 1)
            split("ln7")
            moe(3)

        @block.vector
        def _(dve):
            V = nc.vector
            steps = [0]

            def seq(ins):
                steps[0] += 1
                ins.then_inc(S["vec_step"], 1)
                dve.wait_ge(S["vec_step"], steps[0])

            def bc(ap, n):
                return ap.unsqueeze(len(ap.shape)).broadcast_to(list(ap.shape) + [n])

            def row(ap, n):
                return ap.unsqueeze(1).broadcast_to([ap.shape[0], n] + list(ap.shape[1:]))

            def rsqrt(dst, src, n):
                bits = seed[:, 0:n]
                seq(V.tensor_scalar(bits, src.bitcast(i32), 1, None, ALU.arith_shift_right))
                seq(V.tensor_scalar(dst.bitcast(i32), bits, -1.0, float(0x5F1FFFF9), ALU.mult, ALU.add))
                tmp, part = bits.bitcast(fp32), step_part[:, 0:n]
                seq(V.scalar_tensor_tensor(tmp, dst, -0.703952253, dst, ALU.mult, ALU.mult))
                seq(V.tensor_tensor(tmp, tmp, src, ALU.mult))
                seq(V.scalar_tensor_tensor(dst, tmp, 1.68191391, dst, ALU.add, ALU.mult))
                V.scalar_tensor_tensor(tmp, dst, -1.0, dst, ALU.mult, ALU.mult)
                seq(V.tensor_scalar_mul(part, dst, 3.0 / 8))
                seq(V.tensor_tensor(tmp, tmp, src, ALU.mult))
                seq(V.scalar_tensor_tensor(tmp, tmp, 10.0 / 3, tmp, ALU.add, ALU.mult))
                seq(V.scalar_tensor_tensor(dst, tmp, 5.0, part, ALU.add, ALU.mult))

            def low(name, c, src=xn):
                t = slice(4 * c, 4 * c + 4)
                dve.wait_ge(S["high_ready"], chunks * SPL.index(name) + c + 1)
                V.tensor_tensor(xt[:, t, 1, :], src[:, t, :], xt[:, t, 0, :], ALU.subtract)\
                    .then_inc(S["low_ready"], 1)

            def split(name):
                src = {"stk": stk, "fln": fx}.get(name, xn)
                for c in range(2 if name in AFTER_MOE else 0, chunks):
                    low(name, c, src)
                if name in TRN:
                    dve.wait_ge(S["halves_T"], 2 * TRN.index(name) + 2)
                    V.tensor_copy(xs[:, 1024:2048], bank[7][:, :].bitcast(fp16)).then_inc(S["chan_vec"], 1)

            def stats(src, x0, x1, eps, signal=False):
                for x in range(x0, x1):
                    last = V.bn_stats(bst[:, x, :], src[:, x, :])
                    if x == x0 and signal:
                        last.then_inc(S["norm_begun"], 1)
                seq(last)
                st, t = bst[:, x0:x1, :], slice(x0, x1)
                V.tensor_tensor(mean[:, t], st[:, :, 1], st[:, :, 4], ALU.add)
                V.tensor_tensor(gap[:, t], st[:, :, 1], st[:, :, 4], ALU.subtract)
                seq(V.tensor_tensor(veps[:, t], st[:, :, 2], st[:, :, 5], ALU.add))
                V.tensor_scalar_mul(mean[:, t], mean[:, t], 0.5)
                V.scalar_tensor_tensor(gap[:, t], gap[:, t], 0.25, gap[:, t], ALU.mult, ALU.mult)
                seq(V.tensor_scalar(veps[:, t], veps[:, t], 1.0 / C, eps, ALU.mult, ALU.add))
                seq(V.tensor_tensor(veps[:, t], veps[:, t], gap[:, t], ALU.add))

            def normed(src, x0, x1):
                seq(V.tensor_tensor(xn[:, x0:x1, :], src[:, x0:x1, :], bc(mean[:, x0:x1], C), ALU.subtract))
                for x in range(x0, x1, 4):
                    V.tensor_tensor(xn[:, x:x + 4, :], xn[:, x:x + 4, :], bc(rstd[:, x:x + 4], C), ALU.mult)\
                        .then_inc(S["src_ready"], 1)

            def code_distance(h):
                t = slice(8 * h, 8 * h + 8)
                dve.wait_ge(S["z_squared"], h + 1)
                seq(V.tensor_reduce(zz[:, t], fq[:, t, :], AX, ALU.add))
                V.tensor_scalar_mul(zz[:, t], zz[:, t], -1.0).then_inc(S["zz_ready"], 1)

            def ln(s, src, eps):
                x0 = 8 if f"ln{s}" in AFTER_MOE else 0
                stats(src, x0, NT, eps, signal=True)
                rsqrt(rstd[:, x0:NT], veps[:, x0:NT], NT - x0)
                normed(src, x0, NT)
                dve.wait_ge(S["src_ready"], chunks * SPL.index(f"ln{s}") + chunks)
                if s == 6:
                    code_distance(0)
                split(f"ln{s}")

            def alternate(ins):
                steps[0] += 1
                ins.then_inc(S["vec_step"], 1)
                dve.wait_ge(S["vec_step"], steps[0] - 1)

            def routing(m):
                cfg = MOE[m]
                E = cfg["E"]
                rank = row(K["rank8" if E == 8 else "rank16"], HALF)
                halves = (slice(0, HALF), slice(HALF, NT))
                A = [[a[:, t, 0:E] for a in (rl, rp, rk, o1, o2)] for t in halves]
                D = [[a[:, t] for a in rm] for t in halves]
                dve.wait_ge(S["logits_out"], m + 1)
                logits = bank[5][:, 0:NT * E].rearrange("p (t e) -> p t e", e=E)
                for (L, _, _, _, _), t in zip(A, halves):
                    if f"gb{m}" in K:
                        alternate(V.scalar_tensor_tensor(L, logits[:, t, :], 1 / WSCALE, row(K[f"gb{m}"], HALF),
                                                         ALU.mult, ALU.add))
                    else:
                        alternate(V.tensor_scalar_mul(L, logits[:, t, :], 1 / WSCALE))
                for (L, _, _, _, _), d in zip(A, D):
                    alternate(V.tensor_reduce(d[0], L, AX, ALU.max))
                for h, ((L, _, _, _, _), d) in enumerate(zip(A, D)):
                    dve.wait_ge(S["vec_step"], steps[0] - 1 + h)
                    V.tensor_tensor(L, L, bc(d[0], E), ALU.subtract).then_inc(S["sub_ready"], 1)
                for h, (L, _, Kk, _, _) in enumerate(A):
                    dve.wait_ge(S["sub_ready"], 2 * m + h + 1)
                    alternate(V.scalar_tensor_tensor(Kk, L, 0.0, rank, ALU.is_equal, ALU.mult))
                for (_, _, Kk, _, _), d in zip(A, D):
                    alternate(V.tensor_reduce(d[4], Kk, AX, ALU.max))
                for (_, _, Kk, O1, _), d in zip(A, D):
                    alternate(V.tensor_tensor(O1, Kk, bc(d[4], E), ALU.is_equal))
                dve.wait_ge(S["exp_ready"], 2 * m + 2)
                for L, _, _, O1, _ in A:
                    alternate(V.scalar_tensor_tensor(L, O1, -3e38, L, ALU.mult, ALU.add))
                for (L, _, _, _, _), d in zip(A, D):
                    alternate(V.tensor_reduce(d[3], L, AX, ALU.max))
                for (L, _, Kk, _, _), d in zip(A, D):
                    alternate(V.tensor_tensor(Kk, L, bc(d[3], E), ALU.is_equal))
                for _, _, Kk, _, _ in A:
                    alternate(V.tensor_tensor(Kk, Kk, rank, ALU.mult))
                for (_, _, Kk, _, _), d in zip(A, D):
                    alternate(V.tensor_reduce(d[4], Kk, AX, ALU.max))
                for (_, _, Kk, _, O2), d in zip(A, D):
                    alternate(V.tensor_tensor(O2, Kk, bc(d[4], E), ALU.is_equal))
                for _, _, _, O1, O2 in A:
                    alternate(V.tensor_tensor(O1, O1, O2, ALU.add))
                if m != 1:
                    for (_, Ex, _, _, _), d in zip(A, D):
                        alternate(V.tensor_reduce(d[1], Ex, AX, ALU.add))
                for _, Ex, _, O1, _ in A:
                    alternate(V.tensor_tensor(Ex, Ex, O1, ALU.mult))
                if cfg["norm"]:
                    for (_, Ex, _, _, _), d in zip(A, D):
                        alternate(V.tensor_reduce(d[5], Ex, AX, ALU.add))
                    if m != 1:
                        for d in D:
                            alternate(V.scalar_tensor_tensor(d[1], d[1], 1e-12, d[5], ALU.mult, ALU.max))
                total = 5 if m == 1 else 1
                for d in D:
                    alternate(V.reciprocal(d[2], d[total]))
                for (_, Ex, _, _, _), d in zip(A, D):
                    alternate(V.tensor_tensor(Ex, Ex, bc(d[2], E), ALU.mult))
                if m not in SPREAD:
                    dve.wait_ge(S["vec_step"], steps[0])
                    return
                for (_, Ex, _, _, _), t in zip(A, halves):
                    alternate(V.tensor_scalar_mul(c2[:, t, 0:E], Ex, CSCALE))
                for h, ((_, Ex, _, _, _), t) in enumerate(zip(A, halves)):
                    dve.wait_ge(S["vec_step"], steps[0] - 1 + h)
                    V.scalar_tensor_tensor(c2[:, t, E:2 * E], Ex, CSCALE, c2[:, t, 0:E], ALU.mult, ALU.subtract)\
                        .then_inc(S["comb_ready"], 1)
                if f"b2_{m}" in K:
                    seq(V.tensor_scalar_mul(b2s[:, 0, :], K[f"b2_{m}"], WSCALE))
                    V.scalar_tensor_tensor(b2s[:, 1, :], K[f"b2_{m}"], WSCALE, b2s[:, 0, :], ALU.mult, ALU.subtract)\
                        .then_inc(S["b2_ready"], 1)
                dve.wait_ge(S["comb_T"], 2 * SPREAD.index(m) + 2)
                V.tensor_copy(cT[0:2 * E, 1024:2048], bank[5][0:2 * E, :].bitcast(fp16)).then_inc(S["comb_vec"], 1)

            def moe(m):
                cfg = MOE[m]
                routing(m)
                U = units[m]
                N = chunks * U
                if cfg["swiglu"]:
                    gated_units(m)
                    return
                for k in range(N + LAG + 1):
                    n = first_unit[m] + k
                    if k < N:
                        dve.wait_ge(S["act_out"], n + 1)
                        src = g[:, n % DEPTH, :]
                        dve.wait_ge(S["cb_out"], spreads(m) + k + 1)
                        V.tensor_tensor(gw[:, n % DEPTH, :], src, bank[4 + k % 2][:, :], ALU.mult)\
                            .then_inc(S["weighted"], 1)
                    if LOW_LAG <= k < N + LOW_LAG and not low_on_pool(m, k - LOW_LAG):
                        n -= LOW_LAG
                        dve.wait_ge(S["unit_high"], n + 1)
                        V.tensor_tensor(gl[:, n % DEPTH, :], gw[:, n % DEPTH, :], gh[:, n % DEPTH, :],
                                        ALU.subtract).then_inc(S["unit_low_vec"], 1)
                    if k == N and m < 3:
                        rsqrt(rstd[:, 0:8], veps[:, 0:8], 8)
                        normed(res, 0, 8)
                    if k == N + LAG and m < 3:
                        low(f"ln{2 * m + 2}", 0)
                        low(f"ln{2 * m + 2}", 1)
                    if k == LAG + 2 * U + 1 and m < 3:
                        dve.wait_ge(S["acc_in"], SPREAD.index(m) * chunks + 2)
                        stats(res, 0, 8, EPS_C)
                    if k > LAG and (k - LAG) % U == 0:
                        c = (k - LAG) // U - 1
                        dve.wait_ge(S["second_out"], first_unit[m] + U * (c + 1))
                        src = base if cfg["skip"] else res
                        if cfg["skip"]:
                            dve.wait_ge(S["base_ready"], m // 2 + 1)
                        t = slice(4 * c, 4 * c + 4)
                        acc = bank[6 + c % 2][:, 0:256].rearrange("p (t c) -> p t c", c=C)
                        V.scalar_tensor_tensor(res[:, t, :], acc, 1 / (WSCALE * CSCALE), src[:, t, :],
                                               ALU.mult, ALU.add).then_inc(S["acc_in"], 1)
                dve.wait_ge(S["acc_in"], (SPREAD.index(m) + 1) * chunks)

            def gated_units(m):
                U, N, n0 = units[m], chunks * units[m], first_unit[m]
                for k in range(N + LAG + 1):
                    if k < N:
                        dve.wait_ge(S["act_out"], n0 + k + 1)
                        V.scalar_tensor_tensor(gw[:, (n0 + k) % DEPTH, :], g[:, (n0 + k) % DEPTH, :], CSCALE / WSCALE,
                                               bank[2 + k % 2][:, :], ALU.mult, ALU.mult).then_inc(S["weighted"], 1)
                    j = k - LAG - 1
                    if j >= 0:
                        t = slice(4 * (j // U), 4 * (j // U) + 4)
                        dve.wait_ge(S["out_in"], j + 1)
                        if j >= 1:
                            dve.wait_ge(S["out_added"], j)
                        V.tensor_tensor(res[:, t, :], res[:, t, :], weighed[:, j % 2, :, :], ALU.add)\
                            .then_inc(S["out_added"], 1)
                    j = k - LAG
                    if 0 <= j < N:
                        c, e = j // U, j % U
                        dve.wait_ge(S["second_out"], n0 + j + 1)
                        if j >= 2:
                            dve.wait_ge(S["out_added"], j - 1)
                        V.scalar_tensor_tensor(weighed[:, j % 2, :, :],
                                               bank[4 + j % 4][:, 0:256].rearrange("p (t c) -> p t c", c=C),
                                               1 / (WSCALE * CSCALE), bc(rp[:, 4 * c:4 * c + 4, e], C),
                                               ALU.mult, ALU.mult).then_inc(S["out_in"], 1)
                    if k == LAG + 2 * U + 1:
                        dve.wait_ge(S["out_added"], 2 * U + 1)
                        stats(res, 0, 8, EPS_C)
                    if k == N:
                        rsqrt(rstd[:, 0:8], veps[:, 0:8], 8)
                        normed(res, 0, 8)
                    if k == N + LAG:
                        low(f"ln{2 * m + 2}", 0)
                        low(f"ln{2 * m + 2}", 1)
                dve.wait_ge(S["out_added"], N)

            dve.wait_ge(loaded["x"], 16)
            ln(0, K["xT"].rearrange("p (t c) -> p t c", c=C), EPS_C)
            dve.wait_ge(loaded["c0"], 16)
            seq(V.tensor_scalar_add(small[:, :], K["bnv"], 1e-5))
            rsqrt(bns[:, :], small[:, :], 64)
            seq(V.tensor_tensor(bns[:, :], bns[:, :], K["bng"], ALU.mult))
            V.tensor_tensor(wfs[:, :], K["wf"], bns[:, :], ALU.mult)
            seq(V.tensor_tensor(bfs[:, :], K["bf"], K["bnm"], ALU.subtract))
            seq(V.tensor_tensor(bfs[:, :], bfs[:, :], bns[:, :], ALU.mult))
            V.tensor_tensor(bfs[:, :], bfs[:, :], K["bnb"], ALU.add).then_inc(S["wf_in"], 1)
            for n in range(8):
                dve.wait_ge(S["qkv_out"], n + 1)
                V.scalar_tensor_tensor(qkv[:, 2 * n:2 * n + 2, :],
                                       bank[n % 4][:, :].rearrange("p (t c) -> p t c", c=256), 1 / WSCALE,
                                       row(K["bqkv"], 2), ALU.mult, ALU.add).then_inc(S["qkv_in"], 1)
            dve.wait_ge(S["sq_ready"], 1)
            seq(V.tensor_reduce(veps[:, 0:32], big[:, 0:2048].rearrange("p (t c) -> p t c", c=64), AX, ALU.add))
            seq(V.tensor_scalar(veps[:, 0:32], veps[:, 0:32], 1.0 / 64, 1e-8, ALU.mult, ALU.add))
            rsqrt(ms[:, :], veps[:, 0:32], 32)
            qk = qkv[:, :, 0:P].rearrange("p t (a c) -> p t a c", a=2)
            rq = ms[:, :].rearrange("p (t a) -> p t a", a=2)
            for a, dst in ((0, q1[:, :, :]), (1, qk[:, :, 1, :])):
                V.tensor_tensor(dst, qk[:, :, a, :], bc(rq[:, :, a], 64), ALU.mult)\
                    .then_inc(S["qk_normed"], 1)
            dve.wait_ge(S["kv_out"], 1)
            seq(V.tensor_tensor(kvm[:, :, :], bank[4][:, :].rearrange("p (j c) -> p j c", c=P),
                                row(K["headmask"], 4), ALU.mult))
            seq(V.tensor_reduce(kvc[:, :, :], kvm[:, :, :].rearrange("p j (g c) -> p j c g", c=16), AX, ALU.add))
            flat = kvc[:, :, :].rearrange("p j c -> p (j c)")
            V.tensor_tensor(kvs[:, :], flat, flat, ALU.mult).then_inc(S["kv_sq"], 1)
            dve.wait_ge(S["kvn_out"], 1)
            seq(V.tensor_scalar_add(veps[:, :], bank[5][:, 0:64], 1e-8))
            rsqrt(kvs[:, :], veps[:, :], 64)
            seq(V.tensor_tensor(flat, flat, kvs[:, :], ALU.mult))
            seq(V.tensor_reduce(gsum[:, :], kvc[:, :, 8:16], AX, ALU.add))
            blocks = row(bc(K["blockmask"], 8), 4)
            V.tensor_tensor(bdg[:, :, :, :], bc(bc(gsum[:, :], 16), 8), blocks, ALU.mult)
            V.tensor_tensor(bdc[:, :, :, :], kvc[:, :, 0:8].unsqueeze(2).broadcast_to([P, 4, 16, 8]), blocks,
                            ALU.mult).then_inc(S["heads_ready"], 1)
            dve.wait_ge(S["gate_out"], 1)
            for j in range(2):
                last = V.tensor_reduce(small[:, 2 * j:2 * j + 2],
                                       bank[2 + j][:, :].rearrange("p (a c) -> p a c", c=NPIX), AX, ALU.max)
            seq(last)
            V.tensor_scalar_mul(small[:, 4:8], small[:, 0:4], -1.0 / 128).then_inc(S["gmax_ready"], 1)
            dve.wait_ge(S["gexp_ready"], 4)
            seq(V.reciprocal(small[:, 12:16], small[:, 8:12]))
            for j in range(4):
                V.scalar_tensor_tensor(qkg[:, j, :], bank[j // 2][:, 256 * (j % 2):256 * (j % 2) + 256],
                                       small[:, 12 + j:13 + j], eg[:, j, :], ALU.mult, ALU.mult)\
                    .then_inc(S["gated"], 1)
            dve.wait_ge(loaded["l1"], 16)
            seq(V.tensor_tensor(mix[:, :].rearrange("p (t c) -> p t c", c=16),
                                K["fcmask"].rearrange("p (t c) -> p t c", c=16), bc(K["fcrep"], 16), ALU.mult))
            for h in range(2):
                q = slice(64 * h, 64 * h + 64)
                V.tensor_tensor(mix[q, :], mix[q, :], K["ident"][q, 64 * h:64 * h + 64], ALU.add)
            seq(V.tensor_scalar_mul(projs[:, :], K["projw"], K["lng"]))
            for name, a in (("mix", mix[:, :]), ("projs", projs[:, :])):
                seq(V.tensor_scalar_mul(WH[name], a, WSCALE))
                V.scalar_tensor_tensor(WL[name], a, WSCALE, WH[name], ALU.mult, ALU.subtract)\
                    .then_inc(S["mix_set"], 1)
            dve.wait_ge(loaded["l2"], 16)
            seq(V.tensor_tensor(phig[:, :, :], K["phi"].rearrange("p (k n) -> p k n", n=4), row(K["rms"], 24), ALU.mult))
            V.tensor_reduce(phis[:, :], phig[:, :, :], AX, ALU.add).then_inc(S["phis_ready"], 1)
            dve.wait_ge(loaded["c1"], 16)
            dve.wait_ge(S["wf_out"], 1)
            xR = K["xR"].rearrange("p (t c) -> p t c", c=C)
            for h in range(2):
                q = slice(64 * h, 64 * h + 64)
                for j in range(2):
                    last = V.scalar_tensor_tensor(res[q, 8 * j:8 * j + 8, :],
                                                  bank[2 * h + j][q, :].rearrange("p (t c) -> p t c", c=C), 0.0,
                                                  xR[q, 8 * j:8 * j + 8, :], ALU.max, ALU.add)
            seq(last)
            dve.wait_ge(loaded["r"], 16)
            ln(1, res, EPS_T)
            moe(0)

            ln(2, res, EPS_C)
            for n in range(8):
                t = slice(2 * n, 2 * n + 2)
                dve.wait_ge(S["kv1_out"], n + 1)
                src = bank[n % 4][:, 0:384].rearrange("p (t c) -> p t c", c=192)
                V.scalar_tensor_tensor(q1[:, t, :], src[:, :, 0:64], 1 / WSCALE, row(K["qkvb"][:, 0:64], 2),
                                       ALU.mult, ALU.add)
                V.scalar_tensor_tensor(kvx[:, 1, PADX + 2 * n:PADX + 2 * n + 2, :, :].rearrange("p t a c -> p t (a c)"),
                                       src[:, :, 64:192], 1 / WSCALE, row(K["qkvb"][:, 64:192], 2), ALU.mult, ALU.add)\
                    .then_inc(S["kv1_in"], 1)
            dve.wait_ge(S["kv1_in"], 8)
            dve.wait_ge(S["pb_out"], 1)
            V.tensor_tensor(pbias[:, :], bank[4][:, 0:64], K["projb"], ALU.add).then_inc(S["pbias_in"], 1)
            dve.wait_ge(S["pads_set"], 2)
            for a, r in enumerate(TAP_ROWS):
                for i in range(4):
                    if (a, i) in BY_VECTOR:
                        if r != 1:
                            dve.wait_ge(S["shift_in"], 2 * (2 * i + r // 2) + 2)
                        n = BY_VECTOR.index((a, i))
                        buffer = big[:, 768 * n:768 * n + 768]
                        seq(logit_products(V, buffer, r, i))
                    else:
                        n = BY_POOL.index((a, i))
                        buffer = pool_prod[:, 768 * (n % 3):768 * (n % 3) + 768]
                        dve.wait_ge(S["qk_pool"], n + 1)
                    last = V.tensor_reduce(lg[:, :, i, :, 3 * r:3 * r + 3],
                                           buffer.rearrange("p (x s h c) -> p x h s c", s=3, h=2, c=8), AX, ALU.add)
                    if (a, i) in BY_POOL:
                        last.then_inc(S["qk_pool_used"], 1)
            dve.wait_ge(S["qk_pool_used"], len(BY_POOL))
            lg3 = lg[:, :, :, :, :].rearrange("p x i h t -> p (x i h) t")
            le3 = le[:, :, :, :, :].rearrange("p x i h t -> p (x i h) t")
            seq(V.tensor_reduce(lm[:, :], lg3, AX, ALU.max))
            V.tensor_tensor(lg3, lg3, bc(lm[:, :], 9), ALU.subtract).then_inc(S["att_sub"], 1)
            dve.wait_ge(S["att_exp"], 1)
            seq(V.tensor_reduce(ls[:, :], le3, AX, ALU.add))
            seq(V.reciprocal(ls[:, :], ls[:, :]))
            for i in range(4):
                if i < 2:
                    seq(value_products(V, value_buffers[i], i))
                else:
                    dve.wait_ge(S["pv_pool"], i - 1)
                V.tensor_reduce(stk[:, :, 16 * i:16 * i + 16],
                                value_buffers[i].rearrange("p (x c t) -> p x c t", c=16, t=9), AX, ALU.add)\
                    .then_inc(S["values_summed"], 1)
            dve.wait_ge(S["values_summed"], 4)
            s3 = stk[:, :, :].rearrange("p x (g c) -> p (x g) c", c=8)
            for c in range(chunks):
                q = slice(32 * c, 32 * c + 32)
                V.tensor_tensor(s3[:, q, :], s3[:, q, :], bc(ls[:, q], 8), ALU.mult).then_inc(S["src_ready"], 1)
            dve.wait_ge(S["src_ready"], chunks * SPL.index("stk") + chunks)
            split("stk")
            V.tensor_tensor(base[:, :, :], res[:, :, :], row(pbias[:, :], NT), ALU.add)
            dve.wait_ge(S["mix_out"], 1)
            for h in range(2):
                last = V.scalar_tensor_tensor(fx[:, 8 * h:8 * h + 8, :],
                                              bank[h][:, :].rearrange("p (x c) -> p x c", c=C), 1 / WSCALE,
                                              row(K["fcb"], 8), ALU.mult, ALU.add)
            seq(last)
            f3 = fx[:, :, :].rearrange("p x (t c) -> p (x t) c", c=16)
            seq(V.tensor_reduce(small[:, :], f3, AX, ALU.add))
            seq(V.tensor_scalar_mul(small[:, :], small[:, :], 1.0 / 16))
            for h in range(2):
                q = slice(32 * h, 32 * h + 32)
                V.tensor_tensor(f3[:, q, :], f3[:, q, :], bc(small[:, q], 16), ALU.subtract)\
                    .then_inc(S["cent_ready"], 1)
            for h in range(2):
                dve.wait_ge(S["fsq_ready"], h + 1)
                last = V.tensor_reduce(veps[:, 32 * h:32 * h + 32],
                                       fq[:, 8 * h:8 * h + 8, :].rearrange("p x (t c) -> p (x t) c", c=16), AX,
                                       ALU.add)
            seq(last)
            seq(V.tensor_scalar(veps[:, :], veps[:, :], 1.0 / 16, 1e-5, ALU.mult, ALU.add))
            rsqrt(rstd[:, :], veps[:, :], 64)
            for c in range(chunks):
                q = slice(16 * c, 16 * c + 16)
                V.tensor_tensor(f3[:, q, :], f3[:, q, :], bc(rstd[:, q], 16), ALU.mult).then_inc(S["src_ready"], 1)
            dve.wait_ge(S["src_ready"], chunks * SPL.index("fln") + chunks)
            split("fln")
            dve.wait_ge(S["proj_out"], 1)
            for h in range(2):
                t = slice(8 * h, 8 * h + 8)
                last = V.scalar_tensor_tensor(res[:, t, :], bank[h][:, :].rearrange("p (x c) -> p x c", c=C),
                                              1 / WSCALE, base[:, t, :], ALU.mult, ALU.add)
            seq(last)
            ln(3, res, EPS_T)
            moe(1)

            ln(4, res, EPS_C)
            V.tensor_reduce(xsum[:, :], xn[:, :, :].rearrange("p x c -> p c x"), AX, ALU.add).then_inc(S["xsum_ready"], 1)
            dve.wait_ge(S["pool_out"], 1)
            V.tensor_scalar_mul(pooledT[:, :], bank[6][0:64, 0:P], 1.0 / NPIX).then_inc(S["poolT_in"], 1)
            seq(V.tensor_scalar_mul(pooled[:, :], bank[6][:, P:P + 64], 1.0 / NPIX))
            seq(V.tensor_tensor(cbs[:, :], pooled[:, :], pooled[:, :], ALU.mult))
            seq(V.tensor_reduce(sc[:, 0:1], cbs[:, :], AX, ALU.add))
            seq(V.tensor_scalar(sc[:, 0:1], sc[:, 0:1], 1.0 / 64, 1e-20, ALU.mult, ALU.add))
            rsqrt(sc[:, 1:2], sc[:, 0:1], 1)
            dve.wait_ge(S["norm_out"], 1)
            seq(V.tensor_scalar_mul(code_norm[:, 0, :], bank[1][0:1, 0:CODES], WSCALE ** -2))
            V.scalar_tensor_tensor(code_norm[:, 1, :], bank[1][0:1, 0:CODES], WSCALE ** -2, code_norm[:, 0, :],
                                   ALU.mult, ALU.subtract).then_inc(S["norm_set"], 1)
            dve.wait_ge(S["co_out"], 1)
            seq(V.scalar_tensor_tensor(co[:, :], bank[7][:, 0:24], sc[:, 1:2], K["phib"], ALU.mult, ALU.add))
            V.tensor_tensor(co[:, :], co[:, :], K["alpha"], ALU.mult).then_inc(S["cz_ready"], 1)
            dve.wait_ge(S["ce_ready"], 2)
            M = hx[:, 8:24].rearrange("p (a b) -> p a b", b=4)
            MT = hx[:, 8:24].rearrange("p (a b) -> p b a", b=4)
            for step in range(40):
                v = M if step % 2 == 0 else MT
                total = V.tensor_reduce(rs4[:, :], v, AX, ALU.add)
                if step == 0:
                    V.tensor_scalar_add(hx[:, 0:8], hx[:, 0:8], 1.0)
                elif step == 1:
                    V.reciprocal(hx[:, 0:8], hx[:, 0:8])
                elif step == 2:
                    V.tensor_reduce(sc[:, 2:4], hx[:, 0:8].rearrange("p (a n) -> p a n", n=4), AX, ALU.add)
                elif step == 3:
                    V.tensor_scalar_mul(sc[:, 3:4], sc[:, 3:4], 0.5)
                elif step == 4:
                    V.scalar_tensor_tensor(sc[:, 5:6], sc[:, 2:3], 1 / WSCALE, sc[:, 3:4], ALU.mult, ALU.mult)
                elif step == 5:
                    V.tensor_scalar_mul(cbs[:, :], K["convb"], sc[:, 3:4]).then_inc(S["post_ready"], 1)
                seq(total)
                seq(V.reciprocal(rs4[:, :], rs4[:, :]))
                seq(V.tensor_tensor(v, v, bc(rs4[:, :], 4), ALU.mult))
            seq(V.tensor_reduce(sc[:, 4:5], hx[:, 8:24:5], AX, ALU.add))
            seq(V.tensor_scalar_mul(sc[:, 4:5], sc[:, 4:5], 0.25))
            dve.wait_ge(S["conv_added"], 1)
            seq(V.scalar_tensor_tensor(res[:, :, :], xn[:, :, :], sc[:, 4:5], base[:, :, :], ALU.mult, ALU.add))
            ln(5, res, EPS_T)
            moe(2)

            ln(6, res, EPS_C)
            for n in range(HALF):
                if n == 1:
                    code_distance(1)
                for x in (2 * n, 2 * n + 1):
                    dve.wait_ge(S["nd_ready"], x + 1)
                    V.max(mx8[:, x, :], nd[:, x, :]).then_inc(S["max_ready"], 1)
                for x in (2 * n, 2 * n + 1):
                    dve.wait_ge(S["max_ready"], x + 1)
                    V.max_index(ix8[:, x, :], mx8[:, x, :], nd[:, x, :]).then_inc(S["idx_ready"], 1)
            for c in range(chunks):
                t = slice(4 * c, 4 * c + 4)
                dve.wait_ge(S[f"gathered{c}"], 16 * 4)
                seq(V.tensor_tensor(zq[:, t, :], zq[:, t, :], xn[:, t, :], ALU.subtract))
                seq(V.tensor_tensor(zq[:, t, :], zq[:, t, :], xn[:, t, :], ALU.add))
                seq(V.tensor_tensor(res[:, t, :], res[:, t, :], zq[:, t, :], ALU.add))
                stats(res, 4 * c, 4 * c + 4, EPS_T, signal=(c == 3))
            rsqrt(rstd[:, 0:NT], veps[:, 0:NT], NT)
            normed(res, 0, NT)
            dve.wait_ge(S["src_ready"], chunks * SPL.index("ln7") + chunks)
            split("ln7")
            moe(3)

        @block.tensor
        def _(pe):
            T = nc.tensor
            ident = K["ident"]

            def transposed(name):
                for j in range(2):
                    if name in AFTER_MOE:
                        pe.wait_ge(S["acc_in"], chunks * SPREAD.index(AFTER_MOE.index(name)) + 3 + j)
                    for x in range(8):
                        if x % 4 == 0:
                            pe.wait_ge(S["low_ready"], chunks * SPL.index(name) + 2 * j + x // 4 + 1)
                        mm = T.transpose(bank[6 + j][:, :].bitcast(fp16)[:, P * x:P * x + P],
                                         xt[:, 8 * j + x, :, :].rearrange("p a c -> p (a c)"), K["identh"])
                    mm.then_inc(S["halves_T"], 1)

            def chan_ready(name):
                pe.wait_ge(S["chan_act"], TRN.index(name) + 1)
                pe.wait_ge(S["chan_vec"], TRN.index(name) + 1)

            def project(dst, x, name):
                T.matmul(dst, xs[:, P * x:P * x + P], WH[name], start=True, stop=False)
                return T.matmul(dst, xs[:, P * x:P * x + P], WL[name], start=False, stop=True)

            def keep_warm(n, unused=7):
                for _ in range(n):
                    T.matmul(bank[unused][:, :], xs[:, 0:P], xs[:, 0:512], start=True, stop=True)

            def warm_for_norm(s, n):
                pe.wait_ge(S["norm_begun"], s + 1)
                keep_warm(n, unused=2)

            def split_weights(name):
                pe.wait_ge(S["wsplit"], [b for _, b in SPLIT].index(name) + 1)

            def moe(m):
                cfg = MOE[m]
                E, U = cfg["E"], units[m]
                sel = K["sel3" if m == 3 else "sel0"]
                N = chunks * U
                n0 = first_unit[m]
                ahead = 0 if cfg["swiglu"] else 1
                early_units = 2 if cfg["swiglu"] else 4

                def first(k):
                    n, c, un = n0 + k, k // U, k % U
                    hb = 2 if cfg["swiglu"] else 4
                    if k >= hb:
                        pe.wait_ge(S["act_out"], n - hb + 1)
                    if cfg["swiglu"] and k >= 2:
                        pe.wait_ge(S["weighted"], n - 1)
                    x = xs[:, 512 * c:512 * c + 512]
                    names = [(f"w1_{m}", bank[k % hb])] + ([("wu_1", bank[2 + k % 2])] if cfg["swiglu"] else [])
                    for name, dst in names:
                        T.matmul(dst[:, :], WH[name][:, P * un:P * un + P], x, start=True, stop=False)
                        mm = T.matmul(dst[:, :], WL[name][:, P * un:P * un + P], x, start=False, stop=True)
                    mm.then_inc(S["h_out"], 1)

                def spread(k):
                    n, c, un = n0 + k, k // U, k % U
                    if k >= 2:
                        pe.wait_ge(S["weighted"], n - 1)
                    T.matmul(bank[4 + k % 2][:, :], sel[:, P * un:P * un + P], cT[0:2 * E, 512 * c:512 * c + 512],
                             start=True, stop=True).then_inc(S["cb_out"], 1)

                def second(k):
                    n, c, un = n0 + k, k // U, k % U
                    out_bank = bank[4 + k % 4 if cfg["swiglu"] else 6 + c % 2]
                    if cfg["swiglu"] and k >= 4:
                        pe.wait_ge(S["out_in"], k - 3)
                    if un == 0 and not cfg["swiglu"]:
                        if SPREAD.index(m) * chunks + c >= 2:
                            pe.wait_ge(S["acc_in"], SPREAD.index(m) * chunks + c - 1)
                        for t in range(4):
                            for b in range(2):
                                T.matmul(out_bank[:, 64 * t:64 * t + 64],
                                         cT[0:2 * E, 512 * c + P * t:512 * c + P * t + P], b2s[:, b, :],
                                         start=(t == 0 and b == 0), stop=False, skip_group_check=True)
                    pe.wait_ge(S["unit_high"], n + 1)
                    for part, a in ((gh, 0), (gl, 1)):
                        if a == 1:
                            on_pool = low_on_pool(m, k)
                            pe.wait_ge(S["unit_low_pool" if on_pool else "unit_low_vec"], lows(m, k, on_pool))
                        for t in range(4):
                            for b, w in ((0, WH), (1, WL)):
                                mm = T.matmul(out_bank[:, 64 * t:64 * t + 64],
                                              part[:, n % DEPTH, P * t:P * t + P],
                                              w[f"w2_{m}"][:, 64 * un:64 * un + 64],
                                              start=(cfg["swiglu"] and t == 0 and a == 0 and b == 0),
                                              stop=(a == 1 and (cfg["swiglu"] or un == U - 1)),
                                              skip_group_check=True)
                    mm.then_inc(S["second_out"], 1)

                chan_ready(f"ln{2 * m + 1}")
                split_weights(f"w2_{m}")
                for x in range(NT):
                    mm = project(bank[5][:, E * x:E * x + E], x, f"rw{m}")
                mm.then_inc(S["logits_out"], 1)
                for k in range(early_units):
                    first(k)
                keep_warm(12)
                if m in SPREAD:
                    for j in range(2):
                        pe.wait_ge(S["comb_ready"], 2 * SPREAD.index(m) + j + 1)
                        for x in range(8):
                            mm = T.transpose(bank[4 + j][0:2 * E, :].bitcast(fp16)[:, P * x:P * x + P],
                                             c2[:, 8 * j + x, 0:2 * E], K["identh"])
                        mm.then_inc(S["comb_T"], 1)
                    keep_warm(6)
                    pe.wait_ge(S["comb_act"], SPREAD.index(m) + 1)
                    pe.wait_ge(S["comb_vec"], SPREAD.index(m) + 1)
                    pe.wait_ge(S["b2_ready"], SPREAD.index(m) + 1)
                for k in range(N + LAG):
                    if early_units <= k + ahead < N:
                        first(k + ahead)
                    if k < N and m in SPREAD:
                        spread(k)
                    if k >= LAG:
                        second(k - LAG)

            pe.wait_ge(loaded["half"], 16)
            for _ in range(16):
                T.matmul(bank[2][:, 0:3 * P], K["identh"], K["rowshift"], start=True, stop=True)
            transposed("ln0")
            chan_ready("ln0")
            split_weights("wqkv")
            for n in range(8):
                if n >= 4:
                    pe.wait_ge(S["qkv_in"], n - 3)
                for e in range(2):
                    mm = project(bank[n % 4][:, 256 * e:256 * e + 256], 2 * n + e, "wqkv")
                mm.then_inc(S["qkv_out"], 1)
            keep_warm(26, unused=5)
            pe.wait_ge(S["qk_normed"], 1)
            for i in range(HALF):
                mm = T.transpose(bank[6 + i // 4][:, P * (i % 4):P * (i % 4) + P],
                                 q1[:, 2 * i:2 * i + 2, :], ident)
                if i % 4 == 3:
                    mm.then_inc(S["q_T"], 1)
            pe.wait_ge(S["qk_normed"], 2)
            for h in range(2):
                for j in range(4):
                    for e in range(2):
                        tt = 2 * (2 * j + e) + h
                        mm = T.matmul(bank[4][64 * h:64 * h + 64, P * j:P * j + P], qkv[:, tt, 64:128],
                                      qkv[:, tt, 128:256], start=(j == 0 and e == 0), stop=(j == 3 and e == 1),
                                      skip_group_check=True)
            mm.then_inc(S["kv_out"], 1)
            pe.wait_ge(S["kv_sq"], 1)
            T.matmul(bank[5][:, 0:64], K["headmean"], kvs[:, :], start=True, stop=True).then_inc(S["kvn_out"], 1)
            pe.wait_ge(S["q_chan"], 2)
            keep_warm(12, unused=7)
            pe.wait_ge(S["heads_ready"], 1)
            for bd, b0 in ((bdg, 2), (bdc, 0)):
                for j in range(4):
                    mm = T.matmul(bank[b0 + j // 2][:, 256 * (j % 2):256 * (j % 2) + 256], bd[:, j, :, :].rearrange("p a c -> p (a c)"),
                                  qC[:, 2 * j:2 * j + 2, :], start=True, stop=True)
            mm.then_inc(S["gate_out"], 1)
            keep_warm(20, unused=7)
            pe.wait_ge(S["gated"], 4)
            pe.wait_ge(S["wf_in"], 1)
            pe.wait_ge(S["consts_set"], 1)
            for h in range(2):
                q = slice(64 * h, 64 * h + 64)
                for j in range(2):
                    T.matmul(bank[2 * h + j][q, :], ones[64 * h:64 * h + 1, :],
                             bfs[64 * h:64 * h + 1, :].unsqueeze(1).broadcast_to([1, 8, 64]),
                             start=True, stop=False, skip_group_check=True)
                    for x in range(8):
                        mm = T.matmul(bank[2 * h + j][q, 64 * x:64 * x + 64],
                                      qkg[q, :, :].rearrange("p j (y x) -> p (j y) x", x=W)[:, :, 8 * j + x],
                                      wfs[q, :], start=False, stop=True, skip_group_check=True)
            mm.then_inc(S["wf_out"], 1)
            warm_for_norm(1, 20)
            transposed("ln1")
            moe(0)

            warm_for_norm(2, 14)
            transposed("ln2")
            pe.wait_ge(S["mix_set"], 2)
            T.matmul(bank[4][:, 0:64], K["lnb"][0:64, :], K["projw"][0:64, :], start=True, stop=True)\
                .then_inc(S["pb_out"], 1)
            chan_ready("ln2")
            split_weights("qkvw")
            for n in range(8):
                if n >= 4:
                    pe.wait_ge(S["kv1_in"], n - 3)
                for e in range(2):
                    mm = project(bank[n % 4][:, 192 * e:192 * e + 192], 2 * n + e, "qkvw")
                mm.then_inc(S["kv1_out"], 1)
            pe.wait_ge(S["kv1_in"], 8)
            pe.wait_ge(S["pbias_in"], 1)
            for n in range(8):
                i = n // 2
                mm = T.matmul(bank[n][:, :], K["shift"][:, P * n:P * n + P],
                              kvx[:, 1, PADX:PADX + NT, :, 16 * i:16 * i + 16], start=True, stop=True)
                mm.then_inc(S["shift_out"], 1)
            for name, weight, done in (("stk", "mix", "mix_out"), ("fln", "projs", "proj_out")):
                if name == "stk":
                    pe.wait_ge(S["shift_in"], 16)
                    pe.wait_ge(S["values_summed"], 3)
                else:
                    pe.wait_ge(S["fsq_ready"], 1)
                keep_warm(12, unused=2)
                transposed(name)
                chan_ready(name)
                for x in range(NT):
                    mm = project(bank[x // 8][:, 64 * (x % 8):64 * (x % 8) + 64], x, weight)
                mm.then_inc(S[done], 1)
            warm_for_norm(3, 20)
            transposed("ln3")
            moe(1)

            warm_for_norm(4, 14)
            pe.wait_ge(S["low_ready"], chunks * SPL.index("ln4") + chunks)
            for x in range(NT):
                if x >= 4:
                    pe.wait_ge(S["stack_act"], x - 3)
                T.matmul(bank[2 + x % 4][:, 0:3 * P], xt[:, x, :, :].rearrange("p a c -> p (a c)"), K["rowshift"],
                         start=True, stop=True).then_inc(S["stack_T"], 1)
                if x == 1:
                    pe.wait_ge(S["cb_sq"], 1)
                    T.matmul(bank[1][0:1, 0:CODES], K["first64"], cb2, start=True, stop=True)\
                        .then_inc(S["norm_out"], 1)
                if x == 3:
                    pe.wait_ge(S["xsum_ready"], 1)
                    T.matmul(bank[6][0:64, 0:P], xsum[:, :], K["samebatch"], start=True, stop=True)
                    T.matmul(bank[6][:, P:P + 64], K["samebatch"], xsum[:, :], start=True, stop=True)\
                        .then_inc(S["pool_out"], 1)
                if x == 7:
                    pe.wait_ge(S["poolT_in"], 1)
                    pe.wait_ge(S["phis_ready"], 1)
                    T.matmul(bank[7][:, 0:24], pooledT[:, :], phis[:, :], start=True, stop=True)\
                        .then_inc(S["co_out"], 1)
            split_weights("convw")
            pe.wait_ge(S["norm_set"], 1)
            for h in range(2):
                T.matmul(bank[h][:, :], zrow[:, 0:P], zrow[:, :], start=True, stop=False, skip_group_check=True)
            for x in range(NT):
                pe.wait_ge(S["stack_act"], x + 1)
                for x0, x1 in ((max(x - 1, 0), min(x + 2, 8)), (max(x - 1, 8), min(x + 2, NT))):
                    if x0 >= x1:
                        continue
                    dst = bank[x0 // 8][:, 64 * (x0 % 8):64 * (x0 % 8) + 64 * (x1 - x0)]
                    for r in range(3):
                        for w in (WH, WL):
                            taps = w["convw"][:, 192 * r + 64 * (x0 - x + 1):192 * r + 64 * (x1 - x + 1)]
                            mm = T.matmul(dst, stack[:, r, x, :], taps, start=False, stop=(x == NT - 1),
                                          skip_group_check=True)
                if x in (8, NT - 1):
                    mm.then_inc(S["conv_out"], 1)
            warm_for_norm(5, 18)
            transposed("ln5")
            moe(2)

            warm_for_norm(6, 14)
            transposed("ln6")
            chan_ready("ln6")
            split_weights("cbT")
            pe.wait_ge(S["consts_set"], 4)
            for n in range(8):
                if n >= 4:
                    pe.wait_ge(S["nd_ready"], 2 * (n - 3))
                for x in (2 * n, 2 * n + 1):
                    dst = bank[n % 4][:, 256 * (x % 2):256 * (x % 2) + 256]
                    for a in range(2):
                        T.matmul(dst, minus[:, :], code_norm[:, a, :], start=(a == 0), stop=False)
                    for w in (WH, WL):
                        mm = T.matmul(dst, xs[:, P * x:P * x + P], w["cbT"], start=False, stop=(w is WL))
                mm.then_inc(S["dot_out"], 1)
            warm_for_norm(7, 16)
            transposed("ln7")
            moe(3)


def kernel(**inputs):
    import numpy as np
    import concourse.bacc as bacc
    from concourse.bass_utils import run_bass_kernel_spmd

    v = {k: np.asarray(a) for k, a in inputs.items()}
    two = lambda a: np.concatenate([a, a], axis=0)
    every = lambda a: np.broadcast_to(a, (P,) + a.shape)
    x = v["x"]
    parts = {"ident": np.eye(P, dtype=np.float32)}
    parts["xT"] = x.reshape(2, 4, C, 2, P).transpose(4, 1, 3, 0, 2).reshape(P, NT * C)
    parts["xR"] = x.transpose(0, 2, 3, 1).reshape(P, NT * C)
    parts["wqkv"] = two(np.concatenate([v["L0_conv_Wq"].T, v["L0_conv_Wk"].T, v["L0_conv_Wv"].T], axis=1))
    parts["bqkv"] = every(np.concatenate([v["L0_conv_bq"], v["L0_conv_bk"], v["L0_conv_bv"]]))
    head = np.arange(64) // 8
    parts["headmask"] = two((head[:, None] == np.arange(128)[None, :] // 16).astype(np.float32))
    parts["headmean"] = (np.arange(P)[:, None] // 8 == np.arange(P)[None, :] // 8).astype(np.float32) / np.float32(8)
    parts["wf"] = two(v["L0_conv_Wf"].T)
    for name, src in (("bf", "bf"), ("bng", "bn_gamma"), ("bnb", "bn_beta"), ("bnm", "bn_mean"), ("bnv", "bn_var")):
        parts[name] = every(v["L0_conv_" + src])
    parts["rank8"] = every(np.arange(8, 0, -1, dtype=np.float32))
    parts["rank16"] = every(np.arange(16, 0, -1, dtype=np.float32))
    for m, s in ((0, "L0_ffn_"), (2, "L2_ffn_")):
        parts[f"rw{m}"] = two(v[s + "router_w"].T)
        parts[f"w1_{m}"] = two(v[s + "w1"].transpose(1, 0, 2).reshape(64, 512))
        parts[f"b1_{m}"] = v[s + "b1"].reshape(4, P).T
        parts[f"w2_{m}"] = v[s + "w2"].reshape(4, P, 64).transpose(1, 0, 2).reshape(P, 256)
        parts[f"b2_{m}"] = two(v[s + "b2"])
    parts["rw1"], parts["gb1"] = two(v["L1_ffn_gate_w"]), every(v["L1_ffn_gate_b"])
    parts["w1_1"] = two(v["L1_ffn_w1"].transpose(1, 0, 2).reshape(64, 2048))
    parts["wu_1"] = two(v["L1_ffn_w2"].transpose(1, 0, 2).reshape(64, 2048))
    parts["w2_1"] = v["L1_ffn_w3"].transpose(1, 0, 2).reshape(P, 1024)
    parts["rw3"], parts["gb3"] = two(v["L3_ffn_gate_w"]), every(v["L3_ffn_gate_b"])
    parts["w1_3"] = two(v["L3_ffn_W1"].transpose(1, 0, 2).reshape(64, 1024))
    parts["b1_3"] = v["L3_ffn_b1"].T
    parts["w2_3"] = v["L3_ffn_W2"].transpose(1, 0, 2).reshape(P, 512)
    parts["b2_3"] = two(v["L3_ffn_b2"])
    parts["qkvw"], parts["qkvb"] = two(v["L1_conv_qkv_w"].T), every(v["L1_conv_qkv_b"])
    b, y = np.arange(P) // H, np.arange(P) % H
    shift = [(b[:, None] == b[None, :]) & (y[:, None] == y[None, :] + r * d) for d in DILS for r in (-1, 1)]
    parts["shift"] = np.stack(shift, axis=1).astype(np.float32).reshape(P, 8 * P)
    parts["fcrep"] = two(np.repeat(v["L1_conv_fc_w"].T, 16, axis=0))
    parts["fcb"] = every(np.repeat(v["L1_conv_fc_b"], 16))
    ch = np.arange(64) % 16
    parts["fcmask"] = two((ch[:, None] == ch[None, :]).astype(np.float32))
    parts["lng"] = np.tile(v["L1_conv_ln_g"], 8)[:, None]
    parts["lnb"] = np.broadcast_to(np.tile(v["L1_conv_ln_b"], 8)[:, None], (P, P))
    parts["projw"], parts["projb"] = two(v["L1_conv_proj_w"].T), every(v["L1_conv_proj_b"])
    parts["samebatch"] = (b[:, None] == b[None, :]).astype(np.float32)
    parts["phi"] = v["L2_conv_phi_w"].reshape(24, 4, 64).transpose(2, 0, 1).reshape(64, 96)
    parts["rms"] = v["L2_conv_rms_w"].reshape(4, 64).T
    parts["phib"] = every(v["L2_conv_phi_b"])
    parts["alpha"] = every(np.concatenate([np.repeat(v["L2_conv_alpha_" + n], k)
                                           for n, k in (("pre", 4), ("post", 4), ("res", 16))]))
    parts["convw"] = two(v["L2_conv_conv_w"].transpose(1, 2, 3, 0)[:, :, ::-1, :].reshape(64, 576))
    parts["convb"] = every(v["L2_conv_conv_b"])
    parts["cbT"] = two(v["L3_conv_codebook"].T)
    parts["first64"] = (np.arange(P) < 64).astype(np.float32)[:, None]
    parts["blockmask"] = (np.arange(P)[:, None] // 8 == np.arange(16)[None, :]).astype(np.float32)
    parts["identh"] = np.eye(P)
    parts["rowshift"] = np.concatenate([(b[:, None] == b[None, :]) & (y[:, None] == y[None, :] + r)
                                        for r in (-1, 0, 1)], axis=1)
    for name, E, per, size in (("sel0", 8, 2, 1.0), ("sel3", 8, 1, 1.0)):
        expert = np.arange(E // per * P) // (P // per)
        parts[name] = (np.tile(np.arange(E), 2)[:, None] == expert[None, :]) * size

    def pack(spec, dtype):
        where, width = pack_columns(spec)
        a = np.zeros((P, width), dtype)
        for name, (at, rows, cols) in where.items():
            a[0:rows, at:at + cols] = parts[name].astype(dtype) if dtype != np.float32 else parts[name]
        return a

    nc = bacc.Bacc("TRN2", target_bir_lowering=False, num_devices=1)
    arrays, dram = {}, {}
    for pk, spec in PACKS.items():
        arrays["in_" + pk] = pack(spec, np.float32)
    arrays["in_half"] = pack(HALF_PACK, np.float16)
    arrays["in_codebook"] = np.ascontiguousarray(v["L3_conv_codebook"])
    for name, a in arrays.items():
        dram[name[3:]] = nc.dram_tensor(name, a.shape, mybir.dt.from_np(a.dtype), kind="ExternalInput").ap()
    codebook = dram.pop("codebook")
    out = nc.dram_tensor("out_tokens", (P, NT, C), mybir.dt.float32, kind="ExternalOutput").ap()
    metaformer(nc, dram, codebook, out)
    r = run_bass_kernel_spmd(nc, [arrays], core_ids=[0])
    tokens = r.results[0]["out_tokens"]
    return tokens.reshape(B, H, W, C).transpose(0, 3, 1, 2)
```
